# Optimizing a Trainium2 kernel written in Bass

```python
import numpy as np
import jax
import jax.numpy as jnp

def _softmax(x, axis=-1):
    return jax.nn.softmax(x, axis=axis)

def _gelu(x):
    return jax.nn.gelu(x, approximate=True)

def _silu(x):
    return jax.nn.silu(x)

def _sigmoid(x):
    return jax.nn.sigmoid(x)

def _layernorm(x, axis=-1, eps=1e-05):
    m = jnp.mean(x, axis=axis, keepdims=True)
    v = jnp.var(x, axis=axis, keepdims=True)
    return (x - m) / jnp.sqrt(v + eps)

def _scatter_add(tgt, idx, src, axis=0):
    return tgt.at[idx].add(src)

def _segment_sum(src, seg, n):
    return jax.ops.segment_sum(src, seg, n)
kernel_name = 'mk_gnn_preln_d2_gnn_r32_35b505'

def setup_inputs(seed: int=0):
    np.random.seed(seed)
    _w = jnp.asarray

    def _rec_inputs():
        import jax
        import jax.numpy as jnp
        _gk = jax.random.key(seed)
        x = -0.0003713 + 1 * jax.random.normal(jax.random.fold_in(_gk, 1), (3125, 128), jnp.float32)
        _s = jax.random.randint(jax.random.fold_in(_gk, 2), (50000,), 0, 3125, jnp.int32)
        _d = jax.random.randint(jax.random.fold_in(_gk, 3), (50000,), 0, 3125, jnp.int32)
        _loop = jnp.arange(3125, dtype=jnp.int32)
        src = jnp.concatenate([_s, _d, _loop])
        dst = jnp.concatenate([_d, _s, _loop])
        _o = jnp.argsort(dst, stable=True)
        src = src[_o]
        dst = dst[_o]
        edge_type_4 = jax.random.randint(jax.random.fold_in(_gk, 13), (103125,), 0, 4, jnp.int32)
        return (x, src, dst, edge_type_4)
    x, src, dst, edge_type_4 = _rec_inputs()

    def _L0_gnn_setup():
        import jax, jax.numpy as jnp
        import numpy as np
        N_NODES = 3125
        NFEAT = 128
        NHID = 128
        EPS_NORM = 1e-12
        EPS_BN = 1e-05

        def _sage_conv(x, src, dst, W_l, b_l, W_r):
            agg = jax.ops.segment_sum(x[src], dst, num_segments=N_NODES)
            cnt = jax.ops.segment_sum(jnp.ones_like(dst, dtype=x.dtype), dst, num_segments=N_NODES)
            mean = agg / jnp.maximum(cnt, 1.0)[:, None]
            out = mean @ W_l.T + b_l + x @ W_r.T
            nrm = jnp.sqrt(jnp.sum(out * out, axis=-1, keepdims=True))
            return out / jnp.maximum(nrm, EPS_NORM)
        key = jax.random.key(seed)
        ks = jax.random.split(key, 10)
        x = jax.random.normal(ks[0], (N_NODES, NFEAT), dtype=jnp.float32)
        edge_index = jax.random.randint(ks[1], (2, 50000), 0, N_NODES, dtype=jnp.int64)
        s1 = 1.0 / np.sqrt(NFEAT)
        s2 = 1.0 / np.sqrt(NHID)
        W_l1 = jax.random.uniform(ks[2], (NHID, NFEAT), jnp.float32, -s1, s1)
        b_l1 = jax.random.uniform(ks[3], (NHID,), jnp.float32, -s1, s1)
        W_r1 = jax.random.uniform(ks[4], (NHID, NFEAT), jnp.float32, -s1, s1)
        gamma = jnp.ones((NHID,), jnp.float32)
        beta = jnp.zeros((NHID,), jnp.float32)
        W_l2 = jax.random.uniform(ks[5], (NHID, NHID), jnp.float32, -s2, s2)
        b_l2 = jax.random.uniform(ks[6], (NHID,), jnp.float32, -s2, s2)
        W_r2 = jax.random.uniform(ks[7], (NHID, NHID), jnp.float32, -s2, s2)
        return {'x': x, 'edge_index': edge_index, 'W_l1': W_l1, 'b_l1': b_l1, 'W_r1': W_r1, 'gamma': gamma, 'beta': beta, 'W_l2': W_l2, 'b_l2': b_l2, 'W_r2': W_r2}
    _L0_gnn_all = _L0_gnn_setup()
    _L0_gnn_in = {k: v for k, v in _L0_gnn_all.items() if k in ('W_l1', 'b_l1', 'W_r1', 'gamma', 'beta', 'W_l2', 'b_l2', 'W_r2')}
    del _L0_gnn_all

    def _L1_gnn_setup():
        import jax, jax.numpy as jnp
        import numpy as np
        N = 3125
        E = 50000
        D = 128
        G = 128
        K = 4
        STEPS = 3

        def _gru_cell(a, h, W_ih, b_ih, W_hh, b_hh):
            gi = a @ W_ih.T + b_ih
            gh = h @ W_hh.T + b_hh
            ir, iz, in_ = jnp.split(gi, 3, axis=1)
            hr, hz, hn = jnp.split(gh, 3, axis=1)
            r = jax.nn.sigmoid(ir + hr)
            z = jax.nn.sigmoid(iz + hz)
            n = jnp.tanh(in_ + r * hn)
            return (1.0 - z) * n + z * h
        key = jax.random.key(seed)
        ks = jax.random.split(key, 16)
        s = 0.05
        return {'features': jax.random.normal(ks[0], (N, D), jnp.float32), 'src': jax.random.randint(ks[1], (E,), 0, N, jnp.int32), 'dst': jax.random.randint(ks[2], (E,), 0, N, jnp.int32), 'etypes': jax.random.randint(ks[3], (E,), 0, K, jnp.int32), 'W_et': jax.random.normal(ks[4], (K, D, D), jnp.float32) * s, 'b_et': jax.random.normal(ks[5], (K, D), jnp.float32) * s, 'W_ih': jax.random.normal(ks[6], (3 * D, D), jnp.float32) * s, 'b_ih': jax.random.normal(ks[7], (3 * D,), jnp.float32) * s, 'W_hh': jax.random.normal(ks[8], (3 * D, D), jnp.float32) * s, 'b_hh': jax.random.normal(ks[9], (3 * D,), jnp.float32) * s, 'i_w': jax.random.normal(ks[10], (G, D + D), jnp.float32) * s, 'i_b': jax.random.normal(ks[11], (G,), jnp.float32) * s, 'j_w': jax.random.normal(ks[12], (G, D), jnp.float32) * s, 'j_b': jax.random.normal(ks[13], (G,), jnp.float32) * s}
    _L1_gnn_all = _L1_gnn_setup()
    _L1_gnn_in = {k: v for k, v in _L1_gnn_all.items() if k in ('W_et', 'b_et', 'W_ih', 'b_ih', 'W_hh', 'b_hh', 'i_w', 'i_b', 'j_w', 'j_b')}
    del _L1_gnn_all
    return {'x': x, 'src': src, 'dst': dst, 'edge_type_4': edge_type_4, 'L0_gnn_W_l1': _L0_gnn_in['W_l1'], 'L0_gnn_b_l1': _L0_gnn_in['b_l1'], 'L0_gnn_W_r1': _L0_gnn_in['W_r1'], 'L0_gnn_gamma': _L0_gnn_in['gamma'], 'L0_gnn_beta': _L0_gnn_in['beta'], 'L0_gnn_W_l2': _L0_gnn_in['W_l2'], 'L0_gnn_b_l2': _L0_gnn_in['b_l2'], 'L0_gnn_W_r2': _L0_gnn_in['W_r2'], 'L1_gnn_W_et': _L1_gnn_in['W_et'], 'L1_gnn_b_et': _L1_gnn_in['b_et'], 'L1_gnn_W_ih': _L1_gnn_in['W_ih'], 'L1_gnn_b_ih': _L1_gnn_in['b_ih'], 'L1_gnn_W_hh': _L1_gnn_in['W_hh'], 'L1_gnn_b_hh': _L1_gnn_in['b_hh'], 'L1_gnn_i_w': _L1_gnn_in['i_w'], 'L1_gnn_i_b': _L1_gnn_in['i_b'], 'L1_gnn_j_w': _L1_gnn_in['j_w'], 'L1_gnn_j_b': _L1_gnn_in['j_b']}

def reference(x, src, dst, edge_type_4, L0_gnn_W_l1, L0_gnn_b_l1, L0_gnn_W_r1, L0_gnn_gamma, L0_gnn_beta, L0_gnn_W_l2, L0_gnn_b_l2, L0_gnn_W_r2, L1_gnn_W_et, L1_gnn_b_et, L1_gnn_W_ih, L1_gnn_b_ih, L1_gnn_W_hh, L1_gnn_b_hh, L1_gnn_i_w, L1_gnn_i_b, L1_gnn_j_w, L1_gnn_j_b):
    import jax
    import jax.numpy as jnp

    def _L0_gnn_ref(x, edge_index, W_l1, b_l1, W_r1, gamma, beta, W_l2, b_l2, W_r2):
        import jax, jax.numpy as jnp
        import numpy as np
        N_NODES = 3125
        NFEAT = 128
        NHID = 128
        EPS_NORM = 1e-12
        EPS_BN = 1e-05

        def _sage_conv(x, src, dst, W_l, b_l, W_r):
            agg = jax.ops.segment_sum(x[src], dst, num_segments=N_NODES)
            cnt = jax.ops.segment_sum(jnp.ones_like(dst, dtype=x.dtype), dst, num_segments=N_NODES)
            mean = agg / jnp.maximum(cnt, 1.0)[:, None]
            out = mean @ W_l.T + b_l + x @ W_r.T
            nrm = jnp.sqrt(jnp.sum(out * out, axis=-1, keepdims=True))
            return out / jnp.maximum(nrm, EPS_NORM)
        src, dst = (edge_index[0], edge_index[1])
        h = _sage_conv(x, src, dst, W_l1, b_l1, W_r1)
        h = jax.nn.relu(h)
        mu = jnp.mean(h, axis=0)
        var = jnp.mean((h - mu) ** 2, axis=0)
        h = (h - mu) / jnp.sqrt(var + EPS_BN) * gamma + beta
        return _sage_conv(h, src, dst, W_l2, b_l2, W_r2)

    def _L1_gnn_ref(features, src, dst, etypes, W_et, b_et, W_ih, b_ih, W_hh, b_hh, i_w, i_b, j_w, j_b):
        import jax, jax.numpy as jnp
        import numpy as np
        N = 3125
        E = 50000
        D = 128
        G = 128
        K = 4
        STEPS = 3

        def _gru_cell(a, h, W_ih, b_ih, W_hh, b_hh):
            gi = a @ W_ih.T + b_ih
            gh = h @ W_hh.T + b_hh
            ir, iz, in_ = jnp.split(gi, 3, axis=1)
            hr, hz, hn = jnp.split(gh, 3, axis=1)
            r = jax.nn.sigmoid(ir + hr)
            z = jax.nn.sigmoid(iz + hz)
            n = jnp.tanh(in_ + r * hn)
            return (1.0 - z) * n + z * h
        n_nodes = features.shape[0]
        h = features
        for _ in range(STEPS):
            t = jnp.einsum('nd,kod->kno', h, W_et) + b_et[:, None, :]
            msg = t[etypes, src]
            a = jax.ops.segment_sum(msg, dst, num_segments=n_nodes)
            h = _gru_cell(a, h, W_ih, b_ih, W_hh, b_hh)
        gate = jax.nn.sigmoid(jnp.concatenate([h, features], axis=1) @ i_w.T + i_b)
        return gate * (h @ j_w.T + j_b)
    edge_index = jnp.stack([src, dst])
    h = jnp.maximum(_layernorm(x, axis=-1), 0.0)
    x = x + _L0_gnn_ref(h, edge_index, L0_gnn_W_l1, L0_gnn_b_l1, L0_gnn_W_r1, L0_gnn_gamma, L0_gnn_beta, L0_gnn_W_l2, L0_gnn_b_l2, L0_gnn_W_r2)
    h = jnp.maximum(_layernorm(x, axis=-1), 0.0)
    x = x + _L1_gnn_ref(h, src, dst, edge_type_4, L1_gnn_W_et, L1_gnn_b_et, L1_gnn_W_ih, L1_gnn_b_ih, L1_gnn_W_hh, L1_gnn_b_hh, L1_gnn_i_w, L1_gnn_i_b, L1_gnn_j_w, L1_gnn_j_b)
    return x

_drawn_inputs = setup_inputs


def setup_inputs(seed=0):
    import zlib

    import numpy as np

    out = dict(_drawn_inputs(seed))
    spreads = {'L0_gnn_gamma': (1.0, 0.6), 'L0_gnn_beta': (0.0, 0.573)}
    factors = {'L0_gnn_b_l1': 18.53,
     'L0_gnn_W_l2': 3.006,
     'L0_gnn_b_l2': 6.416,
     'L1_gnn_b_ih': 5.34,
     'L1_gnn_b_hh': 8.0,
     'L1_gnn_i_b': 8.0,
     'L0_gnn_W_l1': 3.505}
    for name, (base, spread) in spreads.items():
        noise = np.random.default_rng([zlib.crc32(name.encode()), seed]).standard_normal(out[name].shape)
        drawn = base * np.exp(spread * noise) if base else spread * noise
        out[name] = jnp.asarray(drawn.astype(out[name].dtype))
    for name, factor in factors.items():
        out[name] = (out[name] * factor).astype(out[name].dtype)
    return out
```

```python
from contextlib import ExitStack

import numpy as np

import concourse.bass as bass
from concourse import mybir

P = 128
N = 3125
D = 128
E = 103125
K = 4
STEPS = 3
Q = -(-N // P)
NP = Q * P
J = 8
TILES = -(-E // P)
NB = -(-TILES // J)
EP = NB * J * P
ACC = K * NP + P
CH = 400
NC = NP // CH
ROUNDS = 2 + STEPS
TG = -(-Q // 4)

F32 = mybir.dt.float32
F16 = mybir.dt.float16
I32 = mybir.dt.int32
ALU = mybir.AluOpType
ACT = mybir.ActivationFunctionType
AX = mybir.AxisListType

WL1, WR1, WL2, WR2, WET, WIH, WHH, IW, JW = 0, 1, 2, 3, 4, 8, 11, 14, 16
NW = 17
BL1, BL2, GAM, BET, BIH, BHH, IB, JB = 0, 1, 2, 3, 4, 7, 10, 11
NBIAS = 12


class Count:

    def __init__(self, base=0):
        self.base, self.step = base, 0

    def up(self, by=1):
        self.step += by
        return self.base + self.step

    def value(self, less=0):
        return self.base + (self.step - less)

    def loop(self, i, per):
        inner = Count(i * per + self.value())
        inner.per = per
        return inner


def gnn_kernel(nc, x, src_c, dst_c, typ_c, dst_r, typ_r, weights, biases, b_et, consts, out):
    with ExitStack() as ctx:
        def sb(name, shape, dt=F32):
            return ctx.enter_context(nc.sbuf_tensor(name, shape, dt))

        def sem(name):
            return ctx.enter_context(nc.semaphore(name))

        table = nc.dram_tensor("table", [NP, D], F32, kind="Internal").ap()
        acc = nc.dram_tensor("acc", [ACC, D], F32, kind="Internal").ap()
        cnt_dram = nc.dram_tensor("cnt_dram", [K + 1, Q, P], F32, kind="Internal").ap()

        xr = sb("xr", [P, Q, D])
        rows = sb("rows", [P, Q, D])
        hT = sb("hT", [P, NP])
        featT = sb("featT", [P, NP])
        ST = sb("ST", [P, K, NP])
        zeros = sb("zeros", [P, ACC * D // P // 32])
        w = sb("w", [P, NW, P])
        bias = sb("bias", [P, NBIAS])
        brz = sb("brz", [P, 2])
        bet = sb("bet", [K, P])
        con = sb("con", [P, 3 * P + 1])
        ident, below, iota, lane = con[:, 0:P], con[:, P:2 * P], con[:, 2 * P:3 * P], con[:, 3 * P:3 * P + 1]
        ones = sb("ones", [P, P])
        dstc = sb("dstc", [P, NB * J], I32)
        typc = sb("typc", [P, NB * J], I32)
        lowi = ST[:, 0, 0:NB * J].bitcast(I32)
        lowf = sb("lowf", [P, NB * J])
        highf = sb("highf", [P, NB * J])
        oh_low = sb("oh_low", [P, 2, J, P], F16)
        oh_high = sb("oh_high", [P, 2, J, K * Q], F16)
        cnt = sb("cnt", [P, K + 1, Q])
        cntT = sb("cntT", [P, P])
        totT = sb("totT", [Q, P])
        cnt4 = sb("cnt4", [K, NP])
        cntb = sb("cntb", [P, NP])
        invb = sb("invb", [P, NP])
        st6 = sb("st6", [P, Q, 6])
        mv = sb("mv", [P, Q, 2])
        rstd = sb("rstd", [P, Q])
        cols = sb("cols", [P, 8])
        b_src = sb("b_src", [P, J], I32)
        b_dst = sb("b_dst", [P, J], I32)
        b_typ = sb("b_typ", [P, J], I32)
        r_dst = sb("r_dst", [P, J * P], I32)
        r_typ = sb("r_typ", [P, J * P], I32)
        key_c = sb("key_c", [P, J])
        key_r = sb("key_r", [P, J, P])
        same = sb("same", [P, J, P])
        comb = sb("comb", [P, J, D])
        earlier = comb
        dup = sb("dup", [P, J])
        spare = sb("spare", [P, J])
        to_row = sb("to_row", [P, J], I32)
        got = sb("got", [P, J, D])
        rowbuf = sb("rowbuf", [P, 4, D])
        aT = sb("aT", [P, CH])
        rT = sb("rT", [P, CH])
        zT = sb("zT", [P, CH])
        tT = sb("tT", [P, CH])
        nT = sb("nT", [P, CH])
        B = [ctx.enter_context(nc.psum_tensor(f"bank{i}", [P, 512], F32)) for i in range(8)]

        names = """loaded consts_loaded edges_in hist_free hist_ready hist_done cnt_psum cnt_sb cnt_written
            cnt_read act_step dve_step ln_var ln_std rows_ready tr_psum tr_copied tab_written acc_zeroed zeros_set
            edges_loaded keys_ready gathered comb_psum combined scattered row_loaded st_psum st_copied
            mean_ready sg_psum sg_sq sg_ssq sg_max sg_std sg_done bn_var bn_std h_ready
            a_psum a_copied gates_psum sig_done pre_n n_ready h_updated rdy_out o_psum o_sig o_done
            stored passed""".split()
        s = {n: sem(n) for n in names}

        def transpose_rows(pe, tr, src, dst_cols):
            for g in range(TG):
                n = min(4, Q - 4 * g)
                if tr.step >= 2 or not isinstance(tr.base, int):
                    pe.wait_ge(s["tr_copied"], tr.value(1))
                for m in range(n):
                    ins = pe.transpose(B[5 + g % 2][:, m * P:(m + 1) * P], src(4 * g + m), ident)
                ins.then_inc(s["tr_psum"], 1)
                tr.up()
            pe.wait_ge(s["tr_copied"], tr.value())

        def copy_rows(act, tr, dst):
            for g in range(TG):
                n = min(4, Q - 4 * g)
                act.wait_ge(s["tr_psum"], tr.up())
                act.activation(dst[:, 4 * g * P:(4 * g + n) * P], B[5 + g % 2][:, 0:n * P], ACT.Copy)\
                   .then_inc(s["tr_copied"], 1)

        block = ctx.enter_context(nc.Block())

        @block.sync
        def _(sp):
            sp.dma_start(dstc[:, :], dst_c).then_inc(s["edges_in"], 16)
            sp.dma_start(typc[:, :], typ_c).then_inc(s["edges_in"], 16)
            sp.dma_start(con[:, :], consts).then_inc(s["consts_loaded"], 16)
            sp.wait_ge(s["zeros_set"], 2)
            full = N // P
            sp.dma_start(xr[:, 0:full, :], x[0:full * P, :].rearrange("(q p) f -> p q f", p=P))\
              .then_inc(s["loaded"], 16)
            sp.dma_start(xr[0:N - full * P, full, :], x[full * P:N, :]).then_inc(s["loaded"], 16)
            sp.dma_start(w[:, :, :], weights).then_inc(s["loaded"], 16)
            sp.dma_start(bias[:, :], biases).then_inc(s["loaded"], 16)
            sp.dma_start(bet[:, :], b_et).then_inc(s["loaded"], 16)
            sp.wait_ge(s["cnt_sb"], 2)
            sp.dma_start(cnt_dram[0:K].rearrange("k q p -> (k q) p"), cntT[0:K * Q, :]).then_inc(s["cnt_written"], 16)
            sp.dma_start(cnt_dram[K], totT[:, :]).then_inc(s["cnt_written"], 16)
            sp.wait_ge(s["cnt_written"], 32)
            sp.dma_start(cnt4[:, :], cnt_dram[0:K].rearrange("k q p -> k (q p)")).then_inc(s["cnt_read"], 16)
            sp.dma_start(cntb[:, :], cnt_dram[K].rearrange("q p -> (q p)").partition_broadcast(P))\
              .then_inc(s["cnt_read"], 16)

            def aggregate(turn):
                sp.wait_ge(s["rows_ready"], 1 + turn)
                sp.dma_start(table.rearrange("(q p) f -> p q f", p=P), rows[:, :, :]).then_inc(s["tab_written"], 16)
                flat = acc.rearrange("(p a) f -> p (a f)", p=P)
                part = ACC * D // P // 32
                for i in range(32):
                    sp.dma_start(flat[:, i * part:(i + 1) * part], zeros[:, :]).then_inc(s["acc_zeroed"], 16)
                with sp.Fori(0, NB) as b:
                    sp.wait_ge(s["scattered"], (turn * NB + b) * (16 * J))
                    sp.dma_start(b_src[:, :], src_c[:, bass.ds(b * J, J)]).then_inc(s["edges_loaded"], 16)
                    sp.dma_start(b_dst[:, :], dst_c[:, bass.ds(b * J, J)]).then_inc(s["edges_loaded"], 16)
                    sp.dma_start(b_typ[:, :], typ_c[:, bass.ds(b * J, J)]).then_inc(s["edges_loaded"], 16)
                    sp.dma_start(r_dst[:, :], dst_r[bass.ds(b * J * P, J * P)].partition_broadcast(P))\
                      .then_inc(s["edges_loaded"], 16)
                    sp.dma_start(r_typ[:, :], typ_r[bass.ds(b * J * P, J * P)].partition_broadcast(P))\
                      .then_inc(s["edges_loaded"], 16)
                sp.wait_ge(s["scattered"], (turn + 1) * (NB * 16 * J))
                sp.sem_inc(s["passed"], 1)
                with sp.Fori(0, K * Q // 4) as i:
                    sp.wait_ge(s["st_psum"], turn * (K * Q // 4) + i)
                    sp.dma_start(rowbuf[:, :, :], acc[bass.ds(i * 4 * P, 4 * P), :].rearrange("(j p) f -> p j f", p=P))\
                      .then_inc(s["row_loaded"], 16)

            aggregate(0)
            aggregate(1)
            with sp.Fori(0, STEPS) as t:
                aggregate(t + 2)
            sp.wait_ge(s["rdy_out"], 1)
            sp.dma_start(out[0:full * P, :].rearrange("(q p) f -> p q f", p=P), rows[:, 0:full, :])\
              .then_inc(s["stored"], 16)
            sp.dma_start(out[full * P:N, :], rows[0:N - full * P, full, :]).then_inc(s["stored"], 16)
            sp.wait_ge(s["stored"], 32)

        @block.gpsimd
        def _(pool):
            pool.memset(zeros[:, :], 0.0).then_inc(s["zeros_set"], 1)
            pool.memset(xr[:, :, :], 0.0).then_inc(s["zeros_set"], 1)

            def aggregate(turn):
                pool.wait_ge(s["tab_written"], (turn + 1) * 16)
                pool.wait_ge(s["acc_zeroed"], (turn + 1) * 512)
                pool.sem_inc(s["passed"], 1)
                with pool.Fori(0, NB) as b:
                    blk = turn * NB + b
                    pool.wait_ge(s["edges_loaded"], (blk + 1) * 80)
                    pool.sem_inc(s["passed"], 1)
                    for j in range(J):
                        pool.indirect_dma_start(got[:, j, :], None, table,
                                                bass.IndirectOffsetOnAxis(ap=b_src[:, j:j + 1], axis=0))\
                            .then_inc(s["gathered"], 16)
                    pool.wait_ge(s["keys_ready"], blk + 1)
                    for j in range(J):
                        pool.wait_ge(s["combined"], blk * (J // 4) + (j // 4 + 1))
                        pool.sem_inc(s["passed"], 1)
                        pool.indirect_dma_start(acc, bass.IndirectOffsetOnAxis(ap=to_row[:, j:j + 1], axis=0),
                                                comb[:, j, :], None, compute_op=ALU.add,
                                                bounds_check=ACC - 1).then_inc(s["scattered"], 16)
                        pool.wait_ge(s["scattered"], blk * (16 * J) + 16 * (j + 1))

            aggregate(0)
            aggregate(1)
            with pool.Fori(0, STEPS) as t:
                aggregate(t + 2)

        @block.tensor
        def _(pe):
            def hist(b, buf, first, last):
                pe.wait_ge(s["hist_ready"], b + 1)
                for j in range(J):
                    ins = pe.matmul(B[7][:, 0:K * Q], oh_low[:, buf, j, :], oh_high[:, buf, j, :],
                                    start=first and j == 0, stop=last and j == J - 1)
                ins.then_inc(s["hist_done"], 1)

            hist(0, 0, True, False)
            with pe.Fori(0, (NB - 3) // 2) as b2:
                hist(b2 * 2 + 1, 1, False, False)
                hist(b2 * 2 + 2, 0, False, False)
            hist(NB - 2, 1, False, False)
            hist(NB - 1, 0, False, True)
            pe.wait_ge(s["consts_loaded"], 16)
            pe.wait_ge(s["cnt_psum"], 1)
            pe.transpose(B[6][0:K * Q, 0:P], cnt[:, 0:K, :].rearrange("p k q -> p (k q)"), ident)
            pe.transpose(B[6][0:Q, P:2 * P], cnt[:, K, :], ident).then_inc(s["cnt_psum"], 1)

            tr = Count()

            def sums_to_columns(turn):
                with pe.Fori(0, K * Q // 4) as i:
                    g = turn * (K * Q // 4) + i
                    pe.wait_ge(s["row_loaded"], (g + 1) * 16)
                    pe.wait_ge(s["st_copied"], g)
                    for m in range(4):
                        ins = pe.transpose(B[5][:, m * P:(m + 1) * P], rowbuf[:, m, :], ident)
                    ins.then_inc(s["st_psum"], 1)

            def aggregate(turn):
                with pe.Fori(0, NB) as b:
                    blk = turn * NB + b
                    pe.wait_ge(s["gathered"], (blk + 1) * (16 * J))
                    pe.wait_ge(s["keys_ready"], blk + 1)
                    for j in range(J):
                        ins = pe.matmul(B[6 + j // 4][:, (j % 4) * P:(j % 4 + 1) * P], same[:, j, :], got[:, j, :],
                                        start=True, stop=True)
                        if j % 4 == 3:
                            ins.then_inc(s["comb_psum"], 1)
                sums_to_columns(turn)
                pe.wait_ge(s["st_copied"], (turn + 1) * (K * Q // 4))
                pe.sem_inc(s["passed"], 1)

            def sage(turn, w_agg, w_own):
                pe.wait_ge(s["mean_ready"], turn + 1)
                with pe.Fori(0, NC) as c:
                    g = turn * NC + c
                    pe.wait_ge(s["sg_done"], g)
                    pe.matmul(B[0][:, 0:CH], w[:, w_agg, :], ST[:, 0, bass.ds(c * CH, CH)], start=True, stop=False)
                    pe.matmul(B[0][:, 0:CH], w[:, w_own, :], hT[:, bass.ds(c * CH, CH)], start=False, stop=True)\
                      .then_inc(s["sg_psum"], 1)
                    pe.wait_ge(s["sg_sq"], g + 1)
                    pe.matmul(B[1][:, 0:CH], ones[:, :], tT[:, :], start=True, stop=True).then_inc(s["sg_ssq"], 1)

            pe.wait_ge(s["cnt_sb"], 2)
            pe.wait_ge(s["rows_ready"], 1)
            transpose_rows(pe, tr, lambda q: rows[:, q, :], None)
            aggregate(0)
            sage(0, WL1, WR1)
            pe.wait_ge(s["sg_done"], NC)
            transpose_rows(pe, tr, lambda q: hT[:, q * P:(q + 1) * P], None)
            aggregate(1)
            sage(1, WL2, WR2)
            pe.wait_ge(s["sg_done"], 2 * NC)
            transpose_rows(pe, tr, lambda q: hT[:, q * P:(q + 1) * P], None)
            pe.wait_ge(s["rows_ready"], 3)
            transpose_rows(pe, tr, lambda q: rows[:, q, :], None)
            with pe.Fori(0, STEPS) as t:
                aggregate(t + 2)
                with pe.Fori(0, NC) as c:
                    g = t * NC + c
                    at = bass.ds(c * CH, CH)
                    pe.wait_ge(s["a_copied"], g)
                    for k in range(K):
                        pe.matmul(B[0][:, 0:CH], w[:, WET + k, :], ST[:, k, at], start=k == 0, stop=False)
                    pe.matmul(B[0][:, 0:CH], bet[:, :], cnt4[:, at], start=False, stop=True)\
                      .then_inc(s["a_psum"], 1)
                    pe.wait_ge(s["a_copied"], g + 1)
                    pe.wait_ge(s["pre_n"], g)
                    for m in range(2):
                        pe.matmul(B[1 + m][:, 0:CH], w[:, WIH + m, :], aT[:, :], start=True, stop=False)
                        pe.matmul(B[1 + m][:, 0:CH], w[:, WHH + m, :], hT[:, at], start=False, stop=True)
                    pe.matmul(B[3][:, 0:CH], w[:, WHH + 2, :], hT[:, at], start=True, stop=True)
                    pe.matmul(B[4][:, 0:CH], w[:, WIH + 2, :], aT[:, :], start=True, stop=True)\
                      .then_inc(s["gates_psum"], 1)
                pe.wait_ge(s["h_updated"], (t + 1) * NC)
                transpose_rows(pe, tr.loop(t, TG), lambda q: hT[:, q * P:(q + 1) * P], None)
            tr.up(STEPS * TG)
            with pe.Fori(0, NC) as c:
                at = bass.ds(c * CH, CH)
                pe.wait_ge(s["o_done"], c)
                pe.matmul(B[0][:, 0:CH], w[:, IW, :], hT[:, at], start=True, stop=False)
                pe.matmul(B[0][:, 0:CH], w[:, IW + 1, :], featT[:, at], start=False, stop=True)
                pe.matmul(B[1][:, 0:CH], w[:, JW, :], hT[:, at], start=True, stop=True).then_inc(s["o_psum"], 1)
            pe.wait_ge(s["o_done"], NC)
            transpose_rows(pe, tr, lambda q: hT[:, q * P:(q + 1) * P], None)

        @block.scalar
        def _(act):
            tr = Count()
            act.wait_ge(s["cnt_psum"], 2)
            act.activation(cntT[0:K * Q, :], B[6][0:K * Q, 0:P], ACT.Copy).then_inc(s["cnt_sb"], 1)
            act.activation(totT[:, :], B[6][0:Q, P:2 * P], ACT.Copy).then_inc(s["cnt_sb"], 1)
            act.wait_ge(s["ln_var"], 1)
            act.activation(rstd[:, :], mv[:, :, 1], ACT.Sqrt).then_inc(s["ln_std"], 1)
            copy_rows(act, tr, hT)

            def sums_to_columns(turn):
                with act.Fori(0, K * Q // 4) as i:
                    act.wait_ge(s["st_psum"], turn * (K * Q // 4) + i + 1)
                    act.activation(ST[:, :, :].rearrange("p k n -> p (k n)")[:, bass.ds(i * 512, 512)],
                                   B[5][:, :], ACT.Copy).then_inc(s["st_copied"], 1)

            def sage(turn, b):
                with act.Fori(0, NC) as c:
                    g = turn * NC + c
                    act.wait_ge(s["sg_psum"], g + 1)
                    act.activation(tT[:, :], B[0][:, 0:CH], ACT.Square, bias=bias[:, b:b + 1])\
                       .then_inc(s["sg_sq"], 1)
                    act.activation(aT[:, :], B[0][:, 0:CH], ACT.Identity, bias=bias[:, b:b + 1])\
                       .then_inc(s["act_step"], 1)
                    act.wait_ge(s["sg_max"], g + 1)
                    act.activation(nT[:, :], rT[:, :], ACT.Sqrt).then_inc(s["sg_std"], 1)

            sums_to_columns(0)
            sage(0, BL1)
            act.wait_ge(s["bn_var"], 1)
            act.activation(cols[:, 2:3], cols[:, 1:2], ACT.Sqrt).then_inc(s["bn_std"], 1)
            copy_rows(act, tr, rows[:, :, :].rearrange("p q f -> p (q f)"))
            act.wait_ge(s["tr_copied"], 2 * TG)
            act.activation(cols[:, 6:7], cols[:, 2:3], ACT.Copy).then_inc(s["rows_ready"], 1)
            sums_to_columns(1)
            sage(1, BL2)
            copy_rows(act, tr, rows[:, :, :].rearrange("p q f -> p (q f)"))
            act.wait_ge(s["ln_var"], 2)
            act.activation(rstd[:, :], mv[:, :, 1], ACT.Sqrt).then_inc(s["ln_std"], 1)
            copy_rows(act, tr, hT)
            with act.Fori(0, STEPS) as t:
                sums_to_columns(t + 2)
                with act.Fori(0, NC) as c:
                    g = t * NC + c
                    act.wait_ge(s["a_psum"], g + 1)
                    act.wait_ge(s["gates_psum"], g)
                    act.activation(aT[:, :], B[0][:, 0:CH], ACT.Copy).then_inc(s["a_copied"], 1)
                    act.wait_ge(s["gates_psum"], g + 1)
                    act.wait_ge(s["h_updated"], g)
                    act.activation(rT[:, :], B[1][:, 0:CH], ACT.Sigmoid, bias=brz[:, 0:1]).then_inc(s["sig_done"], 1)
                    act.activation(zT[:, :], B[2][:, 0:CH], ACT.Sigmoid, bias=brz[:, 1:2]).then_inc(s["sig_done"], 1)
                    act.wait_ge(s["pre_n"], g + 1)
                    act.activation(nT[:, :], tT[:, :], ACT.Tanh, bias=bias[:, BIH + 2:BIH + 3]).then_inc(s["n_ready"], 1)
                inner = tr.loop(t, TG)
                copy_rows(act, inner, rows[:, :, :].rearrange("p q f -> p (q f)"))
                act.wait_ge(s["tr_copied"], inner.value())
                act.activation(cols[:, 6:7], cols[:, 2:3], ACT.Copy).then_inc(s["rows_ready"], 1)
            tr.up(STEPS * TG)
            with act.Fori(0, NC) as c:
                act.wait_ge(s["o_psum"], c + 1)
                act.activation(rT[:, :], B[0][:, 0:CH], ACT.Sigmoid, bias=bias[:, IB:IB + 1]).then_inc(s["o_sig"], 1)
            copy_rows(act, tr, rows[:, :, :].rearrange("p q f -> p (q f)"))

        @block.vector
        def _(dve):
            chain = Count()

            def link(ins, ch):
                ins.then_inc(s["dve_step"], 1)
                dve.wait_ge(s["dve_step"], ch.up())

            dve.memset(ones[:, :], 1.0)
            dve.wait_ge(s["edges_in"], 32)
            dve.wait_ge(s["consts_loaded"], 16)
            link(dve.tensor_single_scalar(lowi, dstc[:, :], P - 1, ALU.bitwise_and), chain)
            link(dve.tensor_copy(lowf[:, :], lowi), chain)
            link(dve.tensor_tensor(highf[:, :], dstc[:, :], lowf[:, :], ALU.subtract), chain)
            link(dve.tensor_single_scalar(highf[:, :], highf[:, :], 1.0 / P, ALU.mult), chain)
            link(dve.scalar_tensor_tensor(out=highf[:, :], in0=typc[:, :], scalar=float(Q), in1=highf[:, :],
                                          op0=ALU.mult, op1=ALU.add), chain)

            def hist(b, buf, free):
                if free:
                    dve.wait_ge(s["hist_done"], b - 1)
                at = bass.ds(b * J, J) if not isinstance(b, int) else slice(b * J, b * J + J)
                dve.tensor_tensor(oh_low[:, buf], iota.unsqueeze(1).to_broadcast([P, J, P]),
                                  lowf[:, at].unsqueeze(2).to_broadcast([P, J, P]), ALU.is_equal)
                dve.tensor_tensor(oh_high[:, buf], iota[:, 0:K * Q].unsqueeze(1).to_broadcast([P, J, K * Q]),
                                  highf[:, at].unsqueeze(2).to_broadcast([P, J, K * Q]), ALU.is_equal)\
                   .then_inc(s["hist_ready"], 1)

            hist(0, 0, False)
            with dve.Fori(0, (NB - 3) // 2) as b2:
                hist(b2 * 2 + 1, 1, True)
                hist(b2 * 2 + 2, 0, True)
            hist(NB - 2, 1, True)
            hist(NB - 1, 0, True)
            dve.wait_ge(s["hist_done"], NB)
            link(dve.tensor_copy(cnt[:, 0:K, :], B[7][:, 0:K * Q].rearrange("p (k q) -> p k q", k=K)), chain)
            link(dve.tensor_reduce(cnt[:, K, :], cnt[:, 0:K, :].rearrange("p k q -> p q k"), AX.X, ALU.add), chain)
            dve.tensor_copy(cols[:, 7:8], lane).then_inc(s["cnt_psum"], 1)

            def norm_rows(n):
                for q in range(Q):
                    dve.bn_stats(st6[:, q, :], xr[:, q, :]).then_inc(s["dve_step"], 1)
                chain.up(Q)
                dve.wait_ge(s["dve_step"], chain.value())
                for q in range(Q):
                    dve.bn_aggr(mv[:, q, :], st6[:, q, :]).then_inc(s["dve_step"], 1)
                chain.up(Q)
                dve.wait_ge(s["dve_step"], chain.value())
                dve.tensor_single_scalar(mv[:, :, 1], mv[:, :, 1], 1e-5, ALU.add).then_inc(s["ln_var"], 1)
                dve.wait_ge(s["ln_std"], n)
                link(dve.reciprocal(rstd[:, :], rstd[:, :]), chain)
                for q in range(Q):
                    dve.tensor_scalar(rows[:, q, :], xr[:, q, :], mv[:, q, 0:1], rstd[:, q:q + 1],
                                      ALU.subtract, ALU.mult).then_inc(s["dve_step"], 1)
                chain.up(Q)
                dve.wait_ge(s["dve_step"], chain.value())
                dve.tensor_single_scalar(rows[:, :, :], rows[:, :, :], 0.0, ALU.max).then_inc(s["rows_ready"], 1)

            dve.wait_ge(s["loaded"], 80)
            norm_rows(1)
            link(dve.tensor_tensor(brz[:, :], bias[:, BIH:BIH + 2], bias[:, BHH:BHH + 2], ALU.add), chain)
            dve.wait_ge(s["cnt_read"], 32)
            link(dve.tensor_single_scalar(invb[:, :], cntb[:, :], 1.0, ALU.max), chain)
            link(dve.reciprocal(invb[:, :], invb[:, :]), chain)

            def aggregate(turn, ch, n0):
                with dve.Fori(0, NB) as b:
                    blk = turn * NB + b
                    c = Count(ch + b * 7)
                    dve.wait_ge(s["edges_loaded"], (blk + 1) * 80)
                    link(dve.scalar_tensor_tensor(out=key_c[:, :], in0=b_typ[:, :], scalar=float(NP), in1=b_dst[:, :],
                                                  op0=ALU.mult, op1=ALU.add), c)
                    link(dve.scalar_tensor_tensor(out=key_r[:, :, :].rearrange("p j e -> p (j e)"), in0=r_typ[:, :],
                                                  scalar=float(NP), in1=r_dst[:, :], op0=ALU.mult, op1=ALU.add), c)
                    link(dve.tensor_tensor(same[:, :, :], key_r[:, :, :],
                                           key_c[:, :].unsqueeze(2).to_broadcast([P, J, P]), ALU.is_equal), c)
                    link(dve.tensor_tensor(earlier[:, :, :], same[:, :, :],
                                           below.unsqueeze(1).to_broadcast([P, J, P]), ALU.mult), c)
                    link(dve.tensor_reduce(dup[:, :], earlier[:, :, :], AX.X, ALU.max), c)
                    link(dve.tensor_scalar(spare[:, :], key_c[:, :], -1.0, cols[:, 7:8], ALU.mult, ALU.add), c)
                    link(dve.scalar_tensor_tensor(out=spare[:, :], in0=spare[:, :], scalar=float(K * NP),
                                                  in1=dup[:, :], op0=ALU.add, op1=ALU.mult), c)
                    dve.tensor_tensor(to_row[:, :], spare[:, :], key_c[:, :], ALU.add).then_inc(s["keys_ready"], 1)
                    for m in range(J // 4):
                        dve.wait_ge(s["comb_psum"], blk * (J // 4) + (m + 1))
                        dve.tensor_copy(comb[:, 4 * m:4 * m + 4, :].rearrange("p j f -> p (j f)"), B[6 + m][:, :])\
                           .then_inc(s["combined"], 1)

            def sage(turn, relu):
                dve.wait_ge(s["st_copied"], (turn + 1) * (K * Q // 4))
                for k in range(1, K):
                    link(dve.tensor_tensor(ST[:, 0, :], ST[:, 0, :], ST[:, k, :], ALU.add), chain)
                if turn == 0:
                    dve.wait_ge(s["tr_copied"], TG)
                    dve.tensor_tensor(ST[:, 0, :], ST[:, 0, :], invb[:, :], ALU.mult).then_inc(s["mean_ready"], 1)
                else:
                    link(dve.tensor_tensor(ST[:, 0, :], ST[:, 0, :], invb[:, :], ALU.mult), chain)
                    link(dve.tensor_tensor(ST[:, 1, :], cntb[:, :], invb[:, :], ALU.mult), chain)
                    link(dve.tensor_scalar(ST[:, 1, :], ST[:, 1, :], cols[:, 4:5], None, ALU.mult), chain)
                    link(dve.scalar_tensor_tensor(out=ST[:, 0, :], in0=ST[:, 0, :], scalar=cols[:, 3:4],
                                                  in1=ST[:, 1, :], op0=ALU.mult, op1=ALU.add), chain)
                    dve.tensor_scalar(hT[:, :], hT[:, :], cols[:, 3:4], cols[:, 4:5], ALU.mult, ALU.add)\
                       .then_inc(s["mean_ready"], 1)
                n0 = chain.value()
                with dve.Fori(0, NC) as c:
                    g = turn * NC + c
                    ch = Count(n0 + c * 1)
                    at = bass.ds(c * CH, CH)
                    dve.wait_ge(s["sg_ssq"], g + 1)
                    dve.tensor_single_scalar(rT[:, :], B[1][:, 0:CH], 1e-24, ALU.max).then_inc(s["sg_max"], 1)
                    dve.wait_ge(s["sg_std"], g + 1)
                    dve.wait_ge(s["act_step"], g + 1)
                    link(dve.reciprocal(zT[:, :], nT[:, :]), ch)
                    if relu:
                        dve.scalar_tensor_tensor(out=hT[:, at], in0=aT[:, :], scalar=0.0, in1=zT[:, :],
                                                 op0=ALU.max, op1=ALU.mult).then_inc(s["sg_done"], 1)
                    else:
                        dve.tensor_tensor(hT[:, at], aT[:, :], zT[:, :], ALU.mult).then_inc(s["sg_done"], 1)
                chain.up(NC)

            aggregate(0, chain.value(), 0)
            chain.up(7 * NB)
            sage(0, True)
            dve.wait_ge(s["sg_done"], NC)
            for q in range(Q):
                dve.bn_stats(st6[:, q, :], hT[:, q * (N // Q):(q + 1) * (N // Q)]).then_inc(s["dve_step"], 1)
            chain.up(Q)
            dve.wait_ge(s["dve_step"], chain.value())
            link(dve.bn_aggr(cols[:, 0:2], st6[:, :, :].rearrange("p q s -> p (q s)")), chain)
            dve.tensor_single_scalar(cols[:, 1:2], cols[:, 1:2], 1e-5, ALU.add).then_inc(s["bn_var"], 1)
            dve.wait_ge(s["bn_std"], 1)
            link(dve.reciprocal(cols[:, 3:4], cols[:, 2:3]), chain)
            link(dve.tensor_tensor(cols[:, 3:4], cols[:, 3:4], bias[:, GAM:GAM + 1], ALU.mult), chain)
            link(dve.tensor_tensor(cols[:, 5:6], cols[:, 0:1], cols[:, 3:4], ALU.mult), chain)
            link(dve.tensor_tensor(cols[:, 4:5], bias[:, BET:BET + 1], cols[:, 5:6], ALU.subtract), chain)
            aggregate(1, chain.value(), 0)
            chain.up(7 * NB)
            sage(1, False)
            dve.wait_ge(s["tr_copied"], 3 * TG)
            link(dve.tensor_tensor(xr[:, :, :], xr[:, :, :], rows[:, :, :], ALU.add), chain)
            norm_rows(2)
            dve.wait_ge(s["tr_copied"], 4 * TG)
            link(dve.tensor_copy(featT[:, :], hT[:, :]), chain)
            n0 = chain.value()
            per = 7 * NB + 3 * NC
            with dve.Fori(0, STEPS) as t:
                aggregate(t + 2, t * per + n0, 0)
                with dve.Fori(0, NC) as c:
                    g = t * NC + c
                    at = bass.ds(c * CH, CH)
                    ch = Count(t * per + c * 3 + (n0 + 7 * NB))
                    dve.wait_ge(s["sig_done"], g * 2 + 2)
                    link(dve.scalar_tensor_tensor(out=tT[:, :], in0=B[3][:, 0:CH], scalar=bias[:, BHH + 2:BHH + 3],
                                                  in1=rT[:, :], op0=ALU.add, op1=ALU.mult), ch)
                    dve.tensor_tensor(tT[:, :], tT[:, :], B[4][:, 0:CH], ALU.add).then_inc(s["pre_n"], 1)
                    dve.wait_ge(s["n_ready"], g + 1)
                    link(dve.tensor_tensor(rT[:, :], hT[:, at], nT[:, :], ALU.subtract), ch)
                    link(dve.tensor_tensor(rT[:, :], rT[:, :], zT[:, :], ALU.mult), ch)
                    dve.tensor_tensor(hT[:, at], rT[:, :], nT[:, :], ALU.add).then_inc(s["h_updated"], 1)
            chain.up(STEPS * per)
            n0 = chain.value()
            with dve.Fori(0, NC) as c:
                at = bass.ds(c * CH, CH)
                dve.wait_ge(s["o_sig"], c + 1)
                dve.scalar_tensor_tensor(out=hT[:, at], in0=B[1][:, 0:CH], scalar=bias[:, JB:JB + 1],
                                         in1=rT[:, :], op0=ALU.add, op1=ALU.mult).then_inc(s["o_done"], 1)
            dve.wait_ge(s["tr_copied"], (5 + STEPS) * TG)
            dve.tensor_tensor(rows[:, :, :], rows[:, :, :], xr[:, :, :], ALU.add).then_inc(s["rdy_out"], 1)


def kernel(x, src, dst, edge_type_4, L0_gnn_W_l1, L0_gnn_b_l1, L0_gnn_W_r1, L0_gnn_gamma, L0_gnn_beta,
           L0_gnn_W_l2, L0_gnn_b_l2, L0_gnn_W_r2, L1_gnn_W_et, L1_gnn_b_et, L1_gnn_W_ih, L1_gnn_b_ih,
           L1_gnn_W_hh, L1_gnn_b_hh, L1_gnn_i_w, L1_gnn_i_b, L1_gnn_j_w, L1_gnn_j_b):
    import concourse.bacc as bacc
    from concourse.bass_utils import run_bass_kernel_spmd

    def tiles_of(wt):
        wt = np.asarray(wt)
        return [wt[o:o + P, i:i + P].T for i in range(0, wt.shape[1], P) for o in range(0, wt.shape[0], P)]

    def edges(a, pad):
        a = np.asarray(a)
        full = np.full(EP, pad, a.dtype)
        full[:E] = a
        return full

    we = np.asarray(L1_gnn_W_et)
    weights = np.stack([t for wt in (L0_gnn_W_l1, L0_gnn_W_r1, L0_gnn_W_l2, L0_gnn_W_r2, we[0], we[1], we[2], we[3],
                                     L1_gnn_W_ih, L1_gnn_W_hh, L1_gnn_i_w, L1_gnn_j_w) for t in tiles_of(wt)], axis=1)
    biases = np.concatenate([np.asarray(b).reshape(-1, P) for b in (
        L0_gnn_b_l1, L0_gnn_b_l2, L0_gnn_gamma, L0_gnn_beta, L1_gnn_b_ih, L1_gnn_b_hh, L1_gnn_i_b, L1_gnn_j_b)]).T
    src_p, dst_p, typ_p = edges(src, 0), edges(dst, N), edges(edge_type_4, 0)
    lane = np.arange(P, dtype=np.float32)
    consts = np.concatenate([np.eye(P, dtype=np.float32), np.tril(np.ones((P, P), np.float32), -1),
                             np.tile(lane, (P, 1)), lane[:, None]], axis=1)
    arrays = {
        "x": np.asarray(x),
        "src_c": src_p.reshape(-1, P).T, "dst_c": dst_p.reshape(-1, P).T, "typ_c": typ_p.reshape(-1, P).T,
        "dst_r": dst_p, "typ_r": typ_p,
        "weights": weights, "biases": biases, "b_et": np.asarray(L1_gnn_b_et), "consts": consts,
    }
    arrays = {k: np.ascontiguousarray(v) for k, v in arrays.items()}
    nc = bacc.Bacc("TRN2", target_bir_lowering=False, num_devices=1)
    args = [nc.dram_tensor(k, v.shape, mybir.dt.from_np(v.dtype), kind="ExternalInput").ap()
            for k, v in arrays.items()]
    args.append(nc.dram_tensor("out", (N, D), F32, kind="ExternalOutput").ap())
    gnn_kernel(nc, *args)
    return run_bass_kernel_spmd(nc, [arrays], core_ids=[0]).results[0]["out"]
```

```python
from contextlib import ExitStack

import numpy as np

import concourse.bass as bass
from concourse import mybir

P = 128
N = 3125
D = 128
E = 103125
K = 4
STEPS = 3
Q = -(-N // P)
NP = Q * P
J = 8
TILES = -(-E // P)
NB = -(-TILES // J)
EP = NB * J * P
ACC = K * NP + P
CH = 400
NC = NP // CH
ROUNDS = 2 + STEPS
TG = -(-Q // 4)

F32 = mybir.dt.float32
F16 = mybir.dt.float16
I32 = mybir.dt.int32
ALU = mybir.AluOpType
ACT = mybir.ActivationFunctionType
AX = mybir.AxisListType

WL1, WR1, WL2, WR2, WET, WIH, WHH, IW, JW = 0, 1, 2, 3, 4, 8, 11, 14, 16
NW = 17
BL1, BL2, GAM, BET, BIH, BHH, IB, JB = 0, 1, 2, 3, 4, 7, 10, 11
NBIAS = 12


class Count:

    def __init__(self, base=0):
        self.base, self.step = base, 0

    def up(self, by=1):
        self.step += by
        return self.base + self.step

    def value(self, less=0):
        return self.base + (self.step - less)

    def loop(self, i, per):
        inner = Count(i * per + self.value())
        inner.per = per
        return inner


SLOTS = 64
KW = 816
RUN = 32
NR = 3232
Q2 = Q + 1
M = Q2 // 2
HQ = K * Q + Q
GR = 16
SC = 512
SIZES = [min(SC, NP - c) for c in range(0, NP, SC)]
NS = len(SIZES)
A_SCALE = 0.125
H_SCALE = 4096.0
UNSCALE = 1.0 / (A_SCALE * H_SCALE)
F8 = mybir.dt.float8e4
U8 = mybir.dt.uint8


def dense_kernel(nc, x, dst_c, typ_c, src_r, dst_r, typ_r, weights, biases, b_et, consts, out, redo):
    with ExitStack() as ctx:
        def sb(name, shape, dt=F32):
            return ctx.enter_context(nc.sbuf_tensor("d_" + name, shape, dt))

        adj = nc.dram_tensor("adj", [Q2, P, K * Q * P], U8, kind="Internal").ap()
        keys_dram = nc.dram_tensor("keys_dram", [P * KW], F32, kind="Internal").ap()
        shifted = nc.dram_tensor("shifted", [RUN * NR, RUN], F32, kind="Internal").ap()
        cnt_dram = nc.dram_tensor("d_cnt_dram", [K + 1, Q, P], F32, kind="Internal").ap()

        xr = sb("xr", [P, Q, D])
        rows = sb("rows", [P, Q, D])
        w = sb("w", [P, NW, P])
        bias = sb("bias", [P, NBIAS])
        brz = sb("brz", [P, 2])
        bet = sb("bet", [K, P])
        con = sb("con", [P, 3 * P + 1])
        ident, iota, above = con[:, 0:P], con[:, P:2 * P], con[:, 2 * P + 1:3 * P + 1]
        ones = sb("ones", [P, P])
        cnt = sb("cnt", [P, K + 1, Q])
        st6 = sb("st6", [P, Q, 6])
        mv = sb("mv", [P, Q, 2])
        rstd = sb("rstd", [P, Q])
        cols = sb("cols", [P, 8])
        flags = sb("flags", [P, 4])
        wide = sb("wide", [P, Q * Q2 * P], U8)
        au = wide[:, :].bitcast(F8).rearrange("p (m q n) -> p m q n", m=M, q=Q)
        widef = wide[:, :].bitcast(F32)
        blk = sb("blk", [P, 2, 2, K * Q * P], U8)
        blk8 = blk[:, :, :, :].bitcast(F8)
        blkf = blk[:, :, :, :].rearrange("p a b n -> p (a b n)").bitcast(F32)
        hT = blkf[:, 0:NP]
        cntb = blkf[:, NP:2 * NP]
        hi = blkf[:, 2 * NP:2 * NP + NP // 2].bitcast(F16).rearrange("p (q f) -> p q f", q=Q)
        lo = blkf[:, 2 * NP + NP // 2:3 * NP].bitcast(F16).rearrange("p (q f) -> p q f", q=Q)
        invb = blkf[:, 3 * NP:4 * NP]
        ublk = sb("ublk", [P, 2, Q, 2, P], U8)
        ublk8 = ublk[:, :, :, :, :].bitcast(F8)
        dstc = widef[:, 0:808].bitcast(I32)
        typc = widef[:, 808:1616].bitcast(I32)
        lowi = widef[:, 1616:2424].bitcast(I32)
        srcr = widef[:, 2424:3240].bitcast(I32)
        typr = widef[:, 3240:4056].bitcast(I32)
        dstr = widef[:, 4056:4872].bitcast(I32)
        dstn = widef[:, 4872:5688].bitcast(I32)
        keyr = widef[:, 5688:6504]
        order = widef[:, 6504:7320]
        slots = widef[:, 7320:7320 + Q2 * SLOTS]
        valid = widef[:, 9000:9000 + Q * SLOTS]
        loi = widef[:, 10640:10640 + Q2 * SLOTS].bitcast(I32)
        lof = widef[:, 12320:12320 + Q2 * SLOTS]
        hif = widef[:, 14000:14000 + Q2 * SLOTS]
        lowf = widef[:, 15700:15700 + 404].bitcast(F16)
        highf = widef[:, 16110:16110 + 808]
        high16 = widef[:, 16930:16930 + 404].bitcast(F16)
        ptr = widef[:, 17400:17400 + Q]
        tot = widef[:, 17430:17430 + Q]
        base = widef[:, 17460:17460 + Q]
        ptri = widef[:, 17490:17490 + Q].bitcast(I32)
        shf = widef[:, 17520:17520 + Q].bitcast(I32)
        cntT = widef[:, 17600:17600 + P]
        totT = widef[0:Q, 17730:17730 + P]
        row_at = sb("row_at", [P, 2, Q], I32)
        klow = sb("klow", [P, M * P], F16)
        khigh = sb("khigh", [P, M * P], F16)
        ksrc = sb("ksrc", [P, M * P], F16)
        ktmp = valid[:, 0:M * P // 2].bitcast(F16)
        iota2 = sb("iota2", [P, P, 2], F16)
        low_n, high_n = 2 * GR * P // 2, 2 * GR * HQ // 2
        work = sb("work", [P, low_n + high_n])
        oh_low = work[:, 0:low_n].bitcast(F16).rearrange("p (b i c e) -> p b i c e", b=2, c=P, e=2)
        oh_high = work[:, low_n:low_n + high_n].bitcast(F16).rearrange("p (b i c e) -> p b i c e", b=2, c=HQ, e=2)
        featT = widef[:, 0:NP]
        cnt4 = widef[0:K, NP:2 * NP]
        atile = [wide[:, 25600 + i * 12800:25600 + (i + 1) * 12800] for i in range(2)]
        sums = [widef[:, 12800 + i * 512:12800 + (i + 1) * 512] for i in range(2)]
        meanT = [work[:, i * SC:(i + 1) * SC] for i in range(2)]
        aT, rT, zT, tT, nT = (work[:, i * SC:(i + 1) * SC] for i in range(2, 7))
        OW = Q * P // 4
        orw = klow[:, 0:2 * OW].bitcast(I32)
        B = ctx.enter_context(nc.psum_tensor("banks", [P, 8, 512], F32))

        names = """edges_in consts_in order_in loaded zeros_set keys_made keys_out shifted_out row_ready slots_in
            hist_ready hist_done totals_sb before_psum kt_psum kt_copied keys_high
            cnt_psum cnt_sb cnt_written cntb_read cnt4_read
            oh_ready oh_used ps_ready typed_out all_out tile_stored0 tile_stored1
            dve_step act_step ln_var ln_std rows_ready tr_psum tr_copied hi_ready lo_ready
            sm_psum mean_ready sg_psum sg_sq sg_out sg_ssq sg_max sg_std sg_done bn_var bn_std h_final
            s_psum s_out a_loaded0 a_loaded1 a_psum a_copied gates_psum sig_done pre_n n_ready
            h_updated o_psum o_sig o_done out_ready stored flag_psum flag_ready au_stored0 au_stored1 feat_ready passed""".split()
        s = {n: ctx.enter_context(nc.semaphore("d_" + n)) for n in names}
        HB = NB

        def transpose_tiles(pe, tr, src, n=Q):
            for g in range(-(-n // 4)):
                if g:
                    pe.wait_ge(s["tr_copied"], tr.value(1))
                for m in range(min(4, n - 4 * g)):
                    ins = pe.transpose(B[:, 5 + g % 2, m * P:(m + 1) * P], src(4 * g + m), ident)
                ins.then_inc(s["tr_psum"], 1)
                tr.up()
            pe.wait_ge(s["tr_copied"], tr.value())

        def copy_tiles(act, tr, dst, n=Q):
            for g in range(-(-n // 4)):
                k = min(4, n - 4 * g)
                act.wait_ge(s["tr_psum"], tr.up())
                act.activation(dst(4 * g, k), B[:, 5 + g % 2, 0:k * P], ACT.Copy).then_inc(s["tr_copied"], 1)

        flat_rows = rows[:, :, :].rearrange("p q f -> p (q f)")
        to_hT = lambda a, k: hT[:, a * P:(a + k) * P]
        to_rows = lambda a, k: flat_rows[:, a * P:(a + k) * P]
        NT2 = 2 * M
        G2 = -(-NT2 // 4)
        block = ctx.enter_context(nc.Block())

        @block.sync
        def _(sp):
            sp.dma_start(dstc, dst_c).then_inc(s["edges_in"], 16)
            sp.dma_start(typc, typ_c).then_inc(s["edges_in"], 16)
            sp.dma_start(con[:, :], consts[:, P:4 * P + 1]).then_inc(s["consts_in"], 16)
            rowed = lambda a, o: a[o:o + P * KW].rearrange("(p i) -> p i", p=P)
            sp.dma_start(srcr, rowed(src_r, 0)).then_inc(s["order_in"], 16)
            sp.dma_start(typr, rowed(typ_r, 0)).then_inc(s["order_in"], 16)
            sp.dma_start(dstr, rowed(dst_r, 0)).then_inc(s["order_in"], 16)
            sp.dma_start(dstn, rowed(dst_r, 1)).then_inc(s["order_in"], 16)
            sp.wait_ge(s["keys_made"], 1)
            sp.dma_start(rowed(keys_dram, 0), keyr).then_inc(s["keys_out"], 16)
            sp.wait_ge(s["zeros_set"], 1)
            full = N // P
            sp.dma_start(xr[:, 0:full, :], x[0:full * P, :].rearrange("(q p) f -> p q f", p=P))\
              .then_inc(s["loaded"], 16)
            sp.dma_start(xr[0:N - full * P, full, :], x[full * P:N, :]).then_inc(s["loaded"], 16)
            sp.dma_start(w[:, :, :], weights).then_inc(s["loaded"], 16)
            sp.dma_start(bias[:, :], biases).then_inc(s["loaded"], 16)
            sp.dma_start(bet[:, :], b_et).then_inc(s["loaded"], 16)
            sp.wait_ge(s["keys_out"], 16)
            copies = shifted.rearrange("(c n) r -> c (n r)", c=RUN)
            with sp.Fori(0, RUN) as c:
                sp.dma_start(copies[bass.ds(c, 1), :].rearrange("o (a b) -> (o a) b", a=P),
                             keys_dram[bass.ds(c, NR * RUN)].rearrange("(a b) -> a b", a=P))\
                  .then_inc(s["shifted_out"], 16)
            sp.wait_ge(s["cnt_sb"], 2)
            sp.dma_start(cnt_dram[0:K].rearrange("k q p -> (k q) p"), cntT[0:K * Q, :]).then_inc(s["cnt_written"], 16)
            sp.dma_start(cnt_dram[K], totT).then_inc(s["cnt_written"], 16)

            def store(m, half):
                sp.wait_ge(s["typed_out"], (m + 1) * 32)
                sp.dma_start(adj[bass.ds(m * 2, 2)].rearrange("b p n -> p b n"), blk[:, half])\
                  .then_inc(s["tile_stored%d" % half], 16)
                sp.wait_ge(s["all_out"], (m + 1) * 32)
                sp.dma_start(wide[:, bass.ds(m * (Q * 2 * P), Q * 2 * P)],
                             ublk[:, half].rearrange("p q h d -> p (q h d)")).then_inc(s["au_stored%d" % half], 16)

            with sp.Fori(0, M // 2) as m2:
                store(m2 * 2, 0)
                store(m2 * 2 + 1, 1)
            store(M - 1, 0)
            sp.wait_ge(s["tile_stored0"], (M + 1) // 2 * 16)
            sp.wait_ge(s["tile_stored1"], M // 2 * 16)
            sp.wait_ge(s["cnt_written"], 32)
            sp.dma_start(cntb, cnt_dram[K].rearrange("q p -> (q p)").partition_broadcast(P))\
              .then_inc(s["cntb_read"], 16)
            sp.wait_ge(s["sm_psum"], 2 * NS)
            sp.wait_ge(s["flag_ready"], 1)
            sp.dma_start(cnt4, cnt_dram[0:K].rearrange("k q p -> k (q p)")).then_inc(s["cnt4_read"], 16)

            def load(c, n, i):
                sp.wait_ge(s["s_psum"], n)
                sp.dma_start(atile[i], adj[bass.ds(c, 1)].rearrange("o p n -> (o p) n"))\
                  .then_inc(s["a_loaded%d" % i], 16)

            with sp.Fori(0, STEPS) as t:
                load(0, t * Q, 0)
                load(1, t * Q, 1)
                with sp.Fori(0, Q // 2 - 1) as c2:
                    load(c2 * 2 + 2, t * Q + (c2 * 2 + 1), 0)
                    load(c2 * 2 + 3, t * Q + (c2 * 2 + 2), 1)
                load(Q - 1, t * Q + (Q - 2), 0)
            sp.wait_ge(s["out_ready"], 1)
            sp.dma_start(out[0:full * P, :].rearrange("(q p) f -> p q f", p=P), rows[:, 0:full, :])\
              .then_inc(s["stored"], 16)
            sp.dma_start(out[full * P:N, :], rows[0:N - full * P, full, :]).then_inc(s["stored"], 16)
            sp.wait_ge(s["stored"], 32)

        @block.gpsimd
        def _(pool):
            pool.memset(xr[:, :, :], 0.0).then_inc(s["zeros_set"], 1)
            pool.wait_ge(s["row_ready"], 1)
            pool.wait_ge(s["shifted_out"], 16 * RUN)
            for q in range(Q):
                for half in range(2):
                    pool.indirect_dma_start(slots[:, q * SLOTS + half * RUN:q * SLOTS + (half + 1) * RUN], None,
                                            shifted, bass.IndirectOffsetOnAxis(ap=row_at[:, half, q:q + 1], axis=0))\
                        .then_inc(s["slots_in"], 16)

        @block.tensor
        def _(pe):
            def hist(b, buf, first, last):
                pe.wait_ge(s["hist_ready"], b + 1)
                for j in range(J):
                    ins = pe.matmul(B[:, 7, 0:K * Q], oh_low[:, buf, j // 2, :, j % 2], oh_high[:, buf, j // 2, 0:K * Q, j % 2],
                                    start=first and j == 0, stop=last and j == J - 1)
                ins.then_inc(s["hist_done"], 1)

            hist(0, 0, True, False)
            with pe.Fori(0, (HB - 3) // 2) as b2:
                hist(b2 * 2 + 1, 1, False, False)
                hist(b2 * 2 + 2, 0, False, False)
            hist(HB - 2, 1, False, False)
            hist(HB - 1, 0, False, True)
            pe.wait_ge(s["totals_sb"], 1)
            pe.matmul(B[:, 0, 0:Q], above, tot, start=True, stop=True)
            pe.matmul(B[:, 0, 64:64 + Q], ones[:, :], tot, start=True, stop=True).then_inc(s["before_psum"], 1)
            pe.transpose(B[0:K * Q, 1, 0:P], cnt[:, 0:K, :].rearrange("p k q -> p (k q)"), ident)
            pe.transpose(B[0:Q, 1, P:2 * P], cnt[:, K, :], ident).then_inc(s["cnt_psum"], 1)
            pe.wait_ge(s["keys_high"], 1)
            pe.wait_ge(s["cnt_sb"], 2)
            for g in range(G2):
                if g >= 2:
                    pe.wait_ge(s["kt_copied"], g - 1)
                for m in range(min(4, NT2 - 4 * g)):
                    i = 4 * g + m
                    part = (lof if i < M else hif)[:, (i % M) * P:(i % M + 1) * P]
                    ins = pe.transpose(B[:, g % 2, m * P:(m + 1) * P], part, ident)
                ins.then_inc(s["kt_psum"], 1)
            pe.wait_ge(s["kt_copied"], G2)

            def build(it, first):
                for buf in range(2):
                    pe.wait_ge(s["oh_ready"], it * 2 + (buf + 1))
                    for g4 in range(4):
                        g = buf * 4 + g4
                        if not first or buf:
                            pe.wait_ge(s["typed_out"], it * 8 + (g - 3))
                            pe.wait_ge(s["all_out"], it * 8 + (g - 3))
                        for h in range(2):
                            for i in range(4):
                                r = g4 * 4 + i
                                ins = pe.matmul(B[:, 2 * g4 + h, i * HQ:(i + 1) * HQ],
                                                oh_low[64 * h:64 * h + 64, buf, r // 2, :, r % 2],
                                                oh_high[64 * h:64 * h + 64, buf, r // 2, :, r % 2],
                                                start=True, stop=True)
                        ins.then_inc(s["ps_ready"], 1)

            build(0, True)
            with pe.Fori(1, M * 4) as it:
                build(it, False)
            pe.wait_ge(s["typed_out"], M * 32)
            pe.wait_ge(s["all_out"], M * 32)

            tr = Count()

            def sage(n, w_agg, w_own):
                pe.wait_ge(s["lo_ready"], n + 1)
                pe.wait_ge(s["hi_ready"], n + 1)

                def project(c):
                    g, at = n * NS + c, slice(c * SC, c * SC + SIZES[c])
                    if g:
                        pe.wait_ge(s["sg_done"], g)
                    pe.wait_ge(s["mean_ready"], g + 1)
                    pe.matmul(B[:, 2, 0:SIZES[c]], w[:, w_agg, :], meanT[g % 2][:, 0:SIZES[c]], start=True, stop=False)
                    pe.matmul(B[:, 2, 0:SIZES[c]], w[:, w_own, :], hT[:, at], start=False, stop=True)\
                      .then_inc(s["sg_psum"], 1)

                def squares(c):
                    pe.wait_ge(s["sg_sq"], n * NS + c + 1)
                    pe.matmul(B[:, 3, 0:SIZES[c]], ones[:, :], tT[:, 0:SIZES[c]], start=True, stop=True)\
                      .then_inc(s["sg_ssq"], 1)

                for c in range(NS):
                    g = n * NS + c
                    if g >= 2:
                        pe.wait_ge(s["mean_ready"], g - 1)
                    pairs = slice(2 * c, min(2 * c + 2, M))
                    for q in range(Q):
                        edges = au[:, pairs, q, :] if SIZES[c] == SC else au[:, 2 * c, q, 0:SIZES[c]]
                        for part in (hi, lo):
                            ins = pe.matmul(B[:, g % 2, 0:SIZES[c]], part[:, q, :], edges,
                                            start=q == 0 and part is hi, stop=q == Q - 1 and part is lo)
                        if q == Q // 2 and c:
                            project(c - 1)
                    ins.then_inc(s["sm_psum"], 1)
                    if c:
                        squares(c - 1)
                project(NS - 1)
                squares(NS - 1)
                pe.wait_ge(s["sg_done"], (n + 1) * NS)

            pe.wait_ge(s["rows_ready"], 1)
            pe.wait_ge(s["cntb_read"], 16)
            pe.wait_ge(s["au_stored0"], (M + 1) // 2 * 16)
            pe.wait_ge(s["au_stored1"], M // 2 * 16)
            transpose_tiles(pe, tr, lambda q: rows[:, q, :])
            sage(0, WL1, WR1)
            transpose_tiles(pe, tr, lambda q: hT[:, q * P:(q + 1) * P])
            pe.wait_ge(s["flag_psum"], 1)
            pe.matmul(B[0:1, 7, 0:1], flags[:, 3:4], ones[:, 0:1], start=True, stop=True).then_inc(s["flag_psum"], 1)
            sage(1, WL2, WR2)
            transpose_tiles(pe, tr, lambda q: hT[:, q * P:(q + 1) * P])
            pe.wait_ge(s["rows_ready"], 2)
            transpose_tiles(pe, tr, lambda q: rows[:, q, :])

            def gather_sums(n, i, free, between):
                pe.wait_ge(s["a_loaded%d" % i], (n + 1) * 16)
                pe.wait_ge(s["s_out"], free)
                pe.sem_inc(s["passed"], 1)
                a4 = atile[i].bitcast(F8).rearrange("p (k q d) -> p k q d", k=K, q=Q)
                for q in range(Q):
                    for part in (hi, lo):
                        ins = pe.matmul(B[:, i, :], part[:, q, :], a4[:, :, q, :],
                                        start=q == 0 and part is hi, stop=q == Q - 1 and part is lo)
                    if q == Q // 2 and between:
                        between()
                ins.then_inc(s["s_psum"], 1)

            def messages(g, i):
                def go():
                    pe.wait_ge(s["s_out"], g + 1)
                    pe.wait_ge(s["a_copied"], g)
                    for k in range(K):
                        pe.matmul(B[:, 2, 0:P], w[:, WET + k, :], sums[i][:, k * P:(k + 1) * P],
                                  start=k == 0, stop=False)
                    pe.matmul(B[:, 2, 0:P], bet[:, :], cnt4[:, bass.ds(tile_of(g), P)], start=False, stop=True)\
                      .then_inc(s["a_psum"], 1)
                return go

            def gates(g):
                at = bass.ds(tile_of(g), P)
                pe.wait_ge(s["a_copied"], g + 1)
                pe.wait_ge(s["pre_n"], g)
                for m in range(2):
                    pe.matmul(B[:, 3, m * P:(m + 1) * P], w[:, WIH + m, :], aT[:, 0:P], start=True, stop=False)
                    pe.matmul(B[:, 3, m * P:(m + 1) * P], w[:, WHH + m, :], hT[:, at], start=False, stop=True)
                pe.matmul(B[:, 4, 0:P], w[:, WHH + 2, :], hT[:, at], start=True, stop=True)
                pe.matmul(B[:, 4, P:2 * P], w[:, WIH + 2, :], aT[:, 0:P], start=True, stop=True)\
                  .then_inc(s["gates_psum"], 1)

            place = {}

            def tile_of(g):
                return place["at"]

            pe.wait_ge(s["cnt4_read"], 16)
            with pe.Fori(0, STEPS) as t:
                pe.wait_ge(s["hi_ready"], t + 3)
                pe.wait_ge(s["lo_ready"], t + 3)
                gather_sums(t * 13, 0, t * Q, None)
                with pe.Fori(0, Q // 2) as c2:
                    for i, c in ((1, c2 * 2 + 1), (0, c2 * 2 + 2)):
                        g = t * Q + c
                        place["at"] = (c - 1) * P
                        gather_sums(t * 12 + c2 if i else t * 13 + (c2 + 1), i, g - 1, messages(g - 1, 1 - i))
                        gates(g - 1)
                place["at"] = (Q - 1) * P
                messages(t * Q + (Q - 1), 0)()
                gates(t * Q + (Q - 1))
                pe.wait_ge(s["h_updated"], (t + 1) * Q)
                transpose_tiles(pe, Count(t * TG + 4 * TG), lambda q: hT[:, q * P:(q + 1) * P])
            with pe.Fori(0, NC) as c:
                at = bass.ds(c * CH, CH)
                pe.wait_ge(s["o_done"], c)
                pe.matmul(B[:, 0, 0:CH], w[:, IW, :], hT[:, at], start=True, stop=False)
                pe.matmul(B[:, 0, 0:CH], w[:, IW + 1, :], featT[:, at], start=False, stop=True)
                pe.matmul(B[:, 1, 0:CH], w[:, JW, :], hT[:, at], start=True, stop=True).then_inc(s["o_psum"], 1)
            pe.wait_ge(s["o_done"], NC)
            transpose_tiles(pe, Count((4 + STEPS) * TG), lambda q: hT[:, q * P:(q + 1) * P])

        @block.scalar
        def _(act):
            act.wait_ge(s["cnt_psum"], 1)
            act.activation(cntT[0:K * Q, :], B[0:K * Q, 1, 0:P], ACT.Copy).then_inc(s["cnt_sb"], 1)
            act.activation(totT, B[0:Q, 1, P:2 * P], ACT.Copy).then_inc(s["cnt_sb"], 1)
            act.wait_ge(s["ln_var"], 1)
            act.activation(rstd[:, :], mv[:, :, 1], ACT.Sqrt).then_inc(s["ln_std"], 1)
            for g in range(G2):
                k = min(4, NT2 - 4 * g)
                act.wait_ge(s["kt_psum"], g + 1)
                for a, b, dst in ((0, M, klow), (M, NT2, khigh)):
                    p0, p1 = max(a, 4 * g), min(b, 4 * g + k)
                    if p0 < p1:
                        ins = act.activation(dst[:, (p0 - a) * P:(p1 - a) * P], B[:, g % 2, (p0 - 4 * g) * P:(p1 - 4 * g) * P],
                                             ACT.Copy)
                        if p1 < 4 * g + k:
                            ins.then_inc(s["act_step"], 1)
                ins.then_inc(s["kt_copied"], 1)

            def pair(m, half, old):
                if old is not None:
                    act.wait_ge(s["tile_stored%d" % half], old * 16)
                tiles = blk8[:, half].rearrange("p h (x d) -> p h x d", d=P)
                for g in range(32):
                    act.wait_ge(s["ps_ready"], m * 32 + (g + 1))
                    act.sem_inc(s["passed"], 1)
                    made = B[:, 2 * (g % 4):2 * (g % 4) + 2, 0:4 * HQ].rearrange("p h (i x) -> p h x i", i=4)
                    act.activation(tiles[:, :, :, 4 * g:4 * g + 4], made[:, :, 0:K * Q, :], ACT.Copy, scale=A_SCALE,
                                   saturate=False).then_inc(s["typed_out"], 1)

            pair(0, 0, None)
            pair(1, 1, None)
            with act.Fori(1, M // 2) as m2:
                pair(m2 * 2, 0, m2)
                pair(m2 * 2 + 1, 1, m2)
            pair(M - 1, 0, M // 2)

            tr = Count()

            def split(n, src):
                act.activation(hi.rearrange("p q f -> p (q f)"), src, ACT.Copy, scale=H_SCALE)\
                   .then_inc(s["hi_ready"], 1)

            def sage(n, b):
                for c in range(NS):
                    g, z = n * NS + c, SIZES[c]
                    act.wait_ge(s["sg_psum"], g + 1)
                    act.activation(tT[:, 0:z], B[:, 2, 0:z], ACT.Square, bias=bias[:, b:b + 1]).then_inc(s["sg_sq"], 1)
                    act.activation(aT[:, 0:z], B[:, 2, 0:z], ACT.Identity, bias=bias[:, b:b + 1])\
                       .then_inc(s["sg_out"], 1)
                    act.wait_ge(s["sg_max"], g + 1)
                    act.activation(nT[:, 0:z], rT[:, 0:z], ACT.Sqrt).then_inc(s["sg_std"], 1)

            act.wait_ge(s["cntb_read"], 16)
            split(0, flat_rows)
            copy_tiles(act, tr, to_hT)
            sage(0, BL1)
            act.wait_ge(s["bn_var"], 1)
            act.activation(cols[:, 2:3], cols[:, 1:2], ACT.Sqrt).then_inc(s["bn_std"], 1)
            copy_tiles(act, tr, to_rows)
            act.wait_ge(s["tr_copied"], 2 * TG)
            split(1, flat_rows)
            sage(1, BL2)
            copy_tiles(act, tr, to_rows)
            act.wait_ge(s["ln_var"], 2)
            act.activation(rstd[:, :], mv[:, :, 1], ACT.Sqrt).then_inc(s["ln_std"], 1)
            act.wait_ge(s["rows_ready"], 2)
            split(2, flat_rows)
            copy_tiles(act, tr, to_hT)

            def update(g, i, first):
                act.wait_ge(s["s_psum"], g + 1)
                if not first:
                    act.wait_ge(s["a_psum"], g - 1)
                act.activation(sums[i], B[:, i, :], ACT.Copy, scale=UNSCALE).then_inc(s["s_out"], 1)
                act.wait_ge(s["a_psum"], g + 1)
                act.wait_ge(s["gates_psum"], g)
                act.activation(aT[:, 0:P], B[:, 2, 0:P], ACT.Copy).then_inc(s["a_copied"], 1)
                act.wait_ge(s["gates_psum"], g + 1)
                act.wait_ge(s["h_updated"], g)
                act.activation(rT[:, 0:P], B[:, 3, 0:P], ACT.Sigmoid, bias=brz[:, 0:1]).then_inc(s["sig_done"], 1)
                act.activation(zT[:, 0:P], B[:, 3, P:2 * P], ACT.Sigmoid, bias=brz[:, 1:2]).then_inc(s["sig_done"], 1)
                act.wait_ge(s["pre_n"], g + 1)
                act.activation(nT[:, 0:P], tT[:, 0:P], ACT.Tanh, bias=bias[:, BIH + 2:BIH + 3])\
                   .then_inc(s["n_ready"], 1)

            act.wait_ge(s["flag_ready"], 1)
            with act.Fori(0, STEPS) as t:
                update(t * Q, 0, True)
                with act.Fori(0, Q // 2) as c2:
                    update(t * Q + (c2 * 2 + 1), 1, False)
                    update(t * Q + (c2 * 2 + 2), 0, False)
                inner = Count(t * TG + 4 * TG)
                copy_tiles(act, inner, to_rows)
                act.wait_ge(s["tr_copied"], inner.value())
                split(3, flat_rows)
            with act.Fori(0, NC) as c:
                act.wait_ge(s["o_psum"], c + 1)
                act.activation(rT[:, 0:CH], B[:, 0, 0:CH], ACT.Sigmoid, bias=bias[:, IB:IB + 1]).then_inc(s["o_sig"], 1)
            copy_tiles(act, Count((4 + STEPS) * TG), to_rows)

        @block.vector
        def _(dve):
            chain = Count()

            def link(ins, ch=chain):
                ins.then_inc(s["dve_step"], 1)
                dve.wait_ge(s["dve_step"], ch.up())

            dve.memset(ones[:, :], 1.0)
            dve.wait_ge(s["consts_in"], 16)
            link(dve.tensor_copy(iota2[:, :, :], iota.unsqueeze(2).to_broadcast([P, P, 2])))
            dve.wait_ge(s["edges_in"], 32)
            link(dve.tensor_single_scalar(lowi, dstc, P - 1, ALU.bitwise_and))
            link(dve.tensor_copy(lowf, lowi))
            link(dve.tensor_tensor(highf, dstc, lowf, ALU.subtract))
            link(dve.tensor_single_scalar(highf, highf, 1.0 / P, ALU.mult))
            link(dve.scalar_tensor_tensor(out=high16, in0=typc, scalar=float(Q), in1=highf, op0=ALU.mult, op1=ALU.add))
            dve.wait_ge(s["order_in"], 64)
            dve.scalar_tensor_tensor(out=keyr, in0=typr, scalar=float(NP), in1=srcr, op0=ALU.mult, op1=ALU.add)\
               .then_inc(s["keys_made"], 1)

            def one_hots(buf, n, width, column, keys, at, out_t):
                k = keys[:, at].rearrange("p (i e) -> p i e", e=2).unsqueeze(2).to_broadcast([P, n // 2, width, 2])
                io = iota2[:, 0:width, :].unsqueeze(1).to_broadcast([P, n // 2, width, 2])
                return dve.tensor_tensor(out_t[:, buf, 0:n // 2, column:column + width, :], io, k, ALU.is_equal)

            def hist(b, buf, free):
                if free:
                    dve.wait_ge(s["hist_done"], b - 1)
                at = bass.ds(b * J, J) if not isinstance(b, int) else slice(b * J, b * J + J)
                one_hots(buf, J, P, 0, lowf, at, oh_low)
                one_hots(buf, J, K * Q, 0, high16, at, oh_high).then_inc(s["hist_ready"], 1)

            hist(0, 0, False)
            with dve.Fori(0, (HB - 3) // 2) as b2:
                hist(b2 * 2 + 1, 1, True)
                hist(b2 * 2 + 2, 0, True)
            hist(HB - 2, 1, True)
            hist(HB - 1, 0, True)
            dve.wait_ge(s["hist_done"], HB)
            link(dve.tensor_copy(cnt[:, 0:K, :], B[:, 7, 0:K * Q].rearrange("p (k q) -> p k q", k=K)))
            link(dve.tensor_reduce(cnt[:, K, :], cnt[:, 0:K, :].rearrange("p k q -> p q k"), AX.X, ALU.add))
            dve.tensor_copy(tot, cnt[:, K, :]).then_inc(s["totals_sb"], 1)
            dve.wait_ge(s["before_psum"], 1)
            link(dve.memset(base, 0.0))
            link(dve.memset(valid[:, Q:2 * Q], 0.0))
            link(dve.tensor_copy(valid[:, 0:Q], B[:, 0, 64:64 + Q]))
            link(dve.tensor_tensor_scan(base[:, 1:Q], valid[:, 0:Q - 1], valid[:, Q:2 * Q - 1], 0.0, ALU.add, ALU.add))
            link(dve.tensor_tensor(ptri, B[:, 0, 0:Q], base, ALU.add))
            link(dve.tensor_single_scalar(shf, ptri, RUN - 1, ALU.bitwise_and))
            link(dve.tensor_single_scalar(ptri, ptri, 5, ALU.arith_shift_right))
            link(dve.scalar_tensor_tensor(out=row_at[:, 0, :], in0=shf, scalar=float(NR), in1=ptri,
                                          op0=ALU.mult, op1=ALU.add))
            dve.tensor_single_scalar(row_at[:, 1, :], row_at[:, 0, :], 1.0, ALU.add).then_inc(s["row_ready"], 1)

            def norm_rows(n):
                for q in range(Q):
                    dve.bn_stats(st6[:, q, :], xr[:, q, :]).then_inc(s["dve_step"], 1)
                chain.up(Q)
                dve.wait_ge(s["dve_step"], chain.value())
                for q in range(Q):
                    dve.bn_aggr(mv[:, q, :], st6[:, q, :]).then_inc(s["dve_step"], 1)
                chain.up(Q)
                dve.wait_ge(s["dve_step"], chain.value())
                dve.tensor_single_scalar(mv[:, :, 1], mv[:, :, 1], 1e-5, ALU.add).then_inc(s["ln_var"], 1)
                dve.wait_ge(s["ln_std"], n)
                link(dve.reciprocal(rstd[:, :], rstd[:, :]))
                for q in range(Q):
                    dve.tensor_scalar(rows[:, q, :], xr[:, q, :], mv[:, q, 0:1], rstd[:, q:q + 1],
                                      ALU.subtract, ALU.mult).then_inc(s["dve_step"], 1)
                chain.up(Q)
                dve.wait_ge(s["dve_step"], chain.value())
                dve.tensor_single_scalar(flat_rows, flat_rows, 0.0, ALU.max).then_inc(s["rows_ready"], 1)

            link(dve.tensor_tensor(order, dstr, dstn, ALU.subtract))
            link(dve.tensor_reduce(flags[:, 0:1], order, AX.X, ALU.max))
            link(dve.tensor_reduce(flags[:, 1:2], tot, AX.X, ALU.max))
            slot_v = valid.rearrange("p (q j) -> p q j", j=SLOTS)
            link(dve.tensor_tensor(slot_v, iota[:, 0:SLOTS].unsqueeze(1).to_broadcast([P, Q, SLOTS]),
                                   tot.unsqueeze(2).to_broadcast([P, Q, SLOTS]), ALU.is_lt))
            dve.wait_ge(s["loaded"], 80)
            link(dve.tensor_tensor(brz[:, :], bias[:, BIH:BIH + 2], bias[:, BHH:BHH + 2], ALU.add))
            norm_rows(1)
            used = slice(0, Q * SLOTS)
            dve.wait_ge(s["slots_in"], 2 * Q * 16)
            link(dve.memset(slots[:, Q * SLOTS:Q2 * SLOTS], -1.0))
            link(dve.scalar_tensor_tensor(out=slots[:, used], in0=slots[:, used], scalar=1.0, in1=valid,
                                          op0=ALU.add, op1=ALU.mult))
            link(dve.tensor_single_scalar(slots[:, used], slots[:, used], -1.0, ALU.add))
            link(dve.tensor_copy(loi, slots))
            link(dve.tensor_single_scalar(loi, loi, P - 1, ALU.bitwise_and))
            link(dve.tensor_copy(lof, loi))
            link(dve.tensor_tensor(hif, slots, lof, ALU.subtract))
            dve.tensor_single_scalar(hif, hif, 1.0 / P, ALU.mult).then_inc(s["keys_high"], 1)
            dve.wait_ge(s["kt_copied"], G2)
            link(dve.tensor_copy(ksrc[:, :], khigh[:, :]))
            for k in range(1, K):
                link(dve.tensor_scalar(ktmp[:, :], khigh[:, :], float(k * Q), -float(Q), ALU.is_ge, ALU.mult))
                link(dve.tensor_tensor(ksrc[:, :], ksrc[:, :], ktmp[:, :], ALU.add))

            def ones_of(u, last_done, buf, at):
                if last_done is not None:
                    dve.wait_ge(s["ps_ready"], last_done)
                one_hots(buf, GR, P, 0, klow, at, oh_low)
                one_hots(buf, GR, K * Q, 0, khigh, at, oh_high)
                one_hots(buf, GR, Q, K * Q, ksrc, at, oh_high).then_inc(s["oh_ready"], 1)

            def all_out(u, g0, half):
                for i in range(4):
                    g = 4 * u + i
                    dve.wait_ge(s["typed_out"], g0 + (g + 1))
                    dve.sem_inc(s["passed"], 1)
                    made = B[:, 2 * i:2 * i + 2, 0:4 * HQ].rearrange("p h (i x) -> p h x i", i=4)
                    dve.tensor_scalar(ublk8[:, half].rearrange("p q h d -> p h q d")[:, :, :, 4 * g:4 * g + 4],
                                      made[:, :, K * Q:HQ, :], A_SCALE, None, ALU.mult, saturate=False)\
                       .then_inc(s["all_out"], 1)

            def pair(m, half, old):
                for u in range(8):
                    at = bass.ds(m * P + u * GR, GR)
                    ones_of(u, m * 32 + (4 * u - 4) if not first(m) or u >= 2 else None, u % 2, at)
                    if u:
                        all_out(u - 1, m * 32, half)
                    elif not first(m):
                        all_out(7, (m - 1) * 32, 1 - half)
                    if u == 0 and old is not None:
                        dve.wait_ge(s["au_stored%d" % half], old * 16)

            dve.wait_ge(s["cnt_written"], 32)
            first = lambda m: isinstance(m, int) and m == 0
            pair(0, 0, None)
            pair(1, 1, None)
            with dve.Fori(1, M // 2) as m2:
                pair(m2 * 2, 0, m2)
                pair(m2 * 2 + 1, 1, m2)
            pair(M - 1, 0, M // 2)
            all_out(7, (M - 1) * 32, 0)

            def split(n):
                dve.wait_ge(s["hi_ready"], n + 1)
                dve.scalar_tensor_tensor(out=lo.rearrange("p q f -> p (q f)"), in0=flat_rows, scalar=H_SCALE,
                                         in1=hi.rearrange("p q f -> p (q f)"), op0=ALU.mult, op1=ALU.subtract)\
                   .then_inc(s["lo_ready"], 1)

            words = wide[:, :].bitcast(I32).rearrange("p (x n) -> p x n", n=OW)

            def look(x):
                if x == 0:
                    link(dve.tensor_copy(orw, words[:, 0, :]))
                else:
                    link(dve.tensor_tensor(orw, orw, words[:, x, :], ALU.bitwise_or))

            def sage(n, relu):
                def mean(c):
                    g, z = n * NS + c, SIZES[c]
                    dve.wait_ge(s["sm_psum"], g + 1)
                    if g >= 2:
                        dve.wait_ge(s["sg_psum"], g - 1)
                    got = meanT[g % 2][:, 0:z]
                    ins = dve.scalar_tensor_tensor(out=got, in0=B[:, g % 2, 0:z], scalar=UNSCALE,
                                                   in1=invb[:, c * SC:c * SC + z], op0=ALU.mult, op1=ALU.mult)
                    if n:
                        link(ins)
                        ins = dve.scalar_tensor_tensor(out=got, in0=got, scalar=cols[:, 3:4],
                                                       in1=cntb[:, c * SC:c * SC + z], op0=ALU.mult, op1=ALU.add)
                    ins.then_inc(s["mean_ready"], 1)

                def normed(c):
                    g, z = n * NS + c, SIZES[c]
                    at = slice(c * SC, c * SC + z)
                    dve.wait_ge(s["sg_ssq"], g + 1)
                    dve.tensor_single_scalar(rT[:, 0:z], B[:, 3, 0:z], 1e-24, ALU.max).then_inc(s["sg_max"], 1)
                    dve.wait_ge(s["sg_std"], g + 1)
                    dve.wait_ge(s["sg_out"], g + 1)
                    link(dve.reciprocal(zT[:, 0:z], nT[:, 0:z]))
                    if relu:
                        ins = dve.scalar_tensor_tensor(out=hT[:, at], in0=aT[:, 0:z], scalar=0.0, in1=zT[:, 0:z],
                                                       op0=ALU.max, op1=ALU.mult)
                    else:
                        ins = dve.tensor_tensor(hT[:, at], aT[:, 0:z], zT[:, 0:z], ALU.mult)
                    ins.then_inc(s["sg_done"], 1)

                for c in range(NS):
                    mean(c)
                    if c:
                        normed(c - 1)
                    if n == 0:
                        for x in range(4 * c, min(4 * c + 4, 2 * M)):
                            look(x)
                normed(NS - 1)
                dve.wait_ge(s["sg_done"], (n + 1) * NS)

            dve.wait_ge(s["cntb_read"], 16)
            dve.wait_ge(s["au_stored0"], (M + 1) // 2 * 16)
            dve.wait_ge(s["au_stored1"], M // 2 * 16)
            split(0)
            link(dve.tensor_single_scalar(invb, cntb, 1.0, ALU.max))
            link(dve.reciprocal(invb, invb))
            sage(0, True)
            for q in range(Q):
                dve.bn_stats(st6[:, q, :], hT[:, q * (N // Q):(q + 1) * (N // Q)]).then_inc(s["dve_step"], 1)
            chain.up(Q)
            dve.wait_ge(s["dve_step"], chain.value())
            link(dve.bn_aggr(cols[:, 0:2], st6[:, :, :].rearrange("p q s -> p (q s)")))
            dve.tensor_single_scalar(cols[:, 1:2], cols[:, 1:2], 1e-5, ALU.add).then_inc(s["bn_var"], 1)
            link(dve.tensor_single_scalar(orw, orw, 0x40404040, ALU.bitwise_and))
            link(dve.tensor_reduce(flags[:, 2:3], orw, AX.X, ALU.max))
            link(dve.tensor_scalar(flags[:, 1:2], flags[:, 1:2], float(SLOTS), None, ALU.is_gt))
            link(dve.tensor_single_scalar(flags[:, 0:1], flags[:, 0:1], 0.0, ALU.is_gt))
            link(dve.tensor_single_scalar(flags[:, 2:3], flags[:, 2:3], 0.0, ALU.is_gt))
            dve.tensor_reduce(flags[:, 3:4], flags[:, 0:3], AX.X, ALU.add).then_inc(s["flag_psum"], 1)
            dve.wait_ge(s["flag_psum"], 2)
            dve.tensor_copy(redo, B[0:1, 7, 0:1]).then_inc(s["flag_ready"], 1)
            dve.wait_ge(s["bn_std"], 1)
            link(dve.reciprocal(cols[:, 3:4], cols[:, 2:3]))
            link(dve.tensor_tensor(cols[:, 3:4], cols[:, 3:4], bias[:, GAM:GAM + 1], ALU.mult))
            link(dve.tensor_tensor(cols[:, 5:6], cols[:, 0:1], cols[:, 3:4], ALU.mult))
            link(dve.tensor_tensor(cols[:, 4:5], bias[:, BET:BET + 1], cols[:, 5:6], ALU.subtract))
            split(1)
            link(dve.tensor_tensor(cntb, cntb, invb, ALU.mult))
            link(dve.tensor_scalar(cntb, cntb, cols[:, 4:5], None, ALU.mult))
            dve.wait_ge(s["tr_copied"], 2 * TG)
            link(dve.tensor_scalar(hT, hT, cols[:, 3:4], cols[:, 4:5], ALU.mult, ALU.add))
            sage(1, False)
            dve.wait_ge(s["tr_copied"], 3 * TG)
            link(dve.tensor_tensor(xr[:, :, :], xr[:, :, :], rows[:, :, :], ALU.add))
            norm_rows(2)
            split(2)
            dve.wait_ge(s["tr_copied"], 4 * TG)
            dve.tensor_copy(featT, hT).then_inc(s["feat_ready"], 1)

            def update(g, at, ch):
                dve.wait_ge(s["sig_done"], g * 2 + 2)
                link(dve.scalar_tensor_tensor(out=tT[:, 0:P], in0=B[:, 4, 0:P], scalar=bias[:, BHH + 2:BHH + 3],
                                              in1=rT[:, 0:P], op0=ALU.add, op1=ALU.mult), ch)
                dve.tensor_tensor(tT[:, 0:P], tT[:, 0:P], B[:, 4, P:2 * P], ALU.add).then_inc(s["pre_n"], 1)
                dve.wait_ge(s["n_ready"], g + 1)
                link(dve.tensor_tensor(rT[:, 0:P], hT[:, at], nT[:, 0:P], ALU.subtract), ch)
                link(dve.tensor_tensor(rT[:, 0:P], rT[:, 0:P], zT[:, 0:P], ALU.mult), ch)
                dve.tensor_tensor(hT[:, at], rT[:, 0:P], nT[:, 0:P], ALU.add).then_inc(s["h_updated"], 1)

            n0 = chain.value()
            dve.wait_ge(s["feat_ready"], 1)
            with dve.Fori(0, STEPS) as t:
                with dve.Fori(0, Q) as c:
                    g = t * Q + c
                    update(g, bass.ds(c * P, P), Count(g * 3 + n0))
                split(t + 3)
            with dve.Fori(0, NC) as c:
                at = bass.ds(c * CH, CH)
                dve.wait_ge(s["o_sig"], c + 1)
                dve.scalar_tensor_tensor(out=hT[:, at], in0=B[:, 1, 0:CH], scalar=bias[:, JB:JB + 1],
                                         in1=rT[:, 0:CH], op0=ALU.add, op1=ALU.mult).then_inc(s["o_done"], 1)
            dve.wait_ge(s["tr_copied"], (5 + STEPS) * TG)
            dve.tensor_tensor(rows[:, :, :], rows[:, :, :], xr[:, :, :], ALU.add).then_inc(s["out_ready"], 1)


def general_kernel(nc, x, src_c, dst_c, typ_c, dst_r, typ_r, weights, biases, b_et, consts, out, redo):
    with ExitStack() as ctx:
        def sb(name, shape, dt=F32):
            return ctx.enter_context(nc.sbuf_tensor(name, shape, dt))

        def sem(name):
            return ctx.enter_context(nc.semaphore(name))

        table = nc.dram_tensor("table", [NP, D], F32, kind="Internal").ap()
        acc = nc.dram_tensor("acc", [ACC, D], F32, kind="Internal").ap()
        cnt_dram = nc.dram_tensor("cnt_dram", [K + 1, Q, P], F32, kind="Internal").ap()

        xr = sb("xr", [P, Q, D])
        rows = sb("rows", [P, Q, D])
        hT = sb("hT", [P, NP])
        featT = sb("featT", [P, NP])
        ST = sb("ST", [P, K, NP])
        zeros = sb("zeros", [P, ACC * D // P // 32])
        w = sb("w", [P, NW, P])
        bias = sb("bias", [P, NBIAS])
        brz = sb("brz", [P, 2])
        bet = sb("bet", [K, P])
        con = sb("con", [P, 3 * P + 1])
        below, ident, iota, lane = con[:, 0:P], con[:, P:2 * P], con[:, 2 * P:3 * P], con[:, 3 * P:3 * P + 1]
        ones = sb("ones", [P, P])
        dstc = sb("dstc", [P, NB * J], I32)
        typc = sb("typc", [P, NB * J], I32)
        lowi = ST[:, 0, 0:NB * J].bitcast(I32)
        lowf = sb("lowf", [P, NB * J])
        highf = sb("highf", [P, NB * J])
        oh_low = sb("oh_low", [P, 2, J, P], F16)
        oh_high = sb("oh_high", [P, 2, J, K * Q], F16)
        cnt = sb("cnt", [P, K + 1, Q])
        cntT = sb("cntT", [P, P])
        totT = sb("totT", [Q, P])
        cnt4 = sb("cnt4", [K, NP])
        cntb = sb("cntb", [P, NP])
        invb = sb("invb", [P, NP])
        st6 = sb("st6", [P, Q, 6])
        mv = sb("mv", [P, Q, 2])
        rstd = sb("rstd", [P, Q])
        cols = sb("cols", [P, 8])
        b_src = sb("b_src", [P, J], I32)
        b_dst = sb("b_dst", [P, J], I32)
        b_typ = sb("b_typ", [P, J], I32)
        r_dst = sb("r_dst", [P, J * P], I32)
        r_typ = sb("r_typ", [P, J * P], I32)
        key_c = sb("key_c", [P, J])
        key_r = sb("key_r", [P, J, P])
        same = sb("same", [P, J, P])
        comb = sb("comb", [P, J, D])
        earlier = comb
        dup = sb("dup", [P, J])
        spare = sb("spare", [P, J])
        to_row = sb("to_row", [P, J], I32)
        got = sb("got", [P, J, D])
        rowbuf = sb("rowbuf", [P, 4, D])
        aT = sb("aT", [P, CH])
        rT = sb("rT", [P, CH])
        zT = sb("zT", [P, CH])
        tT = sb("tT", [P, CH])
        nT = sb("nT", [P, CH])
        B = [ctx.enter_context(nc.psum_tensor(f"bank{i}", [P, 512], F32)) for i in range(8)]

        names = """loaded consts_loaded edges_in hist_free hist_ready hist_done cnt_psum cnt_sb cnt_written
            cnt_read act_step dve_step ln_var ln_std rows_ready tr_psum tr_copied tab_written acc_zeroed zeros_set
            edges_loaded keys_ready gathered comb_psum combined scattered row_loaded st_psum st_copied
            mean_ready sg_psum sg_sq sg_ssq sg_max sg_std sg_done bn_var bn_std h_ready
            a_psum a_copied gates_psum sig_done pre_n n_ready h_updated rdy_out o_psum o_sig o_done
            stored passed""".split()
        s = {n: sem(n) for n in names}

        def transpose_rows(pe, tr, src, dst_cols):
            for g in range(TG):
                n = min(4, Q - 4 * g)
                if tr.step >= 2 or not isinstance(tr.base, int):
                    pe.wait_ge(s["tr_copied"], tr.value(1))
                for m in range(n):
                    ins = pe.transpose(B[5 + g % 2][:, m * P:(m + 1) * P], src(4 * g + m), ident)
                ins.then_inc(s["tr_psum"], 1)
                tr.up()
            pe.wait_ge(s["tr_copied"], tr.value())

        def copy_rows(act, tr, dst):
            for g in range(TG):
                n = min(4, Q - 4 * g)
                act.wait_ge(s["tr_psum"], tr.up())
                act.activation(dst[:, 4 * g * P:(4 * g + n) * P], B[5 + g % 2][:, 0:n * P], ACT.Copy)\
                   .then_inc(s["tr_copied"], 1)

        block = ctx.enter_context(nc.Block())

        @block.sync
        def _(sp):
            again = sp.value_load(redo, min_val=0, max_val=3 * P)
            with sp.If(again != 0):
                sp.dma_start(dstc[:, :], dst_c).then_inc(s["edges_in"], 16)
                sp.dma_start(typc[:, :], typ_c).then_inc(s["edges_in"], 16)
                sp.dma_start(con[:, :], consts).then_inc(s["consts_loaded"], 16)
                sp.wait_ge(s["zeros_set"], 2)
                full = N // P
                sp.dma_start(xr[:, 0:full, :], x[0:full * P, :].rearrange("(q p) f -> p q f", p=P))\
                  .then_inc(s["loaded"], 16)
                sp.dma_start(xr[0:N - full * P, full, :], x[full * P:N, :]).then_inc(s["loaded"], 16)
                sp.dma_start(w[:, :, :], weights).then_inc(s["loaded"], 16)
                sp.dma_start(bias[:, :], biases).then_inc(s["loaded"], 16)
                sp.dma_start(bet[:, :], b_et).then_inc(s["loaded"], 16)
                sp.wait_ge(s["cnt_sb"], 2)
                sp.dma_start(cnt_dram[0:K].rearrange("k q p -> (k q) p"), cntT[0:K * Q, :]).then_inc(s["cnt_written"], 16)
                sp.dma_start(cnt_dram[K], totT[:, :]).then_inc(s["cnt_written"], 16)
                sp.wait_ge(s["cnt_written"], 32)
                sp.dma_start(cnt4[:, :], cnt_dram[0:K].rearrange("k q p -> k (q p)")).then_inc(s["cnt_read"], 16)
                sp.dma_start(cntb[:, :], cnt_dram[K].rearrange("q p -> (q p)").partition_broadcast(P))\
                  .then_inc(s["cnt_read"], 16)

                def aggregate(turn):
                    sp.wait_ge(s["rows_ready"], 1 + turn)
                    sp.dma_start(table.rearrange("(q p) f -> p q f", p=P), rows[:, :, :]).then_inc(s["tab_written"], 16)
                    flat = acc.rearrange("(p a) f -> p (a f)", p=P)
                    part = ACC * D // P // 32
                    for i in range(32):
                        sp.dma_start(flat[:, i * part:(i + 1) * part], zeros[:, :]).then_inc(s["acc_zeroed"], 16)
                    with sp.Fori(0, NB) as b:
                        sp.wait_ge(s["scattered"], (turn * NB + b) * (16 * J))
                        sp.dma_start(b_src[:, :], src_c[:, bass.ds(b * J, J)]).then_inc(s["edges_loaded"], 16)
                        sp.dma_start(b_dst[:, :], dst_c[:, bass.ds(b * J, J)]).then_inc(s["edges_loaded"], 16)
                        sp.dma_start(b_typ[:, :], typ_c[:, bass.ds(b * J, J)]).then_inc(s["edges_loaded"], 16)
                        sp.dma_start(r_dst[:, :], dst_r[bass.ds(b * J * P, J * P)].partition_broadcast(P))\
                          .then_inc(s["edges_loaded"], 16)
                        sp.dma_start(r_typ[:, :], typ_r[bass.ds(b * J * P, J * P)].partition_broadcast(P))\
                          .then_inc(s["edges_loaded"], 16)
                    sp.wait_ge(s["scattered"], (turn + 1) * (NB * 16 * J))
                    sp.sem_inc(s["passed"], 1)
                    with sp.Fori(0, K * Q // 4) as i:
                        sp.wait_ge(s["st_psum"], turn * (K * Q // 4) + i)
                        sp.dma_start(rowbuf[:, :, :], acc[bass.ds(i * 4 * P, 4 * P), :].rearrange("(j p) f -> p j f", p=P))\
                          .then_inc(s["row_loaded"], 16)

                aggregate(0)
                aggregate(1)
                with sp.Fori(0, STEPS) as t:
                    aggregate(t + 2)
                sp.wait_ge(s["rdy_out"], 1)
                sp.dma_start(out[0:full * P, :].rearrange("(q p) f -> p q f", p=P), rows[:, 0:full, :])\
                  .then_inc(s["stored"], 16)
                sp.dma_start(out[full * P:N, :], rows[0:N - full * P, full, :]).then_inc(s["stored"], 16)
                sp.wait_ge(s["stored"], 32)


        @block.gpsimd
        def _(pool):
            again = pool.value_load(redo, min_val=0, max_val=3 * P)
            with pool.If(again != 0):
                pool.memset(zeros[:, :], 0.0).then_inc(s["zeros_set"], 1)
                pool.memset(xr[:, :, :], 0.0).then_inc(s["zeros_set"], 1)

                def aggregate(turn):
                    pool.wait_ge(s["tab_written"], (turn + 1) * 16)
                    pool.wait_ge(s["acc_zeroed"], (turn + 1) * 512)
                    pool.sem_inc(s["passed"], 1)
                    with pool.Fori(0, NB) as b:
                        blk = turn * NB + b
                        pool.wait_ge(s["edges_loaded"], (blk + 1) * 80)
                        pool.sem_inc(s["passed"], 1)
                        for j in range(J):
                            pool.indirect_dma_start(got[:, j, :], None, table,
                                                    bass.IndirectOffsetOnAxis(ap=b_src[:, j:j + 1], axis=0))\
                                .then_inc(s["gathered"], 16)
                        pool.wait_ge(s["keys_ready"], blk + 1)
                        for j in range(J):
                            pool.wait_ge(s["combined"], blk * (J // 4) + (j // 4 + 1))
                            pool.sem_inc(s["passed"], 1)
                            pool.indirect_dma_start(acc, bass.IndirectOffsetOnAxis(ap=to_row[:, j:j + 1], axis=0),
                                                    comb[:, j, :], None, compute_op=ALU.add,
                                                    bounds_check=ACC - 1).then_inc(s["scattered"], 16)
                            pool.wait_ge(s["scattered"], blk * (16 * J) + 16 * (j + 1))

                aggregate(0)
                aggregate(1)
                with pool.Fori(0, STEPS) as t:
                    aggregate(t + 2)


        @block.tensor
        def _(pe):
            again = pe.value_load(redo, min_val=0, max_val=3 * P)
            with pe.If(again != 0):
                def hist(b, buf, first, last):
                    pe.wait_ge(s["hist_ready"], b + 1)
                    for j in range(J):
                        ins = pe.matmul(B[7][:, 0:K * Q], oh_low[:, buf, j, :], oh_high[:, buf, j, :],
                                        start=first and j == 0, stop=last and j == J - 1)
                    ins.then_inc(s["hist_done"], 1)

                hist(0, 0, True, False)
                with pe.Fori(0, (NB - 3) // 2) as b2:
                    hist(b2 * 2 + 1, 1, False, False)
                    hist(b2 * 2 + 2, 0, False, False)
                hist(NB - 2, 1, False, False)
                hist(NB - 1, 0, False, True)
                pe.wait_ge(s["consts_loaded"], 16)
                pe.wait_ge(s["cnt_psum"], 1)
                pe.transpose(B[6][0:K * Q, 0:P], cnt[:, 0:K, :].rearrange("p k q -> p (k q)"), ident)
                pe.transpose(B[6][0:Q, P:2 * P], cnt[:, K, :], ident).then_inc(s["cnt_psum"], 1)

                tr = Count()

                def sums_to_columns(turn):
                    with pe.Fori(0, K * Q // 4) as i:
                        g = turn * (K * Q // 4) + i
                        pe.wait_ge(s["row_loaded"], (g + 1) * 16)
                        pe.wait_ge(s["st_copied"], g)
                        for m in range(4):
                            ins = pe.transpose(B[5][:, m * P:(m + 1) * P], rowbuf[:, m, :], ident)
                        ins.then_inc(s["st_psum"], 1)

                def aggregate(turn):
                    with pe.Fori(0, NB) as b:
                        blk = turn * NB + b
                        pe.wait_ge(s["gathered"], (blk + 1) * (16 * J))
                        pe.wait_ge(s["keys_ready"], blk + 1)
                        for j in range(J):
                            ins = pe.matmul(B[6 + j // 4][:, (j % 4) * P:(j % 4 + 1) * P], same[:, j, :], got[:, j, :],
                                            start=True, stop=True)
                            if j % 4 == 3:
                                ins.then_inc(s["comb_psum"], 1)
                    sums_to_columns(turn)
                    pe.wait_ge(s["st_copied"], (turn + 1) * (K * Q // 4))
                    pe.sem_inc(s["passed"], 1)

                def sage(turn, w_agg, w_own):
                    pe.wait_ge(s["mean_ready"], turn + 1)
                    with pe.Fori(0, NC) as c:
                        g = turn * NC + c
                        pe.wait_ge(s["sg_done"], g)
                        pe.matmul(B[0][:, 0:CH], w[:, w_agg, :], ST[:, 0, bass.ds(c * CH, CH)], start=True, stop=False)
                        pe.matmul(B[0][:, 0:CH], w[:, w_own, :], hT[:, bass.ds(c * CH, CH)], start=False, stop=True)\
                          .then_inc(s["sg_psum"], 1)
                        pe.wait_ge(s["sg_sq"], g + 1)
                        pe.matmul(B[1][:, 0:CH], ones[:, :], tT[:, :], start=True, stop=True).then_inc(s["sg_ssq"], 1)

                pe.wait_ge(s["cnt_sb"], 2)
                pe.wait_ge(s["rows_ready"], 1)
                transpose_rows(pe, tr, lambda q: rows[:, q, :], None)
                aggregate(0)
                sage(0, WL1, WR1)
                pe.wait_ge(s["sg_done"], NC)
                transpose_rows(pe, tr, lambda q: hT[:, q * P:(q + 1) * P], None)
                aggregate(1)
                sage(1, WL2, WR2)
                pe.wait_ge(s["sg_done"], 2 * NC)
                transpose_rows(pe, tr, lambda q: hT[:, q * P:(q + 1) * P], None)
                pe.wait_ge(s["rows_ready"], 3)
                transpose_rows(pe, tr, lambda q: rows[:, q, :], None)
                with pe.Fori(0, STEPS) as t:
                    aggregate(t + 2)
                    with pe.Fori(0, NC) as c:
                        g = t * NC + c
                        at = bass.ds(c * CH, CH)
                        pe.wait_ge(s["a_copied"], g)
                        for k in range(K):
                            pe.matmul(B[0][:, 0:CH], w[:, WET + k, :], ST[:, k, at], start=k == 0, stop=False)
                        pe.matmul(B[0][:, 0:CH], bet[:, :], cnt4[:, at], start=False, stop=True)\
                          .then_inc(s["a_psum"], 1)
                        pe.wait_ge(s["a_copied"], g + 1)
                        pe.wait_ge(s["pre_n"], g)
                        for m in range(2):
                            pe.matmul(B[1 + m][:, 0:CH], w[:, WIH + m, :], aT[:, :], start=True, stop=False)
                            pe.matmul(B[1 + m][:, 0:CH], w[:, WHH + m, :], hT[:, at], start=False, stop=True)
                        pe.matmul(B[3][:, 0:CH], w[:, WHH + 2, :], hT[:, at], start=True, stop=True)
                        pe.matmul(B[4][:, 0:CH], w[:, WIH + 2, :], aT[:, :], start=True, stop=True)\
                          .then_inc(s["gates_psum"], 1)
                    pe.wait_ge(s["h_updated"], (t + 1) * NC)
                    transpose_rows(pe, tr.loop(t, TG), lambda q: hT[:, q * P:(q + 1) * P], None)
                tr.up(STEPS * TG)
                with pe.Fori(0, NC) as c:
                    at = bass.ds(c * CH, CH)
                    pe.wait_ge(s["o_done"], c)
                    pe.matmul(B[0][:, 0:CH], w[:, IW, :], hT[:, at], start=True, stop=False)
                    pe.matmul(B[0][:, 0:CH], w[:, IW + 1, :], featT[:, at], start=False, stop=True)
                    pe.matmul(B[1][:, 0:CH], w[:, JW, :], hT[:, at], start=True, stop=True).then_inc(s["o_psum"], 1)
                pe.wait_ge(s["o_done"], NC)
                transpose_rows(pe, tr, lambda q: hT[:, q * P:(q + 1) * P], None)


        @block.scalar
        def _(act):
            again = act.value_load(redo, min_val=0, max_val=3 * P)
            with act.If(again != 0):
                tr = Count()
                act.wait_ge(s["cnt_psum"], 2)
                act.activation(cntT[0:K * Q, :], B[6][0:K * Q, 0:P], ACT.Copy).then_inc(s["cnt_sb"], 1)
                act.activation(totT[:, :], B[6][0:Q, P:2 * P], ACT.Copy).then_inc(s["cnt_sb"], 1)
                act.wait_ge(s["ln_var"], 1)
                act.activation(rstd[:, :], mv[:, :, 1], ACT.Sqrt).then_inc(s["ln_std"], 1)
                copy_rows(act, tr, hT)

                def sums_to_columns(turn):
                    with act.Fori(0, K * Q // 4) as i:
                        act.wait_ge(s["st_psum"], turn * (K * Q // 4) + i + 1)
                        act.activation(ST[:, :, :].rearrange("p k n -> p (k n)")[:, bass.ds(i * 512, 512)],
                                       B[5][:, :], ACT.Copy).then_inc(s["st_copied"], 1)

                def sage(turn, b):
                    with act.Fori(0, NC) as c:
                        g = turn * NC + c
                        act.wait_ge(s["sg_psum"], g + 1)
                        act.activation(tT[:, :], B[0][:, 0:CH], ACT.Square, bias=bias[:, b:b + 1])\
                           .then_inc(s["sg_sq"], 1)
                        act.activation(aT[:, :], B[0][:, 0:CH], ACT.Identity, bias=bias[:, b:b + 1])\
                           .then_inc(s["act_step"], 1)
                        act.wait_ge(s["sg_max"], g + 1)
                        act.activation(nT[:, :], rT[:, :], ACT.Sqrt).then_inc(s["sg_std"], 1)

                sums_to_columns(0)
                sage(0, BL1)
                act.wait_ge(s["bn_var"], 1)
                act.activation(cols[:, 2:3], cols[:, 1:2], ACT.Sqrt).then_inc(s["bn_std"], 1)
                copy_rows(act, tr, rows[:, :, :].rearrange("p q f -> p (q f)"))
                act.wait_ge(s["tr_copied"], 2 * TG)
                act.activation(cols[:, 6:7], cols[:, 2:3], ACT.Copy).then_inc(s["rows_ready"], 1)
                sums_to_columns(1)
                sage(1, BL2)
                copy_rows(act, tr, rows[:, :, :].rearrange("p q f -> p (q f)"))
                act.wait_ge(s["ln_var"], 2)
                act.activation(rstd[:, :], mv[:, :, 1], ACT.Sqrt).then_inc(s["ln_std"], 1)
                copy_rows(act, tr, hT)
                with act.Fori(0, STEPS) as t:
                    sums_to_columns(t + 2)
                    with act.Fori(0, NC) as c:
                        g = t * NC + c
                        act.wait_ge(s["a_psum"], g + 1)
                        act.wait_ge(s["gates_psum"], g)
                        act.activation(aT[:, :], B[0][:, 0:CH], ACT.Copy).then_inc(s["a_copied"], 1)
                        act.wait_ge(s["gates_psum"], g + 1)
                        act.wait_ge(s["h_updated"], g)
                        act.activation(rT[:, :], B[1][:, 0:CH], ACT.Sigmoid, bias=brz[:, 0:1]).then_inc(s["sig_done"], 1)
                        act.activation(zT[:, :], B[2][:, 0:CH], ACT.Sigmoid, bias=brz[:, 1:2]).then_inc(s["sig_done"], 1)
                        act.wait_ge(s["pre_n"], g + 1)
                        act.activation(nT[:, :], tT[:, :], ACT.Tanh, bias=bias[:, BIH + 2:BIH + 3]).then_inc(s["n_ready"], 1)
                    inner = tr.loop(t, TG)
                    copy_rows(act, inner, rows[:, :, :].rearrange("p q f -> p (q f)"))
                    act.wait_ge(s["tr_copied"], inner.value())
                    act.activation(cols[:, 6:7], cols[:, 2:3], ACT.Copy).then_inc(s["rows_ready"], 1)
                tr.up(STEPS * TG)
                with act.Fori(0, NC) as c:
                    act.wait_ge(s["o_psum"], c + 1)
                    act.activation(rT[:, :], B[0][:, 0:CH], ACT.Sigmoid, bias=bias[:, IB:IB + 1]).then_inc(s["o_sig"], 1)
                copy_rows(act, tr, rows[:, :, :].rearrange("p q f -> p (q f)"))


        @block.vector
        def _(dve):
            again = dve.value_load(redo, min_val=0, max_val=3 * P)
            with dve.If(again != 0):
                chain = Count()

                def link(ins, ch):
                    ins.then_inc(s["dve_step"], 1)
                    dve.wait_ge(s["dve_step"], ch.up())

                dve.memset(ones[:, :], 1.0)
                dve.wait_ge(s["edges_in"], 32)
                dve.wait_ge(s["consts_loaded"], 16)
                link(dve.tensor_single_scalar(lowi, dstc[:, :], P - 1, ALU.bitwise_and), chain)
                link(dve.tensor_copy(lowf[:, :], lowi), chain)
                link(dve.tensor_tensor(highf[:, :], dstc[:, :], lowf[:, :], ALU.subtract), chain)
                link(dve.tensor_single_scalar(highf[:, :], highf[:, :], 1.0 / P, ALU.mult), chain)
                link(dve.scalar_tensor_tensor(out=highf[:, :], in0=typc[:, :], scalar=float(Q), in1=highf[:, :],
                                              op0=ALU.mult, op1=ALU.add), chain)

                def hist(b, buf, free):
                    if free:
                        dve.wait_ge(s["hist_done"], b - 1)
                    at = bass.ds(b * J, J) if not isinstance(b, int) else slice(b * J, b * J + J)
                    dve.tensor_tensor(oh_low[:, buf], iota.unsqueeze(1).to_broadcast([P, J, P]),
                                      lowf[:, at].unsqueeze(2).to_broadcast([P, J, P]), ALU.is_equal)
                    dve.tensor_tensor(oh_high[:, buf], iota[:, 0:K * Q].unsqueeze(1).to_broadcast([P, J, K * Q]),
                                      highf[:, at].unsqueeze(2).to_broadcast([P, J, K * Q]), ALU.is_equal)\
                       .then_inc(s["hist_ready"], 1)

                hist(0, 0, False)
                with dve.Fori(0, (NB - 3) // 2) as b2:
                    hist(b2 * 2 + 1, 1, True)
                    hist(b2 * 2 + 2, 0, True)
                hist(NB - 2, 1, True)
                hist(NB - 1, 0, True)
                dve.wait_ge(s["hist_done"], NB)
                link(dve.tensor_copy(cnt[:, 0:K, :], B[7][:, 0:K * Q].rearrange("p (k q) -> p k q", k=K)), chain)
                link(dve.tensor_reduce(cnt[:, K, :], cnt[:, 0:K, :].rearrange("p k q -> p q k"), AX.X, ALU.add), chain)
                dve.tensor_copy(cols[:, 7:8], lane).then_inc(s["cnt_psum"], 1)

                def norm_rows(n):
                    for q in range(Q):
                        dve.bn_stats(st6[:, q, :], xr[:, q, :]).then_inc(s["dve_step"], 1)
                    chain.up(Q)
                    dve.wait_ge(s["dve_step"], chain.value())
                    for q in range(Q):
                        dve.bn_aggr(mv[:, q, :], st6[:, q, :]).then_inc(s["dve_step"], 1)
                    chain.up(Q)
                    dve.wait_ge(s["dve_step"], chain.value())
                    dve.tensor_single_scalar(mv[:, :, 1], mv[:, :, 1], 1e-5, ALU.add).then_inc(s["ln_var"], 1)
                    dve.wait_ge(s["ln_std"], n)
                    link(dve.reciprocal(rstd[:, :], rstd[:, :]), chain)
                    for q in range(Q):
                        dve.tensor_scalar(rows[:, q, :], xr[:, q, :], mv[:, q, 0:1], rstd[:, q:q + 1],
                                          ALU.subtract, ALU.mult).then_inc(s["dve_step"], 1)
                    chain.up(Q)
                    dve.wait_ge(s["dve_step"], chain.value())
                    dve.tensor_single_scalar(rows[:, :, :], rows[:, :, :], 0.0, ALU.max).then_inc(s["rows_ready"], 1)

                dve.wait_ge(s["loaded"], 80)
                norm_rows(1)
                link(dve.tensor_tensor(brz[:, :], bias[:, BIH:BIH + 2], bias[:, BHH:BHH + 2], ALU.add), chain)
                dve.wait_ge(s["cnt_read"], 32)
                link(dve.tensor_single_scalar(invb[:, :], cntb[:, :], 1.0, ALU.max), chain)
                link(dve.reciprocal(invb[:, :], invb[:, :]), chain)

                def aggregate(turn, ch, n0):
                    with dve.Fori(0, NB) as b:
                        blk = turn * NB + b
                        c = Count(ch + b * 7)
                        dve.wait_ge(s["edges_loaded"], (blk + 1) * 80)
                        link(dve.scalar_tensor_tensor(out=key_c[:, :], in0=b_typ[:, :], scalar=float(NP), in1=b_dst[:, :],
                                                      op0=ALU.mult, op1=ALU.add), c)
                        link(dve.scalar_tensor_tensor(out=key_r[:, :, :].rearrange("p j e -> p (j e)"), in0=r_typ[:, :],
                                                      scalar=float(NP), in1=r_dst[:, :], op0=ALU.mult, op1=ALU.add), c)
                        link(dve.tensor_tensor(same[:, :, :], key_r[:, :, :],
                                               key_c[:, :].unsqueeze(2).to_broadcast([P, J, P]), ALU.is_equal), c)
                        link(dve.tensor_tensor(earlier[:, :, :], same[:, :, :],
                                               below.unsqueeze(1).to_broadcast([P, J, P]), ALU.mult), c)
                        link(dve.tensor_reduce(dup[:, :], earlier[:, :, :], AX.X, ALU.max), c)
                        link(dve.tensor_scalar(spare[:, :], key_c[:, :], -1.0, cols[:, 7:8], ALU.mult, ALU.add), c)
                        link(dve.scalar_tensor_tensor(out=spare[:, :], in0=spare[:, :], scalar=float(K * NP),
                                                      in1=dup[:, :], op0=ALU.add, op1=ALU.mult), c)
                        dve.tensor_tensor(to_row[:, :], spare[:, :], key_c[:, :], ALU.add).then_inc(s["keys_ready"], 1)
                        for m in range(J // 4):
                            dve.wait_ge(s["comb_psum"], blk * (J // 4) + (m + 1))
                            dve.tensor_copy(comb[:, 4 * m:4 * m + 4, :].rearrange("p j f -> p (j f)"), B[6 + m][:, :])\
                               .then_inc(s["combined"], 1)

                def sage(turn, relu):
                    dve.wait_ge(s["st_copied"], (turn + 1) * (K * Q // 4))
                    for k in range(1, K):
                        link(dve.tensor_tensor(ST[:, 0, :], ST[:, 0, :], ST[:, k, :], ALU.add), chain)
                    if turn == 0:
                        dve.wait_ge(s["tr_copied"], TG)
                        dve.tensor_tensor(ST[:, 0, :], ST[:, 0, :], invb[:, :], ALU.mult).then_inc(s["mean_ready"], 1)
                    else:
                        link(dve.tensor_tensor(ST[:, 0, :], ST[:, 0, :], invb[:, :], ALU.mult), chain)
                        link(dve.tensor_tensor(ST[:, 1, :], cntb[:, :], invb[:, :], ALU.mult), chain)
                        link(dve.tensor_scalar(ST[:, 1, :], ST[:, 1, :], cols[:, 4:5], None, ALU.mult), chain)
                        link(dve.scalar_tensor_tensor(out=ST[:, 0, :], in0=ST[:, 0, :], scalar=cols[:, 3:4],
                                                      in1=ST[:, 1, :], op0=ALU.mult, op1=ALU.add), chain)
                        dve.tensor_scalar(hT[:, :], hT[:, :], cols[:, 3:4], cols[:, 4:5], ALU.mult, ALU.add)\
                           .then_inc(s["mean_ready"], 1)
                    n0 = chain.value()
                    with dve.Fori(0, NC) as c:
                        g = turn * NC + c
                        ch = Count(n0 + c * 1)
                        at = bass.ds(c * CH, CH)
                        dve.wait_ge(s["sg_ssq"], g + 1)
                        dve.tensor_single_scalar(rT[:, :], B[1][:, 0:CH], 1e-24, ALU.max).then_inc(s["sg_max"], 1)
                        dve.wait_ge(s["sg_std"], g + 1)
                        dve.wait_ge(s["act_step"], g + 1)
                        link(dve.reciprocal(zT[:, :], nT[:, :]), ch)
                        if relu:
                            dve.scalar_tensor_tensor(out=hT[:, at], in0=aT[:, :], scalar=0.0, in1=zT[:, :],
                                                     op0=ALU.max, op1=ALU.mult).then_inc(s["sg_done"], 1)
                        else:
                            dve.tensor_tensor(hT[:, at], aT[:, :], zT[:, :], ALU.mult).then_inc(s["sg_done"], 1)
                    chain.up(NC)

                aggregate(0, chain.value(), 0)
                chain.up(7 * NB)
                sage(0, True)
                dve.wait_ge(s["sg_done"], NC)
                for q in range(Q):
                    dve.bn_stats(st6[:, q, :], hT[:, q * (N // Q):(q + 1) * (N // Q)]).then_inc(s["dve_step"], 1)
                chain.up(Q)
                dve.wait_ge(s["dve_step"], chain.value())
                link(dve.bn_aggr(cols[:, 0:2], st6[:, :, :].rearrange("p q s -> p (q s)")), chain)
                dve.tensor_single_scalar(cols[:, 1:2], cols[:, 1:2], 1e-5, ALU.add).then_inc(s["bn_var"], 1)
                dve.wait_ge(s["bn_std"], 1)
                link(dve.reciprocal(cols[:, 3:4], cols[:, 2:3]), chain)
                link(dve.tensor_tensor(cols[:, 3:4], cols[:, 3:4], bias[:, GAM:GAM + 1], ALU.mult), chain)
                link(dve.tensor_tensor(cols[:, 5:6], cols[:, 0:1], cols[:, 3:4], ALU.mult), chain)
                link(dve.tensor_tensor(cols[:, 4:5], bias[:, BET:BET + 1], cols[:, 5:6], ALU.subtract), chain)
                aggregate(1, chain.value(), 0)
                chain.up(7 * NB)
                sage(1, False)
                dve.wait_ge(s["tr_copied"], 3 * TG)
                link(dve.tensor_tensor(xr[:, :, :], xr[:, :, :], rows[:, :, :], ALU.add), chain)
                norm_rows(2)
                dve.wait_ge(s["tr_copied"], 4 * TG)
                link(dve.tensor_copy(featT[:, :], hT[:, :]), chain)
                n0 = chain.value()
                per = 7 * NB + 3 * NC
                with dve.Fori(0, STEPS) as t:
                    aggregate(t + 2, t * per + n0, 0)
                    with dve.Fori(0, NC) as c:
                        g = t * NC + c
                        at = bass.ds(c * CH, CH)
                        ch = Count(t * per + c * 3 + (n0 + 7 * NB))
                        dve.wait_ge(s["sig_done"], g * 2 + 2)
                        link(dve.scalar_tensor_tensor(out=tT[:, :], in0=B[3][:, 0:CH], scalar=bias[:, BHH + 2:BHH + 3],
                                                      in1=rT[:, :], op0=ALU.add, op1=ALU.mult), ch)
                        dve.tensor_tensor(tT[:, :], tT[:, :], B[4][:, 0:CH], ALU.add).then_inc(s["pre_n"], 1)
                        dve.wait_ge(s["n_ready"], g + 1)
                        link(dve.tensor_tensor(rT[:, :], hT[:, at], nT[:, :], ALU.subtract), ch)
                        link(dve.tensor_tensor(rT[:, :], rT[:, :], zT[:, :], ALU.mult), ch)
                        dve.tensor_tensor(hT[:, at], rT[:, :], nT[:, :], ALU.add).then_inc(s["h_updated"], 1)
                chain.up(STEPS * per)
                n0 = chain.value()
                with dve.Fori(0, NC) as c:
                    at = bass.ds(c * CH, CH)
                    dve.wait_ge(s["o_sig"], c + 1)
                    dve.scalar_tensor_tensor(out=hT[:, at], in0=B[1][:, 0:CH], scalar=bias[:, JB:JB + 1],
                                             in1=rT[:, :], op0=ALU.add, op1=ALU.mult).then_inc(s["o_done"], 1)
                dve.wait_ge(s["tr_copied"], (5 + STEPS) * TG)
                dve.tensor_tensor(rows[:, :, :], rows[:, :, :], xr[:, :, :], ALU.add).then_inc(s["rdy_out"], 1)




def gnn_kernel(nc, a, out):
    with nc.sbuf_tensor("redo", [1, 1], I32) as redo:
        dense_kernel(nc, a["x"], a["dst_c"], a["typ_c"], a["src_r"], a["dst_r"], a["typ_r"], a["weights"],
                     a["biases"], a["b_et"], a["consts"], out, redo[:, :])
        general_kernel(nc, a["x"], a["src_c"], a["dst_c"], a["typ_c"], a["dst_r"], a["typ_r"], a["weights"],
                       a["biases"], a["b_et"], a["consts"][:, 0:3 * P + 1], out, redo[:, :])


def kernel(x, src, dst, edge_type_4, L0_gnn_W_l1, L0_gnn_b_l1, L0_gnn_W_r1, L0_gnn_gamma, L0_gnn_beta,
           L0_gnn_W_l2, L0_gnn_b_l2, L0_gnn_W_r2, L1_gnn_W_et, L1_gnn_b_et, L1_gnn_W_ih, L1_gnn_b_ih,
           L1_gnn_W_hh, L1_gnn_b_hh, L1_gnn_i_w, L1_gnn_i_b, L1_gnn_j_w, L1_gnn_j_b):
    import concourse.bacc as bacc
    from concourse.bass_utils import run_bass_kernel_spmd

    def tiles_of(wt):
        wt = np.asarray(wt)
        return [wt[o:o + P, i:i + P].T for i in range(0, wt.shape[1], P) for o in range(0, wt.shape[0], P)]

    def edges(a, pad):
        a = np.asarray(a)
        full = np.full(P * KW + P, pad, a.dtype)
        full[:E] = a
        return full

    we = np.asarray(L1_gnn_W_et)
    weights = np.stack([t for wt in (L0_gnn_W_l1, L0_gnn_W_r1, L0_gnn_W_l2, L0_gnn_W_r2, we[0], we[1], we[2], we[3],
                                     L1_gnn_W_ih, L1_gnn_W_hh, L1_gnn_i_w, L1_gnn_j_w) for t in tiles_of(wt)], axis=1)
    biases = np.concatenate([np.asarray(b).reshape(-1, P) for b in (
        L0_gnn_b_l1, L0_gnn_b_l2, L0_gnn_gamma, L0_gnn_beta, L1_gnn_b_ih, L1_gnn_b_hh, L1_gnn_i_b, L1_gnn_j_b)]).T
    src_p, dst_p, typ_p = edges(src, 0), edges(dst, NP), edges(edge_type_4, K - 1)
    lane = np.arange(P, dtype=np.float32)
    consts = np.concatenate([np.tril(np.ones((P, P), np.float32), -1), np.eye(P, dtype=np.float32),
                             np.tile(lane, (P, 1)), lane[:, None],
                             np.triu(np.ones((P, P), np.float32), 1)], axis=1)
    arrays = {
        "x": np.asarray(x),
        "src_c": src_p[:EP].reshape(-1, P).T, "dst_c": dst_p[:EP].reshape(-1, P).T, "typ_c": typ_p[:EP].reshape(-1, P).T,
        "src_r": src_p, "dst_r": dst_p, "typ_r": typ_p,
        "weights": weights, "biases": biases, "b_et": np.asarray(L1_gnn_b_et), "consts": consts,
    }
    arrays = {k: np.ascontiguousarray(v) for k, v in arrays.items()}
    nc = bacc.Bacc("TRN2", target_bir_lowering=False, num_devices=1)
    args = {k: nc.dram_tensor(k, v.shape, mybir.dt.from_np(v.dtype), kind="ExternalInput").ap()
            for k, v in arrays.items()}
    out = nc.dram_tensor("out", (N, D), F32, kind="ExternalOutput").ap()
    gnn_kernel(nc, args, out)
    return run_bass_kernel_spmd(nc, [arrays], core_ids=[0]).results[0]["out"]
```

```python
from contextlib import ExitStack

import numpy as np

import concourse.bass as bass
from concourse import mybir

P = 128
N = 3125
D = 128
E = 103125
K = 4
STEPS = 3
Q = -(-N // P)
NP = Q * P
J = 8
TILES = -(-E // P)
NB = -(-TILES // J)
EP = NB * J * P
ACC = K * NP + P
CH = 400
NC = NP // CH
ROUNDS = 2 + STEPS
TG = -(-Q // 4)

F32 = mybir.dt.float32
F16 = mybir.dt.float16
I32 = mybir.dt.int32
ALU = mybir.AluOpType
ACT = mybir.ActivationFunctionType
AX = mybir.AxisListType

WL1, WR1, WL2, WR2, WET, WIH, WHH, IW, JW = 0, 1, 2, 3, 4, 8, 11, 14, 16
NW = 17
BL1, BL2, GAM, BET, BIH, BHH, IB, JB = 0, 1, 2, 3, 4, 7, 10, 11
NBIAS = 12


class Count:

    def __init__(self, base=0):
        self.base, self.step = base, 0

    def up(self, by=1):
        self.step += by
        return self.base + self.step

    def value(self, less=0):
        return self.base + (self.step - less)

    def loop(self, i, per):
        inner = Count(i * per + self.value())
        inner.per = per
        return inner


SLOTS = 64
KW = 816
RUN = 32
NR = 3232
Q2 = Q + 1
M = Q2 // 2
HQ = K * Q + Q
GR = 16
LOW = 64
HIGH = NP // LOW
STEP = 4
SAMPLES = KW // STEP
HB = -(-SAMPLES // GR)
KEY_BITS = 14
COPIES = RUN // STEP
FIRST = 2
SC = 512
SIZES = [min(SC, NP - c) for c in range(0, NP, SC)]
NS = len(SIZES)
FEW = N - (Q - 1) * P
FEW_IT = -(-FEW // (2 * GR))
A_SCALE = 0.125
H_SCALE = 4096.0
UNSCALE = 1.0 / (A_SCALE * H_SCALE)
F8 = mybir.dt.float8e4
U8 = mybir.dt.uint8


def dense_kernel(nc, x, src_r, dst_r, typ_r, weights, biases, b_et, consts, out, redo):
    with ExitStack() as ctx:
        def sb(name, shape, dt=F32):
            return ctx.enter_context(nc.sbuf_tensor("d_" + name, shape, dt))

        adj = nc.dram_tensor("adj", [Q2, P, K * Q * P], U8, kind="Internal").ap()
        keys_dram = nc.dram_tensor("keys_dram", [P * KW], I32, kind="Internal").ap()
        shifted = nc.dram_tensor("shifted", [COPIES * NR, RUN], I32, kind="Internal").ap()
        inv_dram = nc.dram_tensor("d_inv_dram", [2, Q, P], F32, kind="Internal").ap()

        xr = sb("xr", [P, Q, D])
        rows = sb("rows", [P, Q, D])
        flat_x, flat_rows = (a[:, :, :].rearrange("p q f -> p (q f)") for a in (xr, rows))
        w = sb("w", [P, NW, P])
        bias = sb("bias", [P, NBIAS])
        brz = sb("brz", [P, 2])
        con = sb("con", [P, 3 * P + 1])
        ident, iota, lane, above = con[:, 0:P], con[:, P:2 * P], con[:, 2 * P:2 * P + 1], con[:, 2 * P + 1:3 * P + 1]
        ones = sb("ones", [P, P])
        types_of = sb("types_of", [P, K, 2 * K], F16)
        st6 = sb("st6", [P, Q, 6])
        mv = sb("mv", [P, Q, 2])
        rstd = sb("rstd", [P, Q])
        shift = sb("shift", [P, Q])
        cols = sb("cols", [P, 8])
        flags = sb("flags", [P, 4])
        wide = sb("wide", [P, Q * Q2 * P], U8)
        au = wide[:, :].bitcast(F8).rearrange("p (m q n) -> p m q n", m=M, q=Q)
        widef = wide[:, :].bitcast(F32)
        blk = sb("blk", [P, 2, 2, K * Q * P], U8)
        blk8 = blk[:, :, :, :].bitcast(F8)
        blkf = blk[:, :, :, :].rearrange("p a b n -> p (a b n)").bitcast(F32)
        hT = blkf[:, 0:NP]
        half_words = lambda base, i: base[:, i * (NP // 2):(i + 1) * (NP // 2)].bitcast(F16).rearrange("p (q f) -> p q f", q=Q)
        hi1, lo1 = (half_words(blkf[:, NP:2 * NP], i) for i in range(2))
        invb = blkf[:, 2 * NP:3 * NP]
        anyb = blkf[:, 3 * NP:4 * NP]
        hi0, lo0 = (half_words(flat_x, i) for i in range(2))
        hi, lo = (half_words(flat_rows, i) for i in range(2))
        hi2, lo2 = (half_words(invb, i) for i in range(2))
        ublk = sb("ublk", [P, 2, Q, 2, P], U8)
        ublk8 = ublk[:, :, :, :, :].bitcast(F8)
        ublk16 = ublk[:, :, :, :, :].rearrange("p a q h d -> p (a q h d)").bitcast(F16)
        bet = ublk[:, :, :, :, :].rearrange("p a q h d -> p (a q h d)").bitcast(F32)[0:2 * K, 2560:2560 + 2 * P]
        HS = HB * GR
        low16 = widef[:, 0:HS // 2].bitcast(F16)
        high16 = widef[:, HS // 2:HS].bitcast(F16)
        lowi, highi = (widef[:, HS + i * SAMPLES:HS + (i + 1) * SAMPLES].bitcast(I32) for i in range(2))
        srcr, typr, dstr, dstn, keyr, order = (widef[:, (4 + i) * KW:(5 + i) * KW].bitcast(I32) for i in range(6))
        SL = Q2 * SLOTS
        at0 = 10 * KW
        sloti, loi, hii = (widef[:, at0 + i * SL:at0 + (i + 1) * SL].bitcast(I32) for i in range(3))
        valid, lof, hif = (widef[:, at0 + i * SL:at0 + (i + 1) * SL] for i in range(3, 6))
        at1 = at0 + 6 * SL + Q2
        node_id = widef[:, at1 - Q2:at1]
        tot, base, shift_q = (widef[:, at1 + i * Q2:at1 + i * Q2 + Q] for i in range(3))
        ptri, shf = (widef[:, at1 + i * Q2:at1 + i * Q2 + Q].bitcast(I32) for i in range(3, 5))
        nils = widef[:, at1 + 5 * Q2:at1 + 5 * Q2 + Q]
        at2 = at1 + 6 * Q2
        found = widef[0:LOW, at2:at2 + HIGH]
        inv_any = [widef[:, at2 + 1280 + i * Q2:at2 + 1280 + i * Q2 + Q] for i in range(2)]
        inv_anyT = widef[0:Q, at2 + LOW:at2 + LOW + 2 * P]
        upper = widef[0:LOW, at2 + 320:at2 + 320 + P]
        ktmp = widef[:, at2 + 448:at2 + 448 + M * P // 2].bitcast(F16)
        row_at = sb("row_at", [P, 2, Q], I32)
        klow = sb("klow", [P, M * P], F16)
        khigh = sb("khigh", [P, M * P], F16)
        ksrc = sb("ksrc", [P, M * P], F16)
        iota2 = sb("iota2", [P, P, 2], F16)
        low_n, high_n = 2 * GR * P // 2, 2 * GR * HQ // 2
        work = sb("work", [P, low_n + high_n])
        oh_low = work[:, 0:low_n].bitcast(F16).rearrange("p (b i c e) -> p b i c e", b=2, c=P, e=2)
        oh_high = work[:, low_n:low_n + high_n].bitcast(F16).rearrange("p (b i c e) -> p b i c e", b=2, c=HQ, e=2)
        featT = widef[:, 0:NP]
        countb = widef[:, NP:2 * NP]
        AW = K * Q * P
        atile = [wide[:, 8 * NP + i * AW:8 * NP + (i + 1) * AW] for i in range(4)]
        cnt8 = widef[0:2 * K, 2 * NP:2 * NP + M * P]
        sums = [widef[:, 6 * NP + i * 512:6 * NP + (i + 1) * 512] for i in range(3)]
        meanT = [work[:, i * SC:(i + 1) * SC] for i in range(2)]
        aT, rT, zT, tT, nT = (work[:, i * SC:(i + 1) * SC] for i in range(2, 7))
        fresh = meanT[0][:, 0:P]
        turned_rows = ksrc[:, :].bitcast(F32)[:, 0:SC]
        gate_of = (sums[0], sums[1])
        OW = Q * P // 4
        orw = klow[:, 0:2 * OW].bitcast(I32)
        B = ctx.enter_context(nc.psum_tensor("banks", [P, 8, 512], F32))

        names = """edges_in consts_in order_in loaded zeros_set keys_made order_made keys_out shifted_out row_ready slots_in0
            slots_in halves_made halves_ready hist_ready hist_done found_sb tot_psum totals_sb before_psum kt_psum
            kt_copied keys_high keys_low keys_done inv_made inv_psum inv_sb inv_written inv_read atl_made bet_zero
            bet_in c4_psum c4_copied oh_ready ps_ready typed_out all_out tile_stored0 tile_stored1 dve_step pool_step
            ln_var ln_std shift_made rows_ready hi_ready lo_ready x_clear x_back sm_psum mean_ready sg_psum sg_sq
            sg_out sg_ssq sg_max sg_std sg_done bn_var bn_std tin_psum tin_copied tout_psum tout_hi tout_done h_scaled
            ln_rows ln_hi ln_lo tln_psum tln_copied s_psum s_out a_loaded0 a_loaded1 a_loaded2 a_loaded3 th_psum th_hi
            th_lo h_split cb_psum cb_copied a_psum a_copied gates_psum sig_done pre_n n_ready h_updated o_psum o_sig
            o_done o_turned out_ready stored flag_psum flag_ready au_stored0 au_stored1 feat_ready passed""".split()
        s = {n: ctx.enter_context(nc.semaphore("d_" + n)) for n in names}
        CG = -(-M // 4)
        bias_steps = [(g, h, 4 * g, min(4 * g + 4, M)) for g in range(CG) for h in range(2) if 8 * g + h < Q]
        half_flat = lambda a: a.rearrange("p q f -> p (q f)")

        def turns(m0, m1):
            return [(part, a, min(a + 4, m1)) for part in (1, 0) for a in range(m0, m1, 4)]

        key_turns = turns(0, FIRST) + turns(FIRST, M)
        G1, G2 = len(turns(0, FIRST)), len(key_turns)
        block = ctx.enter_context(nc.Block())

        @block.sync
        def _(sp):
            rowed = lambda a, o: a[o:o + P * KW].rearrange("(p i) -> p i", p=P)
            sp.dma_start(dstr, rowed(dst_r, 0)).then_inc(s["edges_in"], 16)
            sp.dma_start(con[:, :], consts[:, P:4 * P + 1]).then_inc(s["consts_in"], 16)
            sp.dma_start(srcr, rowed(src_r, 0)).then_inc(s["order_in"], 16)
            sp.dma_start(typr, rowed(typ_r, 0)).then_inc(s["order_in"], 16)
            sp.dma_start(dstn, rowed(dst_r, 1)).then_inc(s["order_in"], 16)
            sp.wait_ge(s["keys_made"], 1)
            sp.dma_start(rowed(keys_dram, 0), keyr).then_inc(s["keys_out"], 16)
            sp.wait_ge(s["zeros_set"], 1)
            full = N // P
            sp.dma_start(xr[:, 0:full, :], x[0:full * P, :].rearrange("(q p) f -> p q f", p=P))\
              .then_inc(s["loaded"], 16)
            sp.dma_start(xr[0:N - full * P, full, :], x[full * P:N, :]).then_inc(s["loaded"], 16)
            sp.dma_start(w[:, :, :], weights).then_inc(s["loaded"], 16)
            sp.dma_start(bias[:, :], biases).then_inc(s["loaded"], 16)
            sp.wait_ge(s["keys_out"], 16)
            copies = shifted.rearrange("(c n) r -> c (n r)", c=COPIES)
            with sp.Fori(0, COPIES) as c:
                sp.dma_start(copies[bass.ds(c, 1), :].rearrange("o (a b) -> (o a) b", a=P),
                             keys_dram[bass.ds(c * STEP, NR * RUN)].rearrange("(a b) -> a b", a=P))\
                  .then_inc(s["shifted_out"], 16)

            def store(m, half, short=0):
                sp.wait_ge(s["typed_out"], (m + 1) * 32 - short * 8 if short else (m + 1) * 32)
                sp.dma_start(adj[bass.ds(m * 2, 2)].rearrange("b p n -> p b n"), blk[:, half])\
                  .then_inc(s["tile_stored%d" % half], 16)
                sp.wait_ge(s["all_out"], (m + 1) * 24 - short * 6 if short else (m + 1) * 24)
                sp.dma_start(wide[:, bass.ds(m * (Q * 2 * P), Q * 2 * P)],
                             ublk[:, half].rearrange("p q h d -> p (q h d)")).then_inc(s["au_stored%d" % half], 16)

            store(0, 0)
            store(1, 1)
            sp.wait_ge(s["inv_sb"], 1)
            sp.dma_start(inv_dram.rearrange("i q p -> q i p"), inv_anyT.rearrange("q (i p) -> q i p", i=2))\
              .then_inc(s["inv_written"], 16)
            sp.wait_ge(s["inv_written"], 16)
            sp.wait_ge(s["keys_done"], 1)
            with sp.Fori(1, M // 2) as m2:
                store(m2 * 2, 0)
                store(m2 * 2 + 1, 1)
            sp.wait_ge(s["tile_stored1"], M // 2 * 16)
            for i, dst in enumerate((invb, anyb)):
                sp.dma_start(dst, inv_dram[i].rearrange("q p -> (q p)").partition_broadcast(P)).then_inc(s["inv_read"], 16)
            store(M - 1, 0, 4 - FEW_IT)
            sp.wait_ge(s["tile_stored0"], (M + 1) // 2 * 16)
            sp.wait_ge(s["bet_zero"], 1)
            for h in range(2):
                sp.dma_start(bet[h * K:(h + 1) * K, h * P:(h + 1) * P], b_et).then_inc(s["bet_in"], 16)
            sp.wait_ge(s["x_clear"], 1)
            sp.dma_start(xr[:, 0:full, :], x[0:full * P, :].rearrange("(q p) f -> p q f", p=P))\
              .then_inc(s["x_back"], 16)
            sp.dma_start(xr[0:N - full * P, full, :], x[full * P:N, :]).then_inc(s["x_back"], 16)

            def load(c, i):
                sp.dma_start(atile[i], adj[bass.ds(c, 1)].rearrange("o p n -> (o p) n"))\
                  .then_inc(s["a_loaded%d" % i], 16)

            sp.wait_ge(s["sm_psum"], 2 * NS)
            sp.wait_ge(s["flag_ready"], 1)
            load(Q - 1, 3)
            sp.wait_ge(s["cb_psum"], NS)
            with sp.Fori(0, STEPS) as t:
                with sp.Fori(0, Q // 3) as c3:
                    for i in range(3):
                        sp.wait_ge(s["s_psum"], t * Q + (c3 * 3 + max(i - 1, 0)) + 1)
                        sp.sem_inc(s["passed"], 1)
                        load(c3 * 3 + i, i)
            for c in range(NS):
                sp.wait_ge(s["out_ready"], c + 1)
                if SIZES[c] == SC:
                    sp.dma_start(out[c * SC:(c + 1) * SC, :].rearrange("(q p) f -> p q f", p=P), xr[:, 4 * c:4 * c + 4, :])\
                      .then_inc(s["stored"], 16)
                else:
                    sp.dma_start(out[c * SC:N, :], xr[0:N - c * SC, 4 * c, :]).then_inc(s["stored"], 16)
            sp.wait_ge(s["stored"], 16 * NS)

        @block.gpsimd
        def _(pool):
            pool.memset(xr[:, :, :], 0.0).then_inc(s["zeros_set"], 1)
            pool.wait_ge(s["order_in"], 48)
            pool.tensor_tensor(order, dstr, dstn, ALU.subtract).then_inc(s["order_made"], 1)
            pool.wait_ge(s["row_ready"], 1)
            pool.wait_ge(s["shifted_out"], 16 * COPIES)
            for q in range(Q):
                for half in range(2):
                    pool.indirect_dma_start(sloti[:, q * SLOTS + half * RUN:q * SLOTS + (half + 1) * RUN], None,
                                            shifted, bass.IndirectOffsetOnAxis(ap=row_at[:, half, q:q + 1], axis=0))\
                        .then_inc(s["slots_in0" if q < 2 * FIRST else "slots_in"], 16)
            pool.wait_ge(s["shift_made"], 1)
            for q in range(Q):
                ins = pool.tensor_scalar(rows[:, q, :], xr[:, q, :], rstd[:, q:q + 1], shift[:, q:q + 1], ALU.mult, ALU.add)
            ins.then_inc(s["pool_step"], 1)
            pool.wait_ge(s["pool_step"], 1)
            pool.tensor_single_scalar(flat_rows, flat_rows, 0.0, ALU.max).then_inc(s["rows_ready"], 1)
            pool.wait_ge(s["rows_ready"], 1)
            pool.tensor_copy(half_flat(hi0), flat_rows).then_inc(s["hi_ready"], 1)
            pool.wait_ge(s["hi_ready"], 1)
            pool.tensor_tensor(half_flat(lo0), flat_rows, half_flat(hi0), ALU.subtract).then_inc(s["lo_ready"], 1)
            pool.wait_ge(s["sm_psum"], NS)
            pool.memset(xr[:, N // P, :], 0.0).then_inc(s["x_clear"], 1)

        @block.tensor
        def _(pe):
            pe.sem_inc(s["a_psum"], 1)
            pe.sem_inc(s["gates_psum"], 1)
            pe.sem_inc(s["s_psum"], 1)
            def hist(b, buf, first, last):
                pe.wait_ge(s["hist_ready"], b + 1)
                for j in range(GR):
                    ins = pe.matmul(B[0:LOW, 7, 0:HIGH], oh_low[:, buf, j // 2, 0:LOW, j % 2],
                                    oh_high[:, buf, j // 2, 0:HIGH, j % 2],
                                    start=first and j == 0, stop=last and j == GR - 1)
                ins.then_inc(s["hist_done"], 1)

            hist(0, 0, True, False)
            hist(1, 1, False, False)
            with pe.Fori(1, HB // 2) as b2:
                hist(b2 * 2, 0, False, False)
                hist(b2 * 2 + 1, 1, False, False)
            hist(HB - 1, 0, False, True)
            pe.wait_ge(s["found_sb"], 1)
            by_tile = found.rearrange("l (q two) -> l two q", two=2)
            pe.matmul(B[:, 0, 0:Q], ident[0:LOW, :], by_tile[:, 0, :], start=True, stop=False)
            pe.matmul(B[:, 0, 0:Q], upper, by_tile[:, 1, :], start=False, stop=True).then_inc(s["tot_psum"], 1)
            pe.wait_ge(s["totals_sb"], 1)
            pe.matmul(B[:, 2, 0:Q], above, tot, start=True, stop=True)
            pe.matmul(B[:, 2, 64:64 + Q], ones[:, :], tot, start=True, stop=True).then_inc(s["before_psum"], 1)

            def turn_keys(g0, g1):
                for g in range(g0, g1):
                    part, a, b = key_turns[g]
                    if g >= g0 + 2:
                        pe.wait_ge(s["kt_copied"], g - 1)
                    if not part:
                        pe.wait_ge(s["keys_low"], 2 if g0 else 1)
                    for m in range(a, b):
                        ins = pe.transpose(B[:, g % 2, (m - a) * P:(m - a + 1) * P],
                                           (hif if part else lof)[:, m * P:(m + 1) * P], ident)
                    ins.then_inc(s["kt_psum"], 1)
                pe.wait_ge(s["kt_copied"], g1)

            pe.wait_ge(s["keys_high"], 1)
            turn_keys(0, G1)

            def build(it, first):
                for buf in range(2):
                    pe.wait_ge(s["oh_ready"], it * 2 + (buf + 1))
                    for g4 in range(4):
                        g = buf * 4 + g4
                        if not first or buf:
                            pe.wait_ge(s["typed_out"], it * 8 + (g - 3))
                            if g4 < 3:
                                pe.wait_ge(s["all_out"], it * 6 + (buf * 3 + g4 - 2))
                        for h in range(2):
                            for i in range(4):
                                r = g4 * 4 + i
                                ins = pe.matmul(B[:, 2 * g4 + h, i * HQ:(i + 1) * HQ],
                                                oh_low[64 * h:64 * h + 64, buf, r // 2, :, r % 2],
                                                oh_high[64 * h:64 * h + 64, buf, r // 2, :, r % 2],
                                                start=True, stop=True)
                        ins.then_inc(s["ps_ready"], 1)

            build(0, True)
            with pe.Fori(1, 4 * FIRST) as it:
                build(it, False)
            pe.wait_ge(s["typed_out"], 32 * FIRST)
            pe.wait_ge(s["all_out"], 24 * FIRST)
            pe.wait_ge(s["keys_high"], 2)
            turn_keys(G1, G2)
            pe.wait_ge(s["inv_made"], 1)
            for i in range(2):
                ins = pe.transpose(B[0:Q, 1, i * P:(i + 1) * P], inv_any[i], ident)
            ins.then_inc(s["inv_psum"], 1)
            pe.wait_ge(s["inv_sb"], 1)
            with pe.Fori(4 * FIRST, (M - 1) * 4 + FEW_IT) as it:
                build(it, False)
            pe.wait_ge(s["typed_out"], (M - 1) * 32 + FEW_IT * 8)
            pe.wait_ge(s["all_out"], (M - 1) * 24 + FEW_IT * 6)

            def turn_four(bank, g, src, sem):
                c = g % NS
                for i in range(SIZES[c] // P):
                    ins = pe.transpose(B[:, bank, i * P:(i + 1) * P], src(4 * c + i, i), ident)
                ins.then_inc(s[sem], 1)

            def turn_in(c):
                if c:
                    pe.wait_ge(s["tin_copied"], c)
                turn_four(5, c, lambda q, i: rows[:, q, :], "tin_psum")

            def turn_out(g):
                pe.wait_ge(s["sg_done"], g + 1)
                if g:
                    pe.wait_ge(s["tout_done"], g)
                turn_four(6, g, lambda q, i: hT[:, q * P:(q + 1) * P], "tout_psum")

            def turn_norm(c):
                pe.wait_ge(s["ln_rows"], c + 1)
                if c:
                    pe.wait_ge(s["tln_copied"], c)
                turn_four(4, c, lambda q, i: turned_rows[:, i * P:(i + 1) * P], "tln_psum")

            def project(g):
                n, c = divmod(g, NS)
                at, z = slice(c * SC, c * SC + SIZES[c]), SIZES[c]
                if g:
                    pe.wait_ge(s["sg_done"], g)
                pe.wait_ge(s["mean_ready"], g + 1)
                if n == 0:
                    pe.wait_ge(s["tin_copied"], c + 1)
                else:
                    pe.wait_ge(s["h_scaled"], 1)
                pe.matmul(B[:, 2, 0:z], w[:, (WL1, WL2)[n], :], meanT[g % 2][:, 0:z], start=True, stop=False)
                pe.matmul(B[:, 2, 0:z], w[:, (WR1, WR2)[n], :], hT[:, at], start=False, stop=True)\
                  .then_inc(s["sg_psum"], 1)

            def squares(g):
                z = SIZES[g % NS]
                pe.wait_ge(s["sg_sq"], g + 1)
                pe.matmul(B[:, 3, 0:z], ones[:, :], tT[:, 0:z], start=True, stop=True).then_inc(s["sg_ssq"], 1)

            at_least = [klow[:, :]] + [ublk16[:, k * M * P:(k + 1) * M * P] for k in range(K - 1)]

            def type_counts(g):
                m0, m1 = 4 * g, min(4 * g + 4, M)
                if g >= 2:
                    pe.wait_ge(s["c4_copied"], g - 1)
                for k in range(K):
                    ins = pe.matmul(B[0:2 * K, 5 + 2 * (g % 2), 0:(m1 - m0) * P], types_of[:, k, :],
                                    at_least[k][:, m0 * P:m1 * P], start=k == 0, stop=k == K - 1)
                ins.then_inc(s["c4_psum"], 1)

            def steps_beside(g):
                if g == 0:
                    return {}
                if g == NS - 1:
                    return {2: [(project, g - 1)], 3: [(turn_in, g)], 20: [(squares, g - 1)]}
                if g == NS:
                    return {3: [(turn_out, g - 3)], 12: [(project, g - 1)], 15: [(squares, g - 1)],
                            17: [(turn_out, g - 2)], 21: [(turn_out, g - 1)]}
                if g == NS + 1:
                    return {14: [(project, g - 1)], 20: [(squares, g - 1)]}
                if g == 1:
                    return {1: [(turn_in, 0)], 16: [(project, 0)], 22: [(squares, 0)]}
                if g == 2:
                    return {1: [(turn_in, 1)], 12: [(project, 1)], 17: [(squares, 1)], 22: [(turn_out, 0)]}
                steps = {7: [(project, g - 1)], 13: [(squares, g - 1)]}
                if g < NS:
                    steps[1] = [(turn_in, g - 1)]
                    steps[17] = [(turn_out, g - 2)]
                    if g == NS - 2:
                        steps[22] = [(turn_in, g)]
                else:
                    steps[2] = [(turn_out, g - 2)]
                    steps[20] = [(turn_norm, g - 2 - NS)]
                if g == 2 * NS - 1:
                    steps[4] = [(type_counts, 0), (type_counts, 1)]
                return steps

            pe.wait_ge(s["rows_ready"], 1)
            pe.wait_ge(s["hi_ready"], 1)
            pe.wait_ge(s["lo_ready"], 1)
            for g in range(2 * NS):
                n, c = divmod(g, NS)
                z = SIZES[c]
                pairs = slice(2 * c, min(2 * c + 2, M))
                beside = steps_beside(g)
                if n == 0:
                    pe.wait_ge(s["au_stored0"], (c + 1) * 16)
                    if 2 * c + 1 < M:
                        pe.wait_ge(s["au_stored1"], (c + 1) * 16)
                if g >= 2:
                    pe.wait_ge(s["mean_ready"], g - 1)
                for q in range(Q):
                    for step, of in beside.get(q, ()):
                        step(of)
                    if g == NS and q in (0, 16, 20, 24):
                        pe.wait_ge(s["tout_done"], q // 4 + 1 if q else NS - 3)
                    edges = au[:, pairs, q, :] if z == SC else au[:, 2 * c, q, 0:FEW]
                    high, low = ((hi0, lo0), (hi1, lo1))[n]
                    got = B[:, g % 2, 0:z if z == SC else FEW]
                    pe.matmul(got, high[:, q, :], edges, start=q == 0, stop=False)
                    ins = pe.matmul(got, low[:, q, :], edges, start=False, stop=q == Q - 1)
                ins.then_inc(s["sm_psum"], 1)
                if g == 2 * NS - 2:
                    pe.wait_ge(s["atl_made"], 1)
                    pe.wait_ge(s["flag_ready"], 1)
                if g == NS + 1:
                    pe.wait_ge(s["flag_psum"], 1)
                    pe.matmul(B[0:1, 7, 0:1], flags[:, 3:4], ones[:, 0:1], start=True, stop=True).then_inc(s["flag_psum"], 1)
            def type_biases(c):
                g, h, m0, m1 = bias_steps[c]
                if c >= 2:
                    pe.wait_ge(s["cb_copied"], c - 1)
                pe.matmul(B[:, c % 2, 0:(m1 - m0) * P], bet[:, h * P:(h + 1) * P], cnt8[:, m0 * P:m1 * P],
                          start=True, stop=True).then_inc(s["cb_psum"], 1)

            pe.wait_ge(s["bet_in"], 32)
            last = 2 * NS - 1
            project(last)
            turn_out(last - 1)
            squares(last)
            type_counts(2)
            turn_norm(NS - 2)
            type_counts(3)
            turn_out(last)
            pe.wait_ge(s["c4_copied"], CG)
            for c in range(3):
                type_biases(c)
            turn_norm(NS - 1)
            for c in range(3, NS):
                type_biases(c)

            def products(q, i, bank, few):
                a4 = atile[i].bitcast(F8).rearrange("p (k q d) -> p k q d", k=K, q=Q)
                for part in (hi, lo):
                    ins = pe.matmul(B[:, bank, 0:K * few], part[:, q, :], a4[:, :, q, 0:few],
                                    start=q == 0 and part is hi, stop=q == last_q and part is lo)
                return ins

            def turn(g, src):
                pe.wait_ge(s["h_updated"], g + 1)
                pe.wait_ge(s["th_lo"], g + 1)
                pe.transpose(B[:, 5, 0:P], src, ident).then_inc(s["th_psum"], 1)

            def messages(g, bank, few=P):
                pe.wait_ge(s["s_out"], g + 2)
                pe.wait_ge(s["a_copied"], g + 1)
                for k in range(K):
                    ins = pe.matmul(B[:, 7, 0:few], w[:, WET + k, :], sums[bank][:, k * few:(k + 1) * few],
                                    start=k == 0, stop=k == K - 1)
                ins.then_inc(s["a_psum"], 1)

            def gates(g, at, few=P):
                pe.wait_ge(s["a_copied"], g + 2)
                pe.wait_ge(s["pre_n"], g + 1)
                for m in range(2):
                    pe.matmul(B[:, 3, m * P:m * P + few], w[:, WIH + m, :], aT[:, 0:few], start=True, stop=False)
                    pe.matmul(B[:, 3, m * P:m * P + few], w[:, WHH + m, :], hT[:, at], start=False, stop=True)
                pe.matmul(B[:, 4, 0:few], w[:, WHH + 2, :], hT[:, at], start=True, stop=True)
                pe.matmul(B[:, 4, P:P + few], w[:, WIH + 2, :], aT[:, 0:few], start=True, stop=True)\
                  .then_inc(s["gates_psum"], 1)

            LAST = slice((Q - 1) * P, N)
            BEFORE = slice((Q - 2) * P, (Q - 1) * P)

            def three(t, c3, first):
                for i in range(3):
                    c = c3 * 3 + (i + 1)
                    g = t * Q + c
                    short = first and i == 0
                    pe.wait_ge(s["a_loaded%d" % i], (t * (Q // 3) + (c3 + 1)) * 16)
                    pe.wait_ge(s["s_out"], g)
                    pe.sem_inc(s["passed"], 1)
                    for q in range(Q):
                        ins = products(q, i, i, P)
                        if q == Q // 2:
                            if short:
                                messages(g - 1, 1, FEW)
                            else:
                                turn(g - 1, fresh)
                                messages(g - 1, i - 1 if i else 2)
                    ins.then_inc(s["s_psum"], 1)
                    if short:
                        gates(g - 1, LAST, FEW)
                    else:
                        gates(g - 1, bass.ds((c - 2) * P, P))

            last_q = Q - 1
            pe.wait_ge(s["ln_lo"], NS - 1)
            pe.wait_ge(s["tln_copied"], NS - 1)
            pe.wait_ge(s["cb_copied"], NS)
            pe.wait_ge(s["a_loaded3"], 16)
            with pe.Fori(0, STEPS) as t:
                pe.wait_ge(s["h_split"], t + 1)
                pe.wait_ge(s["s_out"], t * Q + 1)
                pe.sem_inc(s["passed"], 1)
                last_q = Q - 2
                for q in [*range(Q - 2), Q - 1, Q - 2]:
                    if q == Q - 1:
                        pe.wait_ge(s["ln_lo"], NS)
                        pe.wait_ge(s["tln_copied"], NS)
                        pe.sem_inc(s["passed"], 1)
                    if q == Q - 2:
                        pe.wait_ge(s["th_lo"], t * Q + 2)
                        pe.sem_inc(s["passed"], 1)
                    ins = products(q, 3, 1, FEW)
                    if q == Q // 2:
                        turn(t * Q, hT[:, BEFORE])
                ins.then_inc(s["s_psum"], 1)
                last_q = Q - 1
                three(t, 0, True)
                with pe.Fori(1, Q // 3) as c3:
                    three(t, c3, False)
                turn(t * Q + (Q - 1), fresh)
                messages(t * Q + (Q - 1), 2)
                gates(t * Q + (Q - 1), BEFORE)
            def turn_output(c):
                pe.wait_ge(s["o_done"], c + 2)
                if c >= 2:
                    pe.wait_ge(s["out_ready"], c - 1)
                for i in range(SIZES[c] // P):
                    ins = pe.transpose(B[:, 5 + c % 2, i * P:(i + 1) * P], hT[:, c * SC + i * P:c * SC + (i + 1) * P], ident)
                ins.then_inc(s["o_turned"], 1)

            for c in range(NS):
                at, z, bank = slice(c * SC, c * SC + SIZES[c]), SIZES[c], 2 * (c % 2)
                if c == 0:
                    pe.wait_ge(s["s_out"], STEPS * Q + 1)
                if c == 1:
                    pe.wait_ge(s["h_updated"], STEPS * Q + 1)
                if c >= 2:
                    pe.wait_ge(s["o_done"], c)
                pe.matmul(B[:, bank, 0:z], w[:, IW, :], hT[:, at], start=True, stop=False)
                pe.matmul(B[:, bank, 0:z], w[:, IW + 1, :], featT[:, at], start=False, stop=True)
                pe.matmul(B[:, bank + 1, 0:z], w[:, JW, :], hT[:, at], start=True, stop=True).then_inc(s["o_psum"], 1)
                if c:
                    turn_output(c - 1)
            turn_output(NS - 1)

        @block.scalar
        def _(act):
            act.sem_inc(s["s_out"], 1)
            act.wait_ge(s["halves_made"], 1)
            act.activation(low16[:, 0:SAMPLES], lowi, ACT.Copy).then_inc(s["halves_ready"], 1)
            act.activation(high16[:, 0:SAMPLES], highi, ACT.Copy).then_inc(s["halves_ready"], 1)

            def keys_from(g0, g1):
                for g in range(g0, g1):
                    part, a, b = key_turns[g]
                    act.wait_ge(s["kt_psum"], g + 1)
                    act.activation((khigh if part else klow)[:, a * P:b * P], B[:, g % 2, 0:(b - a) * P],
                                   ACT.Copy, bias=-1.0).then_inc(s["kt_copied"], 1)

            keys_from(0, G1)
            act.wait_ge(s["ln_var"], 1)
            act.activation(rstd[:, :], mv[:, :, 1], ACT.Sqrt).then_inc(s["ln_std"], 1)
            def pair(m, half, old, its=4):
                if old is not None:
                    act.wait_ge(s["tile_stored%d" % half], old * 16)
                    act.wait_ge(s["au_stored%d" % half], old * 16)
                tiles = blk8[:, half].rearrange("p h (x d) -> p h x d", d=P)
                for g in range(8 * its):
                    act.wait_ge(s["ps_ready"], m * 32 + (g + 1))
                    act.sem_inc(s["passed"], 1)
                    made = B[:, 2 * (g % 4):2 * (g % 4) + 2, 0:4 * HQ].rearrange("p h (i x) -> p h x i", i=4)
                    if g % 4 == 3:
                        act.activation(ublk8[:, half].rearrange("p q h d -> p h q d")[:, :, :, 4 * g:4 * g + 4],
                                       made[:, :, K * Q:HQ, :], ACT.Copy, scale=A_SCALE, saturate=False)
                    act.activation(tiles[:, :, :, 4 * g:4 * g + 4], made[:, :, 0:K * Q, :], ACT.Copy, scale=A_SCALE,
                                   saturate=False).then_inc(s["typed_out"], 1)

            pair(0, 0, None)
            pair(1, 1, None)
            keys_from(G1, G2)
            act.wait_ge(s["inv_psum"], 1)
            act.activation(inv_anyT, B[0:Q, 1, 0:2 * P], ACT.Copy).then_inc(s["inv_sb"], 1)
            with act.Fori(1, M // 2) as m2:
                pair(m2 * 2, 0, m2)
                pair(m2 * 2 + 1, 1, m2)
            pair(M - 1, 0, M // 2, FEW_IT)

            four = lambda g: (4 * (g % NS), 4 * (g % NS) + SIZES[g % NS] // P)

            def turn_in(c):
                act.wait_ge(s["tin_psum"], c + 1)
                act.activation(hT[:, c * SC:c * SC + SIZES[c]], B[:, 5, 0:SIZES[c]], ACT.Copy, scale=1.0 / H_SCALE)\
                   .then_inc(s["tin_copied"], 1)

            def turn_out(g):
                a, b = four(g)
                act.wait_ge(s["tout_psum"], g + 1)
                act.activation(half_flat(hi1[:, a:b, :]), B[:, 6, 0:(b - a) * P], ACT.Copy, scale=H_SCALE)\
                   .then_inc(s["tout_hi"], 1)

            def norm(c):
                a, b = four(c)
                act.wait_ge(s["ln_var"], c + 2)
                act.activation(rstd[:, a:b], mv[:, a:b, 1], ACT.Sqrt).then_inc(s["ln_std"], 1)
                act.wait_ge(s["shift_made"], c + 2)
                if c:
                    act.wait_ge(s["tln_psum"], c)
                    act.wait_ge(s["ln_lo"], c)
                for q in range(a, b):
                    ins = act.activation(turned_rows[:, (q - a) * P:(q - a + 1) * P], xr[:, q, :], ACT.Relu,
                                         bias=shift[:, q:q + 1], scale=rstd[:, q:q + 1])
                ins.then_inc(s["ln_rows"], 1)
                act.wait_ge(s["ln_rows"], c + 1)
                act.activation(half_flat(hi[:, a:b, :]), turned_rows[:, 0:(b - a) * P], ACT.Copy, scale=H_SCALE)\
                   .then_inc(s["ln_hi"], 1)

            def turn_norm(c):
                act.wait_ge(s["tln_psum"], c + 1)
                act.activation(hT[:, c * SC:c * SC + SIZES[c]], B[:, 4, 0:SIZES[c]], ACT.Copy).then_inc(s["tln_copied"], 1)

            def square(g):
                z, b = SIZES[g % NS], (BL1, BL2)[g // NS]
                act.wait_ge(s["sg_psum"], g + 1)
                act.activation(tT[:, 0:z], B[:, 2, 0:z], ACT.Square, bias=bias[:, b:b + 1]).then_inc(s["sg_sq"], 1)
                act.activation(aT[:, 0:z], B[:, 2, 0:z], ACT.Identity, bias=bias[:, b:b + 1]).then_inc(s["sg_out"], 1)

            def root(g):
                z = SIZES[g % NS]
                act.wait_ge(s["sg_max"], g + 1)
                act.activation(nT[:, 0:z], rT[:, 0:z], ACT.Sqrt).then_inc(s["sg_std"], 1)

            def type_counts(g):
                m0, m1 = 4 * g, min(4 * g + 4, M)
                act.wait_ge(s["c4_psum"], g + 1)
                act.activation(cnt8[:, m0 * P:m1 * P], B[0:2 * K, 5 + 2 * (g % 2), 0:(m1 - m0) * P], ACT.Copy)\
                   .then_inc(s["c4_copied"], 1)

            def type_biases(c):
                g, h, m0, m1 = bias_steps[c]
                act.wait_ge(s["cb_psum"], c + 1)
                got = B[:, c % 2, 0:(m1 - m0) * P].rearrange("p (m r) -> p m r", r=P)
                if (2 * m1 - 1) * P <= NP - P:
                    dst = countb[:, 2 * m0 * P:2 * m1 * P].rearrange("p (m h r) -> p m h r", h=2, r=P)[:, :, h, :]
                    act.activation(dst, got, ACT.Copy).then_inc(s["cb_copied"], 1)
                else:
                    act.activation(countb[:, (Q - 1) * P:Q * P], B[:, c % 2, 0:P], ACT.Copy).then_inc(s["cb_copied"], 1)

            act.wait_ge(s["tile_stored0"], (M + 1) // 2 * 16)
            for g in range(1, NS - 1):
                turn_in(g - 1)
                square(g - 1)
                root(g - 1)
                if g >= 2:
                    turn_out(g - 2)
            turn_in(NS - 2)
            square(NS - 2)
            turn_in(NS - 1)
            root(NS - 2)
            turn_out(NS - 3)
            square(NS - 1)
            root(NS - 1)
            turn_out(NS - 2)
            turn_out(NS - 1)
            act.wait_ge(s["bn_var"], 1)
            act.activation(cols[:, 2:3], cols[:, 1:2], ACT.Sqrt).then_inc(s["bn_std"], 1)
            for g in range(NS + 1, 2 * NS):
                if g >= NS + 2:
                    norm(g - 2 - NS)
                square(g - 1)
                root(g - 1)
                if g >= NS + 2:
                    turn_norm(g - 2 - NS)
            act.wait_ge(s["sm_psum"], 2 * NS)
            type_counts(0)
            type_counts(1)
            square(2 * NS - 1)
            norm(NS - 2)
            root(2 * NS - 1)
            type_counts(2)
            turn_norm(NS - 2)
            type_counts(3)
            norm(NS - 1)
            for c in range(3):
                type_biases(c)
            turn_norm(NS - 1)
            for c in range(3, NS):
                type_biases(c)

            def turned(g, dst):
                act.wait_ge(s["th_psum"], g + 1)
                act.activation(dst, B[:, 5, 0:P], ACT.Copy, scale=H_SCALE).then_inc(s["th_hi"], 1)

            def read_sums(g, bank, few=P):
                act.wait_ge(s["s_psum"], g + 2)
                act.wait_ge(s["a_psum"], g + (0 if bank is not None else 1))
                b = 1 if bank is None else bank
                act.activation(sums[b][:, 0:K * few], B[:, b, 0:K * few], ACT.Copy, scale=UNSCALE).then_inc(s["s_out"], 1)

            def update(g, few=P):
                act.wait_ge(s["gates_psum"], g + 2)
                act.wait_ge(s["h_updated"], g + 1)
                act.activation(rT[:, 0:few], B[:, 3, 0:few], ACT.Sigmoid, bias=brz[:, 0:1]).then_inc(s["sig_done"], 1)
                act.activation(zT[:, 0:few], B[:, 3, P:P + few], ACT.Sigmoid, bias=brz[:, 1:2]).then_inc(s["sig_done"], 1)
                act.wait_ge(s["pre_n"], g + 2)
                act.activation(nT[:, 0:few], tT[:, 0:few], ACT.Tanh, bias=bias[:, BIH + 2:BIH + 3])\
                   .then_inc(s["n_ready"], 1)

            with act.Fori(0, STEPS) as t:
                turned(t * Q, hi[:, Q - 2, :])
                read_sums(t * Q, None, FEW)
                update(t * Q, FEW)
                with act.Fori(0, Q // 3) as c3:
                    for i in range(3):
                        c = c3 * 3 + (i + 1)
                        read_sums(t * Q + c, i)
                        turned(t * Q + c, hi2[:, bass.ds(c - 1, 1), :].rearrange("p o f -> p (o f)"))
                        update(t * Q + c)
            for c in range(NS):
                z = SIZES[c]
                act.wait_ge(s["o_psum"], c + 1)
                if c >= 2:
                    act.wait_ge(s["o_done"], c)
                act.activation(gate_of[c % 2][:, 0:z], B[:, 2 * (c % 2), 0:z], ACT.Sigmoid, bias=bias[:, IB:IB + 1])\
                   .then_inc(s["o_sig"], 1)

        @block.vector
        def _(dve):
            chain = Count()
            dve.sem_inc(s["h_split"], 1)
            dve.sem_inc(s["h_updated"], 1)
            dve.sem_inc(s["th_lo"], 1)
            dve.sem_inc(s["a_copied"], 1)
            dve.sem_inc(s["pre_n"], 1)
            dve.sem_inc(s["o_done"], 1)

            def link(ins, ch=chain):
                ins.then_inc(s["dve_step"], 1)
                dve.wait_ge(s["dve_step"], ch.up())

            dve.memset(ones[:, :], 1.0)
            link(dve.memset(types_of[:, :, :], 0.0))
            for k in range(K):
                for h in range(2):
                    half = types_of[h * SLOTS:(h + 1) * SLOTS, k, h * K:(h + 1) * K]
                    dve.memset(half[:, k:k + 1], 1.0)
                    if k:
                        dve.memset(half[:, k - 1:k], -1.0)
            dve.wait_ge(s["consts_in"], 16)
            link(dve.tensor_copy(iota2[:, :, :], iota.unsqueeze(2).to_broadcast([P, P, 2])))
            dve.wait_ge(s["edges_in"], 16)
            sampled = dstr.rearrange("p (i n) -> p i n", n=STEP)[:, :, STEP - 1]
            dve.tensor_single_scalar(lowi, sampled, LOW - 1, ALU.bitwise_and)
            dve.tensor_single_scalar(highi, sampled, LOW.bit_length() - 1, ALU.arith_shift_right)\
               .then_inc(s["halves_made"], 1)
            dve.memset(low16[:, SAMPLES:HS], -1.0)
            dve.memset(high16[:, SAMPLES:HS], -1.0)
            dve.tensor_scalar(node_id, iota[:, 0:Q2], float(P), lane, ALU.mult, ALU.add)
            dve.memset(upper, 0.0)
            link(dve.memset(nils, 0.0))
            link(dve.tensor_copy(upper[:, LOW:P], ident[0:LOW, 0:LOW]))
            dve.wait_ge(s["halves_ready"], 2)

            def one_hots(buf, n, width, column, keys, at, out_t):
                k = keys[:, at].rearrange("p (i e) -> p i e", e=2).unsqueeze(2).to_broadcast([P, n // 2, width, 2])
                io = iota2[:, 0:width, :].unsqueeze(1).to_broadcast([P, n // 2, width, 2])
                return dve.tensor_tensor(out_t[:, buf, 0:n // 2, column:column + width, :], io, k, ALU.is_equal)

            def hist(b, buf, free):
                if free:
                    dve.wait_ge(s["hist_done"], b - 1)
                at = bass.ds(b * GR, GR)
                one_hots(buf, GR, LOW, 0, low16, at, oh_low)
                one_hots(buf, GR, HIGH, 0, high16, at, oh_high).then_inc(s["hist_ready"], 1)

            hist(0, 0, False)
            hist(1, 1, False)
            dve.wait_ge(s["order_in"], 48)
            link(dve.scalar_tensor_tensor(out=keyr, in0=typr, scalar=float(NP), in1=srcr, op0=ALU.mult, op1=ALU.add))
            dve.scalar_tensor_tensor(out=keyr, in0=dstr, scalar=KEY_BITS, in1=keyr, op0=ALU.logical_shift_left,
                                     op1=ALU.bitwise_or).then_inc(s["keys_made"], 1)
            with dve.Fori(1, HB // 2) as b2:
                hist(b2 * 2, 0, True)
                hist(b2 * 2 + 1, 1, True)
            hist(HB - 1, 0, True)
            dve.wait_ge(s["hist_done"], HB)
            dve.tensor_copy(found, B[0:LOW, 7, 0:HIGH]).then_inc(s["found_sb"], 1)
            dve.wait_ge(s["tot_psum"], 1)
            dve.tensor_copy(tot, B[:, 0, 0:Q]).then_inc(s["totals_sb"], 1)
            dve.wait_ge(s["before_psum"], 1)
            link(dve.memset(base, 0.0))
            link(dve.tensor_copy(shift_q, B[:, 2, 64:64 + Q]))
            link(dve.tensor_tensor_scan(base[:, 1:Q], shift_q[:, 0:Q - 1], nils[:, 0:Q - 1], 0.0, ALU.add, ALU.add))
            link(dve.tensor_tensor(ptri, B[:, 2, 0:Q], base, ALU.add))
            link(dve.tensor_single_scalar(shf, ptri, COPIES - 1, ALU.bitwise_and))
            link(dve.tensor_single_scalar(ptri, ptri, COPIES.bit_length() - 1, ALU.arith_shift_right))
            link(dve.scalar_tensor_tensor(out=row_at[:, 0, :], in0=shf, scalar=float(NR), in1=ptri,
                                          op0=ALU.mult, op1=ALU.add))
            dve.tensor_single_scalar(row_at[:, 1, :], row_at[:, 0, :], 1.0, ALU.add).then_inc(s["row_ready"], 1)

            def norm_stats(a, b):
                for q in range(a, b):
                    ins = dve.bn_stats(st6[:, q, :], xr[:, q, :])
                link(ins)
                for q in range(a, b):
                    ins = dve.bn_aggr(mv[:, q, :], st6[:, q, :])
                link(ins)

            def norm_roots(a, b):
                dve.tensor_single_scalar(mv[:, a:b, 1], mv[:, a:b, 1], 1e-5, ALU.add).then_inc(s["ln_var"], 1)

            def norm_scales(n, a, b, scale):
                dve.wait_ge(s["ln_std"], n)
                link(dve.reciprocal(rstd[:, a:b], rstd[:, a:b]))
                if scale != 1.0:
                    link(dve.tensor_single_scalar(rstd[:, a:b], rstd[:, a:b], scale, ALU.mult))
                dve.scalar_tensor_tensor(out=shift[:, a:b], in0=mv[:, a:b, 0], scalar=-1.0, in1=rstd[:, a:b],
                                         op0=ALU.mult, op1=ALU.mult).then_inc(s["shift_made"], 1)

            slot_v = valid.rearrange("p (q j) -> p q j", j=SLOTS)
            link(dve.memset(sloti[:, Q * SLOTS:Q2 * SLOTS].bitcast(F32), 0.0))
            dve.wait_ge(s["loaded"], 64)
            link(dve.tensor_tensor(brz[:, :], bias[:, BIH:BIH + 2], bias[:, BHH:BHH + 2], ALU.add))

            def slot_keys(m0, m1):
                at = slice(m0 * P, m1 * P)
                link(dve.tensor_single_scalar(loi[:, at], sloti[:, at], KEY_BITS, ALU.arith_shift_right))
                dve.tensor_scalar(hii[:, at], sloti[:, at], P.bit_length() - 1, P - 1, ALU.arith_shift_right,
                                  ALU.bitwise_and)
                link(dve.tensor_tensor(slot_v[:, 2 * m0:2 * m1], loi[:, at].rearrange("p (q j) -> p q j", j=SLOTS),
                                       node_id[:, 2 * m0:2 * m1].unsqueeze(2).to_broadcast([P, 2 * (m1 - m0), SLOTS]),
                                       ALU.is_equal))
                dve.scalar_tensor_tensor(out=hif[:, at], in0=hii[:, at], scalar=1.0, in1=valid[:, at],
                                         op0=ALU.add, op1=ALU.mult).then_inc(s["keys_high"], 1)
                link(dve.tensor_single_scalar(loi[:, at], sloti[:, at], P - 1, ALU.bitwise_and))
                dve.scalar_tensor_tensor(out=lof[:, at], in0=loi[:, at], scalar=1.0, in1=valid[:, at],
                                         op0=ALU.add, op1=ALU.mult).then_inc(s["keys_low"], 1)

            def source_tiles(m0, m1, g):
                at = slice(m0 * P, m1 * P)
                dve.wait_ge(s["kt_copied"], g)
                link(dve.tensor_copy(ksrc[:, at], khigh[:, at]))
                for k in range(1, K):
                    link(dve.tensor_scalar(ktmp[:, at], khigh[:, at], float(k * Q), -float(Q), ALU.is_ge, ALU.mult))
                    link(dve.tensor_tensor(ksrc[:, at], ksrc[:, at], ktmp[:, at], ALU.add))

            norm_stats(0, Q)
            dve.wait_ge(s["slots_in0"], 4 * FIRST * 16)
            slot_keys(0, FIRST)
            norm_roots(0, Q)
            source_tiles(0, FIRST, G1 // 2)
            dve.wait_ge(s["kt_copied"], G1)

            def all_out(u, i, g0, half):
                g = 4 * u + i
                dve.wait_ge(s["typed_out"], g0 + (g + 1))
                dve.sem_inc(s["passed"], 1)
                made = B[:, 2 * i:2 * i + 2, 0:4 * HQ].rearrange("p h (i x) -> p h x i", i=4)
                dve.tensor_scalar(ublk8[:, half].rearrange("p q h d -> p h q d")[:, :, :, 4 * g:4 * g + 4],
                                  made[:, :, K * Q:HQ, :], A_SCALE, None, ALU.mult, saturate=False)\
                   .then_inc(s["all_out"], 1)

            def pair(m, half, old, copied=False, its=4):
                for u in range(2 * its):
                    at, buf = bass.ds(m * P + u * GR, GR), u % 2
                    start = u == 0 and (first(m) or copied)

                    def copy(i):
                        if start:
                            return
                        if u:
                            all_out(u - 1, i, m * 32, half)
                        else:
                            all_out(7, i, (m - 1) * 32, 1 - half)

                    if not first(m) or u >= 2:
                        dve.wait_ge(s["ps_ready"], m * 32 + (4 * u - 4))
                    one_hots(buf, GR, P, 0, klow, at, oh_low)
                    one_hots(buf, GR, K * Q, 0, khigh, at, oh_high)
                    copy(0)
                    one_hots(buf, GR, Q, K * Q, ksrc, at, oh_high).then_inc(s["oh_ready"], 1)
                    copy(1)
                    copy(2)
                    if u == 0 and old is not None:
                        dve.wait_ge(s["au_stored%d" % half], old * 16)

            first = lambda m: isinstance(m, int) and m == 0
            pair(0, 0, None)
            norm_scales(1, 0, Q, H_SCALE)
            pair(1, 1, None)
            for i in range(3):
                all_out(7, i, 32, 1)
            dve.wait_ge(s["order_made"], 1)
            link(dve.tensor_reduce(flags[:, 0:1], order, AX.X, ALU.max))
            dve.wait_ge(s["slots_in"], (2 * Q - 4 * FIRST) * 16)
            slot_keys(FIRST, M)
            dve.tensor_reduce(flags[:, 1:2], slot_v[:, 0:Q, SLOTS - 1], AX.X, ALU.max)
            link(dve.tensor_reduce(tot, slot_v[:, 0:Q], AX.X, ALU.add))
            link(dve.tensor_single_scalar(inv_any[0], tot, 1.0, ALU.max))
            link(dve.reciprocal(inv_any[0], inv_any[0]))
            dve.tensor_single_scalar(inv_any[1], tot, 1.0, ALU.min).then_inc(s["inv_made"], 1)
            source_tiles(FIRST, M, G1 + (G2 - G1) // 2)
            dve.wait_ge(s["kt_copied"], G2)
            dve.sem_inc(s["keys_done"], 1)
            pair(2, 0, 1, copied=True)
            pair(3, 1, 1)
            with dve.Fori(2, M // 2) as m2:
                pair(m2 * 2, 0, m2)
                pair(m2 * 2 + 1, 1, m2)
            pair(M - 1, 0, M // 2, its=FEW_IT)
            for i in range(3):
                all_out(2 * FEW_IT - 1, i, (M - 1) * 32, 0)

            words = wide[:, :].bitcast(I32).rearrange("p (x n) -> p x n", n=OW)

            def look(x):
                if x == 0:
                    link(dve.tensor_copy(orw, words[:, 0, :]))
                else:
                    link(dve.tensor_tensor(orw, orw, words[:, x, :], ALU.bitwise_or))

            def mean(g):
                n, c = divmod(g, NS)
                z = min(SIZES[c], N - c * SC)
                dve.wait_ge(s["sm_psum"], g + 1)
                if g >= 2:
                    dve.wait_ge(s["sg_psum"], g - 1)
                got = meanT[g % 2][:, 0:z]
                ins = dve.scalar_tensor_tensor(out=got, in0=B[:, g % 2, 0:z], scalar=UNSCALE,
                                               in1=invb[:, c * SC:c * SC + z], op0=ALU.mult, op1=ALU.mult)
                if n:
                    link(ins)
                    ins = dve.scalar_tensor_tensor(out=got, in0=got, scalar=cols[:, 3:4],
                                                   in1=anyb[:, c * SC:c * SC + z], op0=ALU.mult, op1=ALU.add)
                ins.then_inc(s["mean_ready"], 1)

            def normed(g):
                n, c = divmod(g, NS)
                z = SIZES[c]
                at = slice(c * SC, c * SC + z)
                dve.wait_ge(s["sg_ssq"], g + 1)
                dve.tensor_single_scalar(rT[:, 0:z], B[:, 3, 0:z], 1e-24, ALU.max).then_inc(s["sg_max"], 1)
                dve.wait_ge(s["sg_std"], g + 1)
                dve.wait_ge(s["sg_out"], g + 1)
                link(dve.reciprocal(zT[:, 0:z], nT[:, 0:z]))
                if n == 0:
                    ins = dve.scalar_tensor_tensor(out=hT[:, at], in0=aT[:, 0:z], scalar=0.0, in1=zT[:, 0:z],
                                                   op0=ALU.max, op1=ALU.mult)
                else:
                    ins = dve.tensor_tensor(hT[:, at], aT[:, 0:z], zT[:, 0:z], ALU.mult)
                ins.then_inc(s["sg_done"], 1)
                if n == 0:
                    dve.wait_ge(s["sg_done"], g + 1)
                    for q in range(Q):
                        if c * SC < (q + 1) * (N // Q) <= c * SC + z:
                            ins = dve.bn_stats(st6[:, q, :], hT[:, q * (N // Q):(q + 1) * (N // Q)])
                    link(ins)

            four = lambda g: (4 * (g % NS), 4 * (g % NS) + SIZES[g % NS] // P)

            def low_half(g):
                a, b = four(g)
                dve.wait_ge(s["tout_hi"], g + 1)
                dve.scalar_tensor_tensor(out=half_flat(lo1[:, a:b, :]), in0=B[:, 6, 0:(b - a) * P], scalar=H_SCALE,
                                         in1=half_flat(hi1[:, a:b, :]), op0=ALU.mult, op1=ALU.subtract)\
                   .then_inc(s["tout_done"], 1)

            def add_norm(c):
                a, b = four(c)
                dve.wait_ge(s["tout_psum"], NS + c + 1)
                dve.tensor_tensor(flat_x[:, a * P:b * P], flat_x[:, a * P:b * P], B[:, 6, 0:(b - a) * P], ALU.add)\
                   .then_inc(s["tout_done"], 1)
                dve.wait_ge(s["tout_done"], NS + c + 1)
                norm_stats(a, b)
                norm_roots(a, b)
                norm_scales(c + 2, a, b, 1.0)
                dve.wait_ge(s["ln_hi"], c + 1)
                dve.scalar_tensor_tensor(out=half_flat(lo[:, a:b, :]), in0=turned_rows[:, 0:(b - a) * P],
                                         scalar=H_SCALE, in1=half_flat(hi[:, a:b, :]), op0=ALU.mult,
                                         op1=ALU.subtract).then_inc(s["ln_lo"], 1)

            dve.wait_ge(s["inv_read"], 32)
            for g in range(1, NS - 1):
                mean(g - 1)
                if g == 1:
                    dve.wait_ge(s["au_stored0"], (M + 1) // 2 * 16)
                    dve.wait_ge(s["au_stored1"], M // 2 * 16)
                    dve.memset(bet, 0.0).then_inc(s["bet_zero"], 1)
                for x in range(2 * M * (g - 1) // (NS - 2), 2 * M * g // (NS - 2)):
                    look(x)
                normed(g - 1)
                if g >= 2:
                    low_half(g - 2)
            mean(NS - 2)
            normed(NS - 2)
            mean(NS - 1)
            low_half(NS - 3)
            normed(NS - 1)
            low_half(NS - 2)
            low_half(NS - 1)
            link(dve.bn_aggr(cols[:, 0:2], st6[:, :, :].rearrange("p q s -> p (q s)")))
            dve.tensor_single_scalar(cols[:, 1:2], cols[:, 1:2], 1e-5, ALU.add).then_inc(s["bn_var"], 1)
            dve.wait_ge(s["bn_std"], 1)
            link(dve.reciprocal(cols[:, 3:4], cols[:, 2:3]))
            link(dve.tensor_tensor(cols[:, 3:4], cols[:, 3:4], bias[:, GAM:GAM + 1], ALU.mult))
            link(dve.tensor_tensor(cols[:, 5:6], cols[:, 0:1], cols[:, 3:4], ALU.mult))
            link(dve.tensor_tensor(cols[:, 4:5], bias[:, BET:BET + 1], cols[:, 5:6], ALU.subtract))
            link(dve.tensor_scalar(anyb, anyb, cols[:, 4:5], None, ALU.mult))
            dve.wait_ge(s["tout_psum"], NS)
            dve.tensor_scalar(hT, hT, cols[:, 3:4], cols[:, 4:5], ALU.mult, ALU.add).then_inc(s["h_scaled"], 1)
            mean(NS)
            link(dve.tensor_single_scalar(orw, orw, 0x40404040, ALU.bitwise_and))
            link(dve.tensor_reduce(flags[:, 2:3], orw, AX.X, ALU.max))
            link(dve.tensor_single_scalar(flags[:, 0:1], flags[:, 0:1], 0.0, ALU.is_gt))
            link(dve.tensor_single_scalar(flags[:, 2:3], flags[:, 2:3], 0.0, ALU.is_gt))
            dve.tensor_reduce(flags[:, 3:4], flags[:, 0:3], AX.X, ALU.add).then_inc(s["flag_psum"], 1)
            normed(NS)
            dve.wait_ge(s["flag_psum"], 2)
            dve.tensor_copy(redo, B[0:1, 7, 0:1]).then_inc(s["flag_ready"], 1)
            for k in range(K):
                at_least = klow[:, :] if k == 0 else ublk16[:, (k - 1) * M * P:k * M * P]
                ins = dve.tensor_single_scalar(at_least, khigh[:, :], float(k * Q), ALU.is_ge)
            ins.then_inc(s["atl_made"], 1)
            dve.wait_ge(s["x_back"], 32)
            for g in range(NS + 2, 2 * NS):
                mean(g - 1)
                add_norm(g - 2 - NS)
                normed(g - 1)
            mean(2 * NS - 1)
            add_norm(NS - 2)
            normed(2 * NS - 1)
            add_norm(NS - 1)
            dve.wait_ge(s["tln_copied"], NS)
            dve.tensor_copy(featT, hT).then_inc(s["feat_ready"], 1)
            link(dve.memset(fresh, 0.0))

            def turned(g, new_hi, dst):
                dve.wait_ge(s["th_hi"], g + 1)
                dve.scalar_tensor_tensor(out=dst, in0=B[:, 5, 0:P], scalar=H_SCALE, in1=new_hi,
                                         op0=ALU.mult, op1=ALU.subtract).then_inc(s["th_lo"], 1)

            def update(g, at, ch, few=P):
                dve.wait_ge(s["a_psum"], g + 2)
                dve.wait_ge(s["gates_psum"], g + 1)
                dve.tensor_tensor(aT[:, 0:few], B[:, 7, 0:few], countb[:, at], ALU.add).then_inc(s["a_copied"], 1)
                dve.wait_ge(s["sig_done"], g * 2 + 2)
                link(dve.scalar_tensor_tensor(out=tT[:, 0:few], in0=B[:, 4, 0:few], scalar=bias[:, BHH + 2:BHH + 3],
                                              in1=rT[:, 0:few], op0=ALU.add, op1=ALU.mult), ch)
                dve.tensor_tensor(tT[:, 0:few], tT[:, 0:few], B[:, 4, P:P + few], ALU.add).then_inc(s["pre_n"], 1)
                dve.wait_ge(s["n_ready"], g + 1)
                link(dve.tensor_tensor(rT[:, 0:few], hT[:, at], nT[:, 0:few], ALU.subtract), ch)
                link(dve.tensor_tensor(rT[:, 0:few], rT[:, 0:few], zT[:, 0:few], ALU.mult), ch)
                dve.tensor_tensor(fresh[:, 0:few], rT[:, 0:few], nT[:, 0:few], ALU.add)
                dve.tensor_tensor(hT[:, at], rT[:, 0:few], nT[:, 0:few], ALU.add).then_inc(s["h_updated"], 1)

            n0 = chain.value()
            dve.wait_ge(s["feat_ready"], 1)
            dve.wait_ge(s["cb_copied"], NS)
            with dve.Fori(0, STEPS) as t:
                turned(t * Q, hi[:, Q - 2, :], lo[:, Q - 2, :])
                update(t * Q, slice((Q - 1) * P, N), Count(t * (Q * 3) + n0), FEW)
                flat = lambda a, i: a[:, bass.ds(i, 1), :].rearrange("p o f -> p (o f)")
                with dve.Fori(1, Q - 1) as c:
                    g = t * Q + c
                    turned(g, flat(hi2, c - 1), flat(lo2, c - 1))
                    update(g, bass.ds((c - 1) * P, P), Count(g * 3 + n0))
                g = t * Q + (Q - 1)
                turned(g, hi2[:, Q - 2, :], lo2[:, Q - 2, :])
                dve.wait_ge(s["s_psum"], (t + 1) * Q + 1)
                dve.wait_ge(s["th_lo"], (t + 1) * Q + 1)
                for new, old in ((hi2, hi), (lo2, lo)):
                    dve.tensor_copy(old[:, 0:Q - 2, :], new[:, 1:Q - 1, :])
                    ins = dve.tensor_copy(old[:, Q - 1, :], new[:, 0, :])
                ins.then_inc(s["h_split"], 1)
                update(g, slice((Q - 2) * P, (Q - 1) * P), Count(g * 3 + n0))

            def add_output(c):
                at, z = slice(c * SC, c * SC + SIZES[c]), SIZES[c]
                dve.wait_ge(s["o_turned"], c + 1)
                dve.tensor_tensor(flat_x[:, at], flat_x[:, at], B[:, 5 + c % 2, 0:z], ALU.add).then_inc(s["out_ready"], 1)

            for c in range(NS):
                at, z = slice(c * SC, c * SC + SIZES[c]), SIZES[c]
                dve.wait_ge(s["o_sig"], c + 1)
                dve.scalar_tensor_tensor(out=hT[:, at], in0=B[:, 2 * (c % 2) + 1, 0:z], scalar=bias[:, JB:JB + 1],
                                         in1=gate_of[c % 2][:, 0:z], op0=ALU.add, op1=ALU.mult).then_inc(s["o_done"], 1)
                if c:
                    add_output(c - 1)
            add_output(NS - 1)


def general_kernel(nc, x, src_c, dst_c, typ_c, dst_r, typ_r, weights, biases, b_et, consts, out, redo):
    with ExitStack() as ctx:
        def sb(name, shape, dt=F32):
            return ctx.enter_context(nc.sbuf_tensor(name, shape, dt))

        def sem(name):
            return ctx.enter_context(nc.semaphore(name))

        table = nc.dram_tensor("table", [NP, D], F32, kind="Internal").ap()
        acc = nc.dram_tensor("acc", [ACC, D], F32, kind="Internal").ap()
        cnt_dram = nc.dram_tensor("cnt_dram", [K + 1, Q, P], F32, kind="Internal").ap()

        xr = sb("xr", [P, Q, D])
        rows = sb("rows", [P, Q, D])
        hT = sb("hT", [P, NP])
        featT = sb("featT", [P, NP])
        ST = sb("ST", [P, K, NP])
        zeros = sb("zeros", [P, ACC * D // P // 32])
        w = sb("w", [P, NW, P])
        bias = sb("bias", [P, NBIAS])
        brz = sb("brz", [P, 2])
        bet = sb("bet", [K, P])
        con = sb("con", [P, 3 * P + 1])
        below, ident, iota, lane = con[:, 0:P], con[:, P:2 * P], con[:, 2 * P:3 * P], con[:, 3 * P:3 * P + 1]
        ones = sb("ones", [P, P])
        dstc = sb("dstc", [P, NB * J], I32)
        typc = sb("typc", [P, NB * J], I32)
        lowi = ST[:, 0, 0:NB * J].bitcast(I32)
        lowf = sb("lowf", [P, NB * J])
        highf = sb("highf", [P, NB * J])
        oh_low = sb("oh_low", [P, 2, J, P], F16)
        oh_high = sb("oh_high", [P, 2, J, K * Q], F16)
        cnt = sb("cnt", [P, K + 1, Q])
        cntT = sb("cntT", [P, P])
        totT = sb("totT", [Q, P])
        cnt4 = sb("cnt4", [K, NP])
        cntb = sb("cntb", [P, NP])
        invb = sb("invb", [P, NP])
        st6 = sb("st6", [P, Q, 6])
        mv = sb("mv", [P, Q, 2])
        rstd = sb("rstd", [P, Q])
        cols = sb("cols", [P, 8])
        b_src = sb("b_src", [P, J], I32)
        b_dst = sb("b_dst", [P, J], I32)
        b_typ = sb("b_typ", [P, J], I32)
        r_dst = sb("r_dst", [P, J * P], I32)
        r_typ = sb("r_typ", [P, J * P], I32)
        key_c = sb("key_c", [P, J])
        key_r = sb("key_r", [P, J, P])
        same = sb("same", [P, J, P])
        comb = sb("comb", [P, J, D])
        earlier = comb
        dup = sb("dup", [P, J])
        spare = sb("spare", [P, J])
        to_row = sb("to_row", [P, J], I32)
        got = sb("got", [P, J, D])
        rowbuf = sb("rowbuf", [P, 4, D])
        aT = sb("aT", [P, CH])
        rT = sb("rT", [P, CH])
        zT = sb("zT", [P, CH])
        tT = sb("tT", [P, CH])
        nT = sb("nT", [P, CH])
        B = [ctx.enter_context(nc.psum_tensor(f"bank{i}", [P, 512], F32)) for i in range(8)]

        names = """loaded consts_loaded edges_in hist_free hist_ready hist_done cnt_psum cnt_sb cnt_written
            cnt_read act_step dve_step ln_var ln_std rows_ready tr_psum tr_copied tab_written acc_zeroed block_summed zeros_set
            edges_loaded keys_ready gathered comb_psum combined scattered row_loaded st_psum st_copied
            mean_ready sg_psum sg_sq sg_ssq sg_max sg_std sg_done bn_var bn_std h_ready
            a_psum a_copied gates_psum sig_done pre_n n_ready h_updated rdy_out o_psum o_sig o_done
            stored passed""".split()
        s = {n: sem(n) for n in names}

        def transpose_rows(pe, tr, src, dst_cols):
            for g in range(TG):
                n = min(4, Q - 4 * g)
                if tr.step >= 2 or not isinstance(tr.base, int):
                    pe.wait_ge(s["tr_copied"], tr.value(1))
                for m in range(n):
                    ins = pe.transpose(B[5 + g % 2][:, m * P:(m + 1) * P], src(4 * g + m), ident)
                ins.then_inc(s["tr_psum"], 1)
                tr.up()
            pe.wait_ge(s["tr_copied"], tr.value())

        def copy_rows(act, tr, dst):
            for g in range(TG):
                n = min(4, Q - 4 * g)
                act.wait_ge(s["tr_psum"], tr.up())
                act.activation(dst[:, 4 * g * P:(4 * g + n) * P], B[5 + g % 2][:, 0:n * P], ACT.Copy)\
                   .then_inc(s["tr_copied"], 1)

        block = ctx.enter_context(nc.Block())

        @block.sync
        def _(sp):
            again = sp.value_load(redo, min_val=0, max_val=3 * P)
            with sp.If(again != 0):
                sp.dma_start(dstc[:, :], dst_c).then_inc(s["edges_in"], 16)
                sp.dma_start(typc[:, :], typ_c).then_inc(s["edges_in"], 16)
                sp.dma_start(con[:, :], consts).then_inc(s["consts_loaded"], 16)
                sp.wait_ge(s["zeros_set"], 2)
                full = N // P
                sp.dma_start(xr[:, 0:full, :], x[0:full * P, :].rearrange("(q p) f -> p q f", p=P))\
                  .then_inc(s["loaded"], 16)
                sp.dma_start(xr[0:N - full * P, full, :], x[full * P:N, :]).then_inc(s["loaded"], 16)
                sp.dma_start(w[:, :, :], weights).then_inc(s["loaded"], 16)
                sp.dma_start(bias[:, :], biases).then_inc(s["loaded"], 16)
                sp.dma_start(bet[:, :], b_et).then_inc(s["loaded"], 16)
                sp.wait_ge(s["cnt_sb"], 2)
                sp.dma_start(cnt_dram[0:K].rearrange("k q p -> (k q) p"), cntT[0:K * Q, :]).then_inc(s["cnt_written"], 16)
                sp.dma_start(cnt_dram[K], totT[:, :]).then_inc(s["cnt_written"], 16)
                sp.wait_ge(s["cnt_written"], 32)
                sp.dma_start(cnt4[:, :], cnt_dram[0:K].rearrange("k q p -> k (q p)")).then_inc(s["cnt_read"], 16)
                sp.dma_start(cntb[:, :], cnt_dram[K].rearrange("q p -> (q p)").partition_broadcast(P))\
                  .then_inc(s["cnt_read"], 16)

                def aggregate(turn):
                    sp.wait_ge(s["rows_ready"], 1 + turn)
                    sp.dma_start(table.rearrange("(q p) f -> p q f", p=P), rows[:, :, :]).then_inc(s["tab_written"], 16)
                    flat = acc.rearrange("(p a) f -> p (a f)", p=P)
                    part = ACC * D // P // 32
                    for i in range(32):
                        sp.dma_start(flat[:, i * part:(i + 1) * part], zeros[:, :]).then_inc(s["acc_zeroed"], 16)
                    with sp.Fori(0, NB) as b:
                        sp.wait_ge(s["block_summed"], turn * NB + b + 1)
                        sp.dma_start(b_src[:, :], src_c[:, bass.ds(b * J, J)]).then_inc(s["edges_loaded"], 16)
                        sp.dma_start(b_dst[:, :], dst_c[:, bass.ds(b * J, J)]).then_inc(s["edges_loaded"], 16)
                        sp.dma_start(b_typ[:, :], typ_c[:, bass.ds(b * J, J)]).then_inc(s["edges_loaded"], 16)
                        sp.dma_start(r_dst[:, :], dst_r[bass.ds(b * J * P, J * P)].partition_broadcast(P))\
                          .then_inc(s["edges_loaded"], 16)
                        sp.dma_start(r_typ[:, :], typ_r[bass.ds(b * J * P, J * P)].partition_broadcast(P))\
                          .then_inc(s["edges_loaded"], 16)
                    sp.wait_ge(s["scattered"], (turn + 1) * (NB * 16 * J))
                    sp.sem_inc(s["passed"], 1)
                    with sp.Fori(0, K * Q // 4) as i:
                        sp.wait_ge(s["st_psum"], turn * (K * Q // 4) + i + 1)
                        sp.dma_start(rowbuf[:, :, :], acc[bass.ds(i * 4 * P, 4 * P), :].rearrange("(j p) f -> p j f", p=P))\
                          .then_inc(s["row_loaded"], 16)

                aggregate(0)
                aggregate(1)
                with sp.Fori(0, STEPS) as t:
                    aggregate(t + 2)
                sp.wait_ge(s["rdy_out"], 1)
                sp.dma_start(out[0:full * P, :].rearrange("(q p) f -> p q f", p=P), rows[:, 0:full, :])\
                  .then_inc(s["stored"], 16)
                sp.dma_start(out[full * P:N, :], rows[0:N - full * P, full, :]).then_inc(s["stored"], 16)
                sp.wait_ge(s["stored"], 32)


        @block.gpsimd
        def _(pool):
            again = pool.value_load(redo, min_val=0, max_val=3 * P)
            with pool.If(again != 0):
                pool.sem_inc(s["block_summed"], 1)
                pool.memset(zeros[:, :], 0.0).then_inc(s["zeros_set"], 1)
                pool.memset(xr[:, :, :], 0.0).then_inc(s["zeros_set"], 1)

                def aggregate(turn):
                    pool.wait_ge(s["tab_written"], (turn + 1) * 16)
                    pool.wait_ge(s["acc_zeroed"], (turn + 1) * 512)
                    pool.sem_inc(s["passed"], 1)
                    with pool.Fori(0, NB) as b:
                        blk = turn * NB + b
                        pool.wait_ge(s["edges_loaded"], (blk + 1) * 80)
                        pool.sem_inc(s["passed"], 1)
                        for j in range(J):
                            pool.indirect_dma_start(got[:, j, :], None, table,
                                                    bass.IndirectOffsetOnAxis(ap=b_src[:, j:j + 1], axis=0))\
                                .then_inc(s["gathered"], 16)
                        pool.wait_ge(s["keys_ready"], blk + 1)
                        for j in range(J):
                            pool.wait_ge(s["combined"], blk * (J // 4) + (j // 4 + 1))
                            pool.sem_inc(s["passed"], 1)
                            pool.indirect_dma_start(acc, bass.IndirectOffsetOnAxis(ap=to_row[:, j:j + 1], axis=0),
                                                    comb[:, j, :], None, compute_op=ALU.add,
                                                    bounds_check=ACC - 1).then_inc(s["scattered"], 16)
                            pool.wait_ge(s["scattered"], blk * (16 * J) + 16 * (j + 1))
                        pool.sem_inc(s["block_summed"], 1)

                aggregate(0)
                aggregate(1)
                with pool.Fori(0, STEPS) as t:
                    aggregate(t + 2)


        @block.tensor
        def _(pe):
            again = pe.value_load(redo, min_val=0, max_val=3 * P)
            with pe.If(again != 0):
                pe.sem_inc(s["hist_done"], 1)
                pe.sem_inc(s["st_psum"], 1)
                pe.sem_inc(s["gates_psum"], 1)
                def hist(b, buf, first, last):
                    pe.wait_ge(s["hist_ready"], b + 1)
                    for j in range(J):
                        ins = pe.matmul(B[7][:, 0:K * Q], oh_low[:, buf, j, :], oh_high[:, buf, j, :],
                                        start=first and j == 0, stop=last and j == J - 1)
                    ins.then_inc(s["hist_done"], 1)

                hist(0, 0, True, False)
                with pe.Fori(0, (NB - 3) // 2) as b2:
                    hist(b2 * 2 + 1, 1, False, False)
                    hist(b2 * 2 + 2, 0, False, False)
                hist(NB - 2, 1, False, False)
                hist(NB - 1, 0, False, True)
                pe.wait_ge(s["consts_loaded"], 16)
                pe.wait_ge(s["cnt_psum"], 1)
                pe.transpose(B[6][0:K * Q, 0:P], cnt[:, 0:K, :].rearrange("p k q -> p (k q)"), ident)
                pe.transpose(B[6][0:Q, P:2 * P], cnt[:, K, :], ident).then_inc(s["cnt_psum"], 1)

                tr = Count()

                def sums_to_columns(turn):
                    with pe.Fori(0, K * Q // 4) as i:
                        g = turn * (K * Q // 4) + i
                        pe.wait_ge(s["row_loaded"], (g + 1) * 16)
                        pe.wait_ge(s["st_copied"], g + 1)
                        for m in range(4):
                            ins = pe.transpose(B[5][:, m * P:(m + 1) * P], rowbuf[:, m, :], ident)
                        ins.then_inc(s["st_psum"], 1)

                def aggregate(turn):
                    with pe.Fori(0, NB) as b:
                        blk = turn * NB + b
                        pe.wait_ge(s["gathered"], (blk + 1) * (16 * J))
                        pe.wait_ge(s["keys_ready"], blk + 1)
                        for j in range(J):
                            ins = pe.matmul(B[6 + j // 4][:, (j % 4) * P:(j % 4 + 1) * P], same[:, j, :], got[:, j, :],
                                            start=True, stop=True)
                            if j % 4 == 3:
                                ins.then_inc(s["comb_psum"], 1)
                    sums_to_columns(turn)
                    pe.wait_ge(s["st_copied"], (turn + 1) * (K * Q // 4) + 1)
                    pe.sem_inc(s["passed"], 1)

                def sage(turn, w_agg, w_own):
                    pe.wait_ge(s["mean_ready"], turn + 1)
                    with pe.Fori(0, NC) as c:
                        g = turn * NC + c
                        pe.wait_ge(s["sg_done"], g + 1)
                        pe.matmul(B[0][:, 0:CH], w[:, w_agg, :], ST[:, 0, bass.ds(c * CH, CH)], start=True, stop=False)
                        pe.matmul(B[0][:, 0:CH], w[:, w_own, :], hT[:, bass.ds(c * CH, CH)], start=False, stop=True)\
                          .then_inc(s["sg_psum"], 1)
                        pe.wait_ge(s["sg_sq"], g + 1)
                        pe.matmul(B[1][:, 0:CH], ones[:, :], tT[:, :], start=True, stop=True).then_inc(s["sg_ssq"], 1)

                pe.wait_ge(s["cnt_sb"], 2)
                pe.wait_ge(s["rows_ready"], 1)
                transpose_rows(pe, tr, lambda q: rows[:, q, :], None)
                aggregate(0)
                sage(0, WL1, WR1)
                pe.wait_ge(s["sg_done"], NC + 1)
                transpose_rows(pe, tr, lambda q: hT[:, q * P:(q + 1) * P], None)
                aggregate(1)
                sage(1, WL2, WR2)
                pe.wait_ge(s["sg_done"], 2 * NC + 1)
                transpose_rows(pe, tr, lambda q: hT[:, q * P:(q + 1) * P], None)
                pe.wait_ge(s["rows_ready"], 3)
                transpose_rows(pe, tr, lambda q: rows[:, q, :], None)
                with pe.Fori(0, STEPS) as t:
                    aggregate(t + 2)
                    with pe.Fori(0, NC) as c:
                        g = t * NC + c
                        at = bass.ds(c * CH, CH)
                        pe.wait_ge(s["a_copied"], g + 1)
                        for k in range(K):
                            pe.matmul(B[0][:, 0:CH], w[:, WET + k, :], ST[:, k, at], start=k == 0, stop=False)
                        pe.matmul(B[0][:, 0:CH], bet[:, :], cnt4[:, at], start=False, stop=True)\
                          .then_inc(s["a_psum"], 1)
                        pe.wait_ge(s["a_copied"], g + 2)
                        pe.wait_ge(s["pre_n"], g + 1)
                        for m in range(2):
                            pe.matmul(B[1 + m][:, 0:CH], w[:, WIH + m, :], aT[:, :], start=True, stop=False)
                            pe.matmul(B[1 + m][:, 0:CH], w[:, WHH + m, :], hT[:, at], start=False, stop=True)
                        pe.matmul(B[3][:, 0:CH], w[:, WHH + 2, :], hT[:, at], start=True, stop=True)
                        pe.matmul(B[4][:, 0:CH], w[:, WIH + 2, :], aT[:, :], start=True, stop=True)\
                          .then_inc(s["gates_psum"], 1)
                    pe.wait_ge(s["h_updated"], (t + 1) * NC + 1)
                    transpose_rows(pe, tr.loop(t, TG), lambda q: hT[:, q * P:(q + 1) * P], None)
                tr.up(STEPS * TG)
                with pe.Fori(0, NC) as c:
                    at = bass.ds(c * CH, CH)
                    pe.wait_ge(s["o_done"], c + 1)
                    pe.matmul(B[0][:, 0:CH], w[:, IW, :], hT[:, at], start=True, stop=False)
                    pe.matmul(B[0][:, 0:CH], w[:, IW + 1, :], featT[:, at], start=False, stop=True)
                    pe.matmul(B[1][:, 0:CH], w[:, JW, :], hT[:, at], start=True, stop=True).then_inc(s["o_psum"], 1)
                pe.wait_ge(s["o_done"], NC + 1)
                transpose_rows(pe, tr, lambda q: hT[:, q * P:(q + 1) * P], None)


        @block.scalar
        def _(act):
            again = act.value_load(redo, min_val=0, max_val=3 * P)
            with act.If(again != 0):
                act.sem_inc(s["st_copied"], 1)
                act.sem_inc(s["a_copied"], 1)
                tr = Count()
                act.wait_ge(s["cnt_psum"], 2)
                act.activation(cntT[0:K * Q, :], B[6][0:K * Q, 0:P], ACT.Copy).then_inc(s["cnt_sb"], 1)
                act.activation(totT[:, :], B[6][0:Q, P:2 * P], ACT.Copy).then_inc(s["cnt_sb"], 1)
                act.wait_ge(s["ln_var"], 1)
                act.activation(rstd[:, :], mv[:, :, 1], ACT.Sqrt).then_inc(s["ln_std"], 1)
                copy_rows(act, tr, hT)

                def sums_to_columns(turn):
                    with act.Fori(0, K * Q // 4) as i:
                        act.wait_ge(s["st_psum"], turn * (K * Q // 4) + i + 2)
                        act.activation(ST[:, :, :].rearrange("p k n -> p (k n)")[:, bass.ds(i * 512, 512)],
                                       B[5][:, :], ACT.Copy).then_inc(s["st_copied"], 1)

                def sage(turn, b):
                    with act.Fori(0, NC) as c:
                        g = turn * NC + c
                        act.wait_ge(s["sg_psum"], g + 1)
                        act.activation(tT[:, :], B[0][:, 0:CH], ACT.Square, bias=bias[:, b:b + 1])\
                           .then_inc(s["sg_sq"], 1)
                        act.activation(aT[:, :], B[0][:, 0:CH], ACT.Identity, bias=bias[:, b:b + 1])\
                           .then_inc(s["act_step"], 1)
                        act.wait_ge(s["sg_max"], g + 1)
                        act.activation(nT[:, :], rT[:, :], ACT.Sqrt).then_inc(s["sg_std"], 1)

                sums_to_columns(0)
                sage(0, BL1)
                act.wait_ge(s["bn_var"], 1)
                act.activation(cols[:, 2:3], cols[:, 1:2], ACT.Sqrt).then_inc(s["bn_std"], 1)
                copy_rows(act, tr, rows[:, :, :].rearrange("p q f -> p (q f)"))
                act.wait_ge(s["tr_copied"], 2 * TG)
                act.activation(cols[:, 6:7], cols[:, 2:3], ACT.Copy).then_inc(s["rows_ready"], 1)
                sums_to_columns(1)
                sage(1, BL2)
                copy_rows(act, tr, rows[:, :, :].rearrange("p q f -> p (q f)"))
                act.wait_ge(s["ln_var"], 2)
                act.activation(rstd[:, :], mv[:, :, 1], ACT.Sqrt).then_inc(s["ln_std"], 1)
                copy_rows(act, tr, hT)
                with act.Fori(0, STEPS) as t:
                    sums_to_columns(t + 2)
                    with act.Fori(0, NC) as c:
                        g = t * NC + c
                        act.wait_ge(s["a_psum"], g + 1)
                        act.wait_ge(s["gates_psum"], g + 1)
                        act.activation(aT[:, :], B[0][:, 0:CH], ACT.Copy).then_inc(s["a_copied"], 1)
                        act.wait_ge(s["gates_psum"], g + 2)
                        act.wait_ge(s["h_updated"], g + 1)
                        act.activation(rT[:, :], B[1][:, 0:CH], ACT.Sigmoid, bias=brz[:, 0:1]).then_inc(s["sig_done"], 1)
                        act.activation(zT[:, :], B[2][:, 0:CH], ACT.Sigmoid, bias=brz[:, 1:2]).then_inc(s["sig_done"], 1)
                        act.wait_ge(s["pre_n"], g + 2)
                        act.activation(nT[:, :], tT[:, :], ACT.Tanh, bias=bias[:, BIH + 2:BIH + 3]).then_inc(s["n_ready"], 1)
                    inner = tr.loop(t, TG)
                    copy_rows(act, inner, rows[:, :, :].rearrange("p q f -> p (q f)"))
                    act.wait_ge(s["tr_copied"], inner.value())
                    act.activation(cols[:, 6:7], cols[:, 2:3], ACT.Copy).then_inc(s["rows_ready"], 1)
                tr.up(STEPS * TG)
                with act.Fori(0, NC) as c:
                    act.wait_ge(s["o_psum"], c + 1)
                    act.activation(rT[:, :], B[0][:, 0:CH], ACT.Sigmoid, bias=bias[:, IB:IB + 1]).then_inc(s["o_sig"], 1)
                copy_rows(act, tr, rows[:, :, :].rearrange("p q f -> p (q f)"))


        @block.vector
        def _(dve):
            again = dve.value_load(redo, min_val=0, max_val=3 * P)
            with dve.If(again != 0):
                chain = Count()
                dve.sem_inc(s["sg_done"], 1)
                dve.sem_inc(s["pre_n"], 1)
                dve.sem_inc(s["h_updated"], 1)
                dve.sem_inc(s["o_done"], 1)

                def link(ins, ch):
                    ins.then_inc(s["dve_step"], 1)
                    dve.wait_ge(s["dve_step"], ch.up())

                dve.memset(ones[:, :], 1.0)
                dve.wait_ge(s["edges_in"], 32)
                dve.wait_ge(s["consts_loaded"], 16)
                link(dve.tensor_single_scalar(lowi, dstc[:, :], P - 1, ALU.bitwise_and), chain)
                link(dve.tensor_copy(lowf[:, :], lowi), chain)
                link(dve.tensor_tensor(highf[:, :], dstc[:, :], lowf[:, :], ALU.subtract), chain)
                link(dve.tensor_single_scalar(highf[:, :], highf[:, :], 1.0 / P, ALU.mult), chain)
                link(dve.scalar_tensor_tensor(out=highf[:, :], in0=typc[:, :], scalar=float(Q), in1=highf[:, :],
                                              op0=ALU.mult, op1=ALU.add), chain)

                def hist(b, buf, free):
                    if free:
                        dve.wait_ge(s["hist_done"], b)
                    at = bass.ds(b * J, J) if not isinstance(b, int) else slice(b * J, b * J + J)
                    dve.tensor_tensor(oh_low[:, buf], iota.unsqueeze(1).to_broadcast([P, J, P]),
                                      lowf[:, at].unsqueeze(2).to_broadcast([P, J, P]), ALU.is_equal)
                    dve.tensor_tensor(oh_high[:, buf], iota[:, 0:K * Q].unsqueeze(1).to_broadcast([P, J, K * Q]),
                                      highf[:, at].unsqueeze(2).to_broadcast([P, J, K * Q]), ALU.is_equal)\
                       .then_inc(s["hist_ready"], 1)

                hist(0, 0, False)
                with dve.Fori(0, (NB - 3) // 2) as b2:
                    hist(b2 * 2 + 1, 1, True)
                    hist(b2 * 2 + 2, 0, True)
                hist(NB - 2, 1, True)
                hist(NB - 1, 0, True)
                dve.wait_ge(s["hist_done"], NB + 1)
                link(dve.tensor_copy(cnt[:, 0:K, :], B[7][:, 0:K * Q].rearrange("p (k q) -> p k q", k=K)), chain)
                link(dve.tensor_reduce(cnt[:, K, :], cnt[:, 0:K, :].rearrange("p k q -> p q k"), AX.X, ALU.add), chain)
                dve.tensor_copy(cols[:, 7:8], lane).then_inc(s["cnt_psum"], 1)

                def norm_rows(n):
                    for q in range(Q):
                        dve.bn_stats(st6[:, q, :], xr[:, q, :]).then_inc(s["dve_step"], 1)
                    chain.up(Q)
                    dve.wait_ge(s["dve_step"], chain.value())
                    for q in range(Q):
                        dve.bn_aggr(mv[:, q, :], st6[:, q, :]).then_inc(s["dve_step"], 1)
                    chain.up(Q)
                    dve.wait_ge(s["dve_step"], chain.value())
                    dve.tensor_single_scalar(mv[:, :, 1], mv[:, :, 1], 1e-5, ALU.add).then_inc(s["ln_var"], 1)
                    dve.wait_ge(s["ln_std"], n)
                    link(dve.reciprocal(rstd[:, :], rstd[:, :]), chain)
                    for q in range(Q):
                        dve.tensor_scalar(rows[:, q, :], xr[:, q, :], mv[:, q, 0:1], rstd[:, q:q + 1],
                                          ALU.subtract, ALU.mult).then_inc(s["dve_step"], 1)
                    chain.up(Q)
                    dve.wait_ge(s["dve_step"], chain.value())
                    dve.tensor_single_scalar(rows[:, :, :], rows[:, :, :], 0.0, ALU.max).then_inc(s["rows_ready"], 1)

                dve.wait_ge(s["loaded"], 80)
                norm_rows(1)
                link(dve.tensor_tensor(brz[:, :], bias[:, BIH:BIH + 2], bias[:, BHH:BHH + 2], ALU.add), chain)
                dve.wait_ge(s["cnt_read"], 32)
                link(dve.tensor_single_scalar(invb[:, :], cntb[:, :], 1.0, ALU.max), chain)
                link(dve.reciprocal(invb[:, :], invb[:, :]), chain)

                def aggregate(turn, ch, n0):
                    with dve.Fori(0, NB) as b:
                        blk = turn * NB + b
                        c = Count(ch + b * 7)
                        dve.wait_ge(s["edges_loaded"], (blk + 1) * 80)
                        link(dve.scalar_tensor_tensor(out=key_c[:, :], in0=b_typ[:, :], scalar=float(NP), in1=b_dst[:, :],
                                                      op0=ALU.mult, op1=ALU.add), c)
                        link(dve.scalar_tensor_tensor(out=key_r[:, :, :].rearrange("p j e -> p (j e)"), in0=r_typ[:, :],
                                                      scalar=float(NP), in1=r_dst[:, :], op0=ALU.mult, op1=ALU.add), c)
                        link(dve.tensor_tensor(same[:, :, :], key_r[:, :, :],
                                               key_c[:, :].unsqueeze(2).to_broadcast([P, J, P]), ALU.is_equal), c)
                        link(dve.tensor_tensor(earlier[:, :, :], same[:, :, :],
                                               below.unsqueeze(1).to_broadcast([P, J, P]), ALU.mult), c)
                        link(dve.tensor_reduce(dup[:, :], earlier[:, :, :], AX.X, ALU.max), c)
                        link(dve.tensor_scalar(spare[:, :], key_c[:, :], -1.0, cols[:, 7:8], ALU.mult, ALU.add), c)
                        link(dve.scalar_tensor_tensor(out=spare[:, :], in0=spare[:, :], scalar=float(K * NP),
                                                      in1=dup[:, :], op0=ALU.add, op1=ALU.mult), c)
                        dve.tensor_tensor(to_row[:, :], spare[:, :], key_c[:, :], ALU.add).then_inc(s["keys_ready"], 1)
                        for m in range(J // 4):
                            dve.wait_ge(s["comb_psum"], blk * (J // 4) + (m + 1))
                            dve.tensor_copy(comb[:, 4 * m:4 * m + 4, :].rearrange("p j f -> p (j f)"), B[6 + m][:, :])\
                               .then_inc(s["combined"], 1)

                def sage(turn, relu):
                    dve.wait_ge(s["st_copied"], (turn + 1) * (K * Q // 4) + 1)
                    for k in range(1, K):
                        link(dve.tensor_tensor(ST[:, 0, :], ST[:, 0, :], ST[:, k, :], ALU.add), chain)
                    if turn == 0:
                        dve.wait_ge(s["tr_copied"], TG)
                        dve.tensor_tensor(ST[:, 0, :], ST[:, 0, :], invb[:, :], ALU.mult).then_inc(s["mean_ready"], 1)
                    else:
                        link(dve.tensor_tensor(ST[:, 0, :], ST[:, 0, :], invb[:, :], ALU.mult), chain)
                        link(dve.tensor_tensor(ST[:, 1, :], cntb[:, :], invb[:, :], ALU.mult), chain)
                        link(dve.tensor_scalar(ST[:, 1, :], ST[:, 1, :], cols[:, 4:5], None, ALU.mult), chain)
                        link(dve.scalar_tensor_tensor(out=ST[:, 0, :], in0=ST[:, 0, :], scalar=cols[:, 3:4],
                                                      in1=ST[:, 1, :], op0=ALU.mult, op1=ALU.add), chain)
                        dve.tensor_scalar(hT[:, :], hT[:, :], cols[:, 3:4], cols[:, 4:5], ALU.mult, ALU.add)\
                           .then_inc(s["mean_ready"], 1)
                    n0 = chain.value()
                    with dve.Fori(0, NC) as c:
                        g = turn * NC + c
                        ch = Count(n0 + c * 1)
                        at = bass.ds(c * CH, CH)
                        dve.wait_ge(s["sg_ssq"], g + 1)
                        dve.tensor_single_scalar(rT[:, :], B[1][:, 0:CH], 1e-24, ALU.max).then_inc(s["sg_max"], 1)
                        dve.wait_ge(s["sg_std"], g + 1)
                        dve.wait_ge(s["act_step"], g + 1)
                        link(dve.reciprocal(zT[:, :], nT[:, :]), ch)
                        if relu:
                            dve.scalar_tensor_tensor(out=hT[:, at], in0=aT[:, :], scalar=0.0, in1=zT[:, :],
                                                     op0=ALU.max, op1=ALU.mult).then_inc(s["sg_done"], 1)
                        else:
                            dve.tensor_tensor(hT[:, at], aT[:, :], zT[:, :], ALU.mult).then_inc(s["sg_done"], 1)
                    chain.up(NC)

                aggregate(0, chain.value(), 0)
                chain.up(7 * NB)
                sage(0, True)
                dve.wait_ge(s["sg_done"], NC + 1)
                for q in range(Q):
                    dve.bn_stats(st6[:, q, :], hT[:, q * (N // Q):(q + 1) * (N // Q)]).then_inc(s["dve_step"], 1)
                chain.up(Q)
                dve.wait_ge(s["dve_step"], chain.value())
                link(dve.bn_aggr(cols[:, 0:2], st6[:, :, :].rearrange("p q s -> p (q s)")), chain)
                dve.tensor_single_scalar(cols[:, 1:2], cols[:, 1:2], 1e-5, ALU.add).then_inc(s["bn_var"], 1)
                dve.wait_ge(s["bn_std"], 1)
                link(dve.reciprocal(cols[:, 3:4], cols[:, 2:3]), chain)
                link(dve.tensor_tensor(cols[:, 3:4], cols[:, 3:4], bias[:, GAM:GAM + 1], ALU.mult), chain)
                link(dve.tensor_tensor(cols[:, 5:6], cols[:, 0:1], cols[:, 3:4], ALU.mult), chain)
                link(dve.tensor_tensor(cols[:, 4:5], bias[:, BET:BET + 1], cols[:, 5:6], ALU.subtract), chain)
                aggregate(1, chain.value(), 0)
                chain.up(7 * NB)
                sage(1, False)
                dve.wait_ge(s["tr_copied"], 3 * TG)
                link(dve.tensor_tensor(xr[:, :, :], xr[:, :, :], rows[:, :, :], ALU.add), chain)
                norm_rows(2)
                dve.wait_ge(s["tr_copied"], 4 * TG)
                link(dve.tensor_copy(featT[:, :], hT[:, :]), chain)
                n0 = chain.value()
                per = 7 * NB + 3 * NC
                with dve.Fori(0, STEPS) as t:
                    aggregate(t + 2, t * per + n0, 0)
                    with dve.Fori(0, NC) as c:
                        g = t * NC + c
                        at = bass.ds(c * CH, CH)
                        ch = Count(t * per + c * 3 + (n0 + 7 * NB))
                        dve.wait_ge(s["sig_done"], g * 2 + 2)
                        link(dve.scalar_tensor_tensor(out=tT[:, :], in0=B[3][:, 0:CH], scalar=bias[:, BHH + 2:BHH + 3],
                                                      in1=rT[:, :], op0=ALU.add, op1=ALU.mult), ch)
                        dve.tensor_tensor(tT[:, :], tT[:, :], B[4][:, 0:CH], ALU.add).then_inc(s["pre_n"], 1)
                        dve.wait_ge(s["n_ready"], g + 1)
                        link(dve.tensor_tensor(rT[:, :], hT[:, at], nT[:, :], ALU.subtract), ch)
                        link(dve.tensor_tensor(rT[:, :], rT[:, :], zT[:, :], ALU.mult), ch)
                        dve.tensor_tensor(hT[:, at], rT[:, :], nT[:, :], ALU.add).then_inc(s["h_updated"], 1)
                chain.up(STEPS * per)
                n0 = chain.value()
                with dve.Fori(0, NC) as c:
                    at = bass.ds(c * CH, CH)
                    dve.wait_ge(s["o_sig"], c + 1)
                    dve.scalar_tensor_tensor(out=hT[:, at], in0=B[1][:, 0:CH], scalar=bias[:, JB:JB + 1],
                                             in1=rT[:, :], op0=ALU.add, op1=ALU.mult).then_inc(s["o_done"], 1)
                dve.wait_ge(s["tr_copied"], (5 + STEPS) * TG)
                dve.tensor_tensor(rows[:, :, :], rows[:, :, :], xr[:, :, :], ALU.add).then_inc(s["rdy_out"], 1)




def gnn_kernel(nc, a, out):
    with nc.sbuf_tensor("redo", [1, 1], I32) as redo:
        dense_kernel(nc, a["x"], a["src_r"], a["dst_r"], a["typ_r"], a["weights"],
                     a["biases"], a["b_et"], a["consts"], out, redo[:, :])
        general_kernel(nc, a["x"], a["src_c"], a["dst_c"], a["typ_c"], a["dst_r"], a["typ_r"], a["weights"],
                       a["biases"], a["b_et"], a["consts"][:, 0:3 * P + 1], out, redo[:, :])


def kernel(x, src, dst, edge_type_4, L0_gnn_W_l1, L0_gnn_b_l1, L0_gnn_W_r1, L0_gnn_gamma, L0_gnn_beta,
           L0_gnn_W_l2, L0_gnn_b_l2, L0_gnn_W_r2, L1_gnn_W_et, L1_gnn_b_et, L1_gnn_W_ih, L1_gnn_b_ih,
           L1_gnn_W_hh, L1_gnn_b_hh, L1_gnn_i_w, L1_gnn_i_b, L1_gnn_j_w, L1_gnn_j_b):
    import concourse.bacc as bacc
    from concourse.bass_utils import run_bass_kernel_spmd

    def tiles_of(wt):
        wt = np.asarray(wt)
        return [wt[o:o + P, i:i + P].T for i in range(0, wt.shape[1], P) for o in range(0, wt.shape[0], P)]

    def edges(a, pad):
        a = np.asarray(a)
        full = np.full(P * KW + P, pad, a.dtype)
        full[:E] = a
        return full

    we = np.asarray(L1_gnn_W_et)
    weights = np.stack([t for wt in (L0_gnn_W_l1, L0_gnn_W_r1, L0_gnn_W_l2, L0_gnn_W_r2, we[0], we[1], we[2], we[3],
                                     L1_gnn_W_ih, L1_gnn_W_hh, L1_gnn_i_w, L1_gnn_j_w) for t in tiles_of(wt)], axis=1)
    biases = np.concatenate([np.asarray(b).reshape(-1, P) for b in (
        L0_gnn_b_l1, L0_gnn_b_l2, L0_gnn_gamma, L0_gnn_beta, L1_gnn_b_ih, L1_gnn_b_hh, L1_gnn_i_b, L1_gnn_j_b)]).T
    src_p, dst_p, typ_p = edges(src, 0), edges(dst, NP), edges(edge_type_4, K - 1)
    lane = np.arange(P, dtype=np.float32)
    consts = np.concatenate([np.tril(np.ones((P, P), np.float32), -1), np.eye(P, dtype=np.float32),
                             np.tile(lane, (P, 1)), lane[:, None],
                             np.triu(np.ones((P, P), np.float32), 1)], axis=1)
    arrays = {
        "x": np.asarray(x),
        "src_c": src_p[:EP].reshape(-1, P).T, "dst_c": dst_p[:EP].reshape(-1, P).T, "typ_c": typ_p[:EP].reshape(-1, P).T,
        "src_r": src_p, "dst_r": dst_p, "typ_r": typ_p,
        "weights": weights, "biases": biases, "b_et": np.asarray(L1_gnn_b_et), "consts": consts,
    }
    arrays = {k: np.ascontiguousarray(v) for k, v in arrays.items()}
    nc = bacc.Bacc("TRN2", target_bir_lowering=False, num_devices=1)
    args = {k: nc.dram_tensor(k, v.shape, mybir.dt.from_np(v.dtype), kind="ExternalInput").ap()
            for k, v in arrays.items()}
    out = nc.dram_tensor("out", (N, D), F32, kind="ExternalOutput").ap()
    gnn_kernel(nc, args, out)
    return run_bass_kernel_spmd(nc, [arrays], core_ids=[0]).results[0]["out"]
```
